# Optimizing a Trainium2 kernel written in Bass

```python
import numpy as np
import jax
import jax.numpy as jnp

def _softmax(x, axis=-1):
    return jax.nn.softmax(x, axis=axis)

def _gelu(x):
    return jax.nn.gelu(x, approximate=True)

def _silu(x):
    return jax.nn.silu(x)

def _sigmoid(x):
    return jax.nn.sigmoid(x)

def _layernorm(x, axis=-1, eps=1e-05):
    m = jnp.mean(x, axis=axis, keepdims=True)
    v = jnp.var(x, axis=axis, keepdims=True)
    return (x - m) / jnp.sqrt(v + eps)

def _scatter_add(tgt, idx, src, axis=0):
    return tgt.at[idx].add(src)

def _segment_sum(src, seg, n):
    return jax.ops.segment_sum(src, seg, n)
kernel_name = 'mk_adj_resnorm_d4_adj_r2_f9703f'

def setup_inputs(seed: int=0):
    np.random.seed(seed)
    _w = jnp.asarray

    def _rec_inputs():
        import jax
        import jax.numpy as jnp
        _gk = jax.random.key(seed)
        x = 7.22e-05 + 1 * jax.random.normal(jax.random.fold_in(_gk, 1), (128, 64, 256), jnp.float32)
        _w = (1.0 + jnp.arange(64, dtype=jnp.float32)) ** (-0.5)
        _w = _w / _w.mean()
        _pij = jnp.clip(0.0625 * _w[:, None] * _w[None, :], 0.0, 1.0)
        _a = jax.random.uniform(jax.random.fold_in(_gk, 2), (64, 64)) < _pij
        _a = jnp.logical_or(_a, jnp.swapaxes(_a, -1, -2))
        _a = jnp.logical_or(_a, jnp.eye(64, dtype=bool))
        _af = _a.astype(jnp.float32)
        _af = _af * jax.random.uniform(jax.random.fold_in(_gk, 3), (64, 64), jnp.float32, 0.05, 0.00390622)
        adj = _af
        return (x, adj)
    x, adj = _rec_inputs()

    def _L0_gnn_setup():
        import jax, jax.numpy as jnp
        import numpy as np
        B, N, D, T = (64, 128, 256, 3)

        def _lin(v, W, b):
            return jnp.einsum('...i,oi->...o', v, W) + b
        key = jax.random.key(seed)
        ks = jax.random.split(key, 12)
        s2 = 1.0 / np.sqrt(2 * D)
        s1 = 1.0 / np.sqrt(D)
        return {'x': jax.random.normal(ks[0], (B, N, D), jnp.float32), 'in_mat': jax.random.uniform(ks[1], (N, N), jnp.float32) / N, 'out_mat': jax.random.uniform(ks[2], (N, N), jnp.float32) / N, 'w3_w': jax.random.normal(ks[3], (D, 2 * D), jnp.float32) * s2, 'w3_b': jnp.zeros((D,), jnp.float32), 'u3_w': jax.random.normal(ks[4], (D, D), jnp.float32) * s1, 'u3_b': jnp.zeros((D,), jnp.float32), 'w4_w': jax.random.normal(ks[5], (D, 2 * D), jnp.float32) * s2, 'w4_b': jnp.zeros((D,), jnp.float32), 'w5_w': jax.random.normal(ks[6], (D, 2 * D), jnp.float32) * s2, 'w5_b': jnp.zeros((D,), jnp.float32), 'u5_w': jax.random.normal(ks[7], (D, D), jnp.float32) * s1, 'u5_b': jnp.zeros((D,), jnp.float32)}
    _L0_gnn_all = _L0_gnn_setup()
    _L0_gnn_in = {k: v for k, v in _L0_gnn_all.items() if k in ('w3_w', 'w3_b', 'u3_w', 'u3_b', 'w4_w', 'w4_b', 'w5_w', 'w5_b', 'u5_w', 'u5_b')}
    del _L0_gnn_all

    def _L1_gnn_setup():
        import jax, jax.numpy as jnp
        import numpy as np
        B, N, D = (8, 1024, 256)
        key = jax.random.key(seed)
        k1, k2, k3, k4, k5 = jax.random.split(key, 5)
        neuron_states = jax.random.normal(k1, (B, N, D), dtype=jnp.float32)
        adjacency = jax.random.randint(k2, (N, N), 0, 2).astype(jnp.float32)
        scale = 1.0 / np.sqrt(D)
        Wq = jax.random.normal(k3, (D, D), dtype=jnp.float32) * scale
        Wk = jax.random.normal(k4, (D, D), dtype=jnp.float32) * scale
        Wv = jax.random.normal(k5, (D, D), dtype=jnp.float32) * scale
        return {'neuron_states': neuron_states, 'adjacency': adjacency, 'Wq': Wq, 'Wk': Wk, 'Wv': Wv}
    _L1_gnn_all = _L1_gnn_setup()
    _L1_gnn_in = {k: v for k, v in _L1_gnn_all.items() if k in ('Wq', 'Wk', 'Wv')}
    del _L1_gnn_all

    def _L2_gnn_setup():
        import jax, jax.numpy as jnp
        import numpy as np
        B, N, D, H = (16, 1025, 256, 8)
        LN_EPS = 1e-05

        def _make_mask(key, n):
            n_proto = n - 1
            adj = jax.random.bernoulli(key, 0.03, (n_proto, n_proto)).astype(jnp.float32)
            adj = jnp.clip(adj + adj.T + jnp.eye(n_proto, dtype=jnp.float32), 0.0, 1.0)
            mask = jnp.zeros((n, n), dtype=jnp.float32)
            mask = mask.at[0, :].set(1.0).at[:, 0].set(1.0)
            mask = mask.at[1:, 1:].set(adj)
            return mask
        key = jax.random.key(seed)
        ks = jax.random.split(key, 7)
        s = 1.0 / np.sqrt(D)
        return {'x': jax.random.normal(ks[0], (B, N, D), dtype=jnp.float32), 'w_qkv': jax.random.uniform(ks[1], (D, 3 * D), dtype=jnp.float32, minval=-s, maxval=s), 'w_proj': jax.random.uniform(ks[2], (D, D), dtype=jnp.float32, minval=-s, maxval=s), 'b_proj': jnp.zeros((D,), dtype=jnp.float32), 'ln_gamma': jnp.ones((D,), dtype=jnp.float32), 'ln_beta': jnp.zeros((D,), dtype=jnp.float32), 'attn_mask': _make_mask(ks[3], N)}
    _L2_gnn_all = _L2_gnn_setup()
    _L2_gnn_in = {k: v for k, v in _L2_gnn_all.items() if k in ('w_qkv', 'w_proj', 'b_proj', 'ln_gamma', 'ln_beta')}
    del _L2_gnn_all

    def _L3_gnn_setup():
        import jax, jax.numpy as jnp
        import numpy as np
        ALPHA = 0.2
        key = jax.random.key(seed)
        k0, k1, k2, k3 = jax.random.split(key, 4)
        B, N, C, F = (64, 512, 256, 256)
        x = jax.random.normal(k0, (B, N, C), dtype=jnp.float32)
        W = jax.random.normal(k1, (C, F), dtype=jnp.float32) * (1.414 / np.sqrt(C + F))
        a = jax.random.normal(k2, (2 * F, 1), dtype=jnp.float32) * (1.414 / np.sqrt(2 * F + 1))
        beta = jnp.ones((1,), dtype=jnp.float32)
        mask = (jax.random.uniform(k3, (N, N)) < 0.3).astype(jnp.float32)
        return {'x': x, 'W': W, 'a': a, 'beta': beta, 'mask': mask}
    _L3_gnn_all = _L3_gnn_setup()
    _L3_gnn_in = {k: v for k, v in _L3_gnn_all.items() if k in ('W', 'a', 'beta')}
    del _L3_gnn_all
    return {'x': x, 'adj': adj, 'L0_gnn_w3_w': _L0_gnn_in['w3_w'], 'L0_gnn_w3_b': _L0_gnn_in['w3_b'], 'L0_gnn_u3_w': _L0_gnn_in['u3_w'], 'L0_gnn_u3_b': _L0_gnn_in['u3_b'], 'L0_gnn_w4_w': _L0_gnn_in['w4_w'], 'L0_gnn_w4_b': _L0_gnn_in['w4_b'], 'L0_gnn_w5_w': _L0_gnn_in['w5_w'], 'L0_gnn_w5_b': _L0_gnn_in['w5_b'], 'L0_gnn_u5_w': _L0_gnn_in['u5_w'], 'L0_gnn_u5_b': _L0_gnn_in['u5_b'], 'L1_gnn_Wq': _L1_gnn_in['Wq'], 'L1_gnn_Wk': _L1_gnn_in['Wk'], 'L1_gnn_Wv': _L1_gnn_in['Wv'], 'L2_gnn_w_qkv': _L2_gnn_in['w_qkv'], 'L2_gnn_w_proj': _L2_gnn_in['w_proj'], 'L2_gnn_b_proj': _L2_gnn_in['b_proj'], 'L2_gnn_ln_gamma': _L2_gnn_in['ln_gamma'], 'L2_gnn_ln_beta': _L2_gnn_in['ln_beta'], 'L3_gnn_W': _L3_gnn_in['W'], 'L3_gnn_a': _L3_gnn_in['a'], 'L3_gnn_beta': _L3_gnn_in['beta']}

def reference(x, adj, L0_gnn_w3_w, L0_gnn_w3_b, L0_gnn_u3_w, L0_gnn_u3_b, L0_gnn_w4_w, L0_gnn_w4_b, L0_gnn_w5_w, L0_gnn_w5_b, L0_gnn_u5_w, L0_gnn_u5_b, L1_gnn_Wq, L1_gnn_Wk, L1_gnn_Wv, L2_gnn_w_qkv, L2_gnn_w_proj, L2_gnn_b_proj, L2_gnn_ln_gamma, L2_gnn_ln_beta, L3_gnn_W, L3_gnn_a, L3_gnn_beta):
    import jax
    import jax.numpy as jnp

    def _L0_gnn_ref(x, in_mat, out_mat, w3_w, w3_b, u3_w, u3_b, w4_w, w4_b, w5_w, w5_b, u5_w, u5_b):
        import jax, jax.numpy as jnp
        import numpy as np
        B, N, D, T = (64, 128, 256, 3)

        def _lin(v, W, b):
            return jnp.einsum('...i,oi->...o', v, W) + b
        h = x
        for _ in range(T):
            a_in = jnp.einsum('nm,bmd->bnd', in_mat, h)
            a_out = jnp.einsum('nm,bmd->bnd', out_mat, h)
            av = jnp.concatenate([a_in, a_out], axis=-1)
            z = jax.nn.sigmoid(_lin(av, w3_w, w3_b) + _lin(h, u3_w, u3_b))
            r = jax.nn.sigmoid(_lin(av, w4_w, w4_b) + _lin(h, u3_w, u3_b))
            hv = jnp.tanh(_lin(av, w5_w, w5_b) + _lin(r * h, u5_w, u5_b))
            h = (1.0 - z) * h + z * hv
        return h

    def _L1_gnn_ref(neuron_states, adjacency, Wq, Wk, Wv):
        import jax, jax.numpy as jnp
        import numpy as np
        B, N, D = (8, 1024, 256)
        q = jnp.einsum('bnd,ed->bne', neuron_states, Wq)
        k = jnp.einsum('bnd,ed->bne', neuron_states, Wk)
        v = jnp.einsum('bnd,ed->bne', neuron_states, Wv)
        rel = jnp.einsum('bnd,bmd->bnm', q, k)
        rel = adjacency.T[None, :, :] * rel
        rel = rel / jnp.linalg.norm(rel, axis=2, keepdims=True)
        return jnp.einsum('bnm,bmd->bnd', rel, v)

    def _L2_gnn_ref(x, w_qkv, w_proj, b_proj, ln_gamma, ln_beta, attn_mask):
        import jax, jax.numpy as jnp
        import numpy as np
        B, N, D, H = (16, 1025, 256, 8)
        LN_EPS = 1e-05

        def _make_mask(key, n):
            n_proto = n - 1
            adj = jax.random.bernoulli(key, 0.03, (n_proto, n_proto)).astype(jnp.float32)
            adj = jnp.clip(adj + adj.T + jnp.eye(n_proto, dtype=jnp.float32), 0.0, 1.0)
            mask = jnp.zeros((n, n), dtype=jnp.float32)
            mask = mask.at[0, :].set(1.0).at[:, 0].set(1.0)
            mask = mask.at[1:, 1:].set(adj)
            return mask
        b, n, d = x.shape
        hd = d // H
        scale = hd ** (-0.5)
        qkv = (x @ w_qkv).reshape(b, n, 3, H, hd).transpose(2, 0, 3, 1, 4)
        q, k, v = (qkv[0], qkv[1], qkv[2])
        attn = jnp.einsum('bhnd,bhmd->bhnm', q, k) * scale
        attn = jnp.where(attn_mask[None, None] == 0, -jnp.inf, attn)
        attn = jax.nn.softmax(attn, axis=-1)
        o = jnp.einsum('bhnm,bhmd->bhnd', attn, v).transpose(0, 2, 1, 3).reshape(b, n, d)
        o = o @ w_proj + b_proj
        mu = jnp.mean(o, axis=-1, keepdims=True)
        var = jnp.mean(jnp.square(o - mu), axis=-1, keepdims=True)
        ln = (o - mu) * jax.lax.rsqrt(var + LN_EPS) * ln_gamma + ln_beta
        return o + ln

    def _L3_gnn_ref(x, W, a, beta, mask):
        import jax, jax.numpy as jnp
        import numpy as np
        ALPHA = 0.2
        F_ = W.shape[1]
        h = jnp.einsum('bnc,cf->bnf', x, W)
        a1, a2 = (a[:F_, 0], a[F_:, 0])
        s1 = jnp.einsum('bnf,f->bn', h, a1)
        s2 = jnp.einsum('bnf,f->bn', h, a2)
        e = jax.nn.leaky_relu(s1[:, :, None] + s2[:, None, :], negative_slope=ALPHA)
        e = e * mask[None, :, :]
        att = jax.nn.softmax(e, axis=2)
        h_prime = jnp.einsum('bij,bjf->bif', att, h)
        return jax.nn.elu(h_prime + beta * h)
    x = _layernorm(x + _L0_gnn_ref(x, adj, adj, L0_gnn_w3_w, L0_gnn_w3_b, L0_gnn_u3_w, L0_gnn_u3_b, L0_gnn_w4_w, L0_gnn_w4_b, L0_gnn_w5_w, L0_gnn_w5_b, L0_gnn_u5_w, L0_gnn_u5_b), axis=-1)
    x = _layernorm(x + _L1_gnn_ref(x, adj, L1_gnn_Wq, L1_gnn_Wk, L1_gnn_Wv), axis=-1)
    x = _layernorm(x + _L2_gnn_ref(x, L2_gnn_w_qkv, L2_gnn_w_proj, L2_gnn_b_proj, L2_gnn_ln_gamma, L2_gnn_ln_beta, adj), axis=-1)
    x = _layernorm(x + _L3_gnn_ref(x, L3_gnn_W, L3_gnn_a, L3_gnn_beta, adj), axis=-1)
    return x

_drawn_inputs = setup_inputs


def setup_inputs(seed=0):
    import zlib

    import numpy as np

    out = dict(_drawn_inputs(seed))
    spreads = {'L0_gnn_w3_b': (0.0, 0.34),
     'L0_gnn_u3_b': (0.0, 0.299),
     'L0_gnn_w4_b': (0.0, 0.728),
     'L0_gnn_w5_b': (0.0, 0.1),
     'L0_gnn_u5_b': (0.0, 0.1),
     'L2_gnn_b_proj': (0.0, 0.1),
     'L2_gnn_ln_gamma': (1.0, 0.2),
     'L2_gnn_ln_beta': (0.0, 0.1)}
    factors = {'L0_gnn_w4_w': 5.102, 'L3_gnn_a': 36.187}
    for name, (base, spread) in spreads.items():
        noise = np.random.default_rng([zlib.crc32(name.encode()), seed]).standard_normal(out[name].shape)
        drawn = base * np.exp(spread * noise) if base else spread * noise
        out[name] = jnp.asarray(drawn.astype(out[name].dtype))
    for name, factor in factors.items():
        out[name] = (out[name] * factor).astype(out[name].dtype)
    return out
```

```python
from contextlib import ExitStack

import concourse.bass as bass
from concourse import mybir

F32 = mybir.dt.float32
F32R = mybir.dt.float32r
ALU = mybir.AluOpType
ACT = mybir.ActivationFunctionType
AX = mybir.AxisListType

P = 128
STEPS = 3
HEADS = 8
LN_EPS = 1e-5
MASKED = -3.0e38
LEAKY_SLOPE = 0.2

ORDER = [
    ("A", "turn_x", 0), ("B", "norm1", 0),
    ("A", "neighbours", 0), ("B", "products1", 0),
    ("A", "gates", 0), ("B", "relate", 0),
    ("A", "turn_h", 0), ("B", "mix1", 0),
    ("A", "neighbours", 1), ("B", "turn2", 0),
    ("A", "gates", 1), ("B", "qkv", 0), ("B", "scores", 0),
    ("A", "turn_h", 1), ("B", "turn_probs", 0),
    ("A", "neighbours", 2), ("B", "attend", 0),
    ("A", "gates", 2), ("B", "project", 0), ("B", "turn3", 0),
    ("A", "turn_h", 2), ("B", "products3", 0), ("B", "attend3", 0),
]


class Signal:

    def __init__(self, sem, per):
        self.s, self.per = sem, per

    def at(self, g, k):
        return g * self.per + k


def gnn_kernel(nc, x, adj, w3, w3_b, u3, u3_b, w4, w4_b, w5, w5_b, u5, u5_b, Wq, Wk, Wv,
               w_qkv, w_proj, b_proj, ln_gamma, ln_beta, W, a, beta, out):
    BATCH, N, D = x.shape
    T = 4
    GT = T * P
    GROUPS = BATCH * N // GT
    H = D // P
    HD = D // HEADS
    R = P // HD
    SCALE = float(HD) ** -0.5
    assert P == 2 * N and H == 2 and R == 4

    x_g = x.rearrange("(g t b) n d -> g (b n) t d", t=T, b=2)
    out_g = out.rearrange("(g t b) n d -> g (b n) t d", t=T, b=2)

    with ExitStack() as ctx:
        def sb(name, shape, dt=F32):
            return ctx.enter_context(nc.sbuf_tensor(name, shape, dt))

        def sig(name, per=0):
            return Signal(ctx.enter_context(nc.semaphore(name)), per)

        psA = ctx.enter_context(nc.psum_tensor("psA", [P, 4, GT], F32))
        psB = ctx.enter_context(nc.psum_tensor("psB", [P, 4, GT], F32))

        w3h, w3l, w4h, w4l, w5h, w5l, u3h, u3l, wvh, wvl, mh, ml, wph, wpl, w3gh, w3gl = (
            sb(n, [P, H, D], F32R) for n in
            ("w3h", "w3l", "w4h", "w4l", "w5h", "w5l", "u3h", "u3l", "wvh", "wvl", "mh", "ml",
             "wph", "wpl", "w3gh", "w3gl"))
        u5t = sb("u5t", [P, H, D])
        qkvh, qkvl = sb("qkvh", [P, H, 3 * D], F32R), sb("qkvl", [P, H, 3 * D], F32R)
        wah, wal = sb("wah", [P, H, 2], F32R), sb("wal", [P, H, 2], F32R)
        wa2h, wa2l = sb("wa2h", [P, H, P], F32R), sb("wa2l", [P, H, P], F32R)
        wa32 = sb("wa32", [P, H, 2])
        a_sb = sb("a_sb", [P, 2, H])
        biases = sb("biases", [P, 5, H])
        bias_z, bias_r, bias_h = (sb(n, [P, H]) for n in ("bias_z", "bias_r", "bias_h"))
        bproj_bc, gamma_bc, beta_bc = (sb(n, [P, D]) for n in ("bproj_bc", "gamma_bc", "beta_bc"))
        ident = sb("ident", [P, P])
        adj2 = sb("adj2", [P, N])
        adj_bd = sb("adj_bd", [P, P])
        adjT_bd = sb("adjT_bd", [P, P])
        mask_add = sb("mask_add", [P, N])
        beta_col = sb("beta_col", [P, 1])
        beta_eye = sb("beta_eye", [P, N])
        minus_half = sb("minus_half", [P, T])
        ones_col = sb("ones_col", [P, 1])

        x_in = sb("x_in", [P, T, D])
        x_res = sb("x_res", [P, T, D])
        h_tok = sb("h_tok", [P, T, D])
        h = sb("h", [P, H, GT])
        hh, hl = sb("hh", [P, H, GT], F32R), sb("hl", [P, H, GT], F32R)
        ah, al = sb("ah", [P, H, GT], F32R), sb("al", [P, H, GT], F32R)
        tr, rh, tz, th = (sb(n, [P, H, GT]) for n in ("tr", "rh", "tz", "th"))
        pre1 = sb("pre1", [P, T, D])

        y1, y2, y3, y4, pre = (sb(n, [P, T, D]) for n in ("y1", "y2", "y3", "y4", "pre"))
        yTh, yTl = sb("yTh", [P, H, GT], F32R), sb("yTl", [P, H, GT], F32R)
        tTh, tTl = sb("tTh", [P, H, GT], F32R), sb("tTl", [P, H, GT], F32R)
        v1 = sb("v1", [P, T, D])
        relw, relsq = sb("relw", [P, T, P]), sb("relsq", [P, T, P])
        norm2, rnorm = sb("norm2", [P, T]), sb("rnorm", [P, T])
        qk = sb("qk", [P, 2, H, GT])
        vbd = sb("vbd", [P, T, 2, R, H, HD + 1])
        probs = sb("probs", [P, R, T * H, N])
        probsT = sb("probsT", [P, R, GT])
        smax = sb("smax", [P, R * T * H])
        rsum = sb("rsum", [P, T, R, H])
        o_tok = sb("o_tok", [P, T, D])
        s_tok = sb("s_tok", [P, T, 2])
        e3 = sb("e3", [P, T, N])
        e3max, e3sum, e3inv = sb("e3max", [P, T]), sb("e3sum", [P, T]), sb("e3inv", [P, T])
        att_bd, attT = sb("att_bd", [P, T, P]), sb("attT", [P, T, P])
        ln_st, ln_mv = sb("ln_st", [P, T, 6]), sb("ln_mv", [P, T, 2])
        ln_ve, ln_rs = sb("ln_ve", [P, T]), sb("ln_rs", [P, T])

        w3_in = probs[:, :, :, :].rearrange("p r a n -> p (r a n)")[:, 0:4 * D].rearrange(
            "p (c i) -> p c i", c=H)
        w4_in = probs[:, :, :, :].rearrange("p r a n -> p (r a n)")[:, 4 * D:8 * D].rearrange(
            "p (c i) -> p c i", c=H)
        pT_flat = probsT[:, :, :].rearrange("p r n -> p (r n)")
        w5_in = pT_flat[:, 0:4 * D].rearrange("p (c i) -> p c i", c=H)
        u3_in = pT_flat[:, 4 * D:6 * D].rearrange("p (c i) -> p c i", c=H)
        u5_in = pT_flat[:, 6 * D:8 * D].rearrange("p (c i) -> p c i", c=H)
        qk_flat = qk[:, :, :, :].rearrange("p a h n -> p (a h n)")
        Wq_in = qk_flat[:, 0:2 * D].rearrange("p (c i) -> p c i", c=H)
        Wk_in = qk_flat[:, 2 * D:4 * D].rearrange("p (c i) -> p c i", c=H)
        Wv_in = qk_flat[:, 4 * D:6 * D].rearrange("p (c i) -> p c i", c=H)
        W_in = qk_flat[:, 6 * D:8 * D].rearrange("p (c i) -> p c i", c=H)
        WT = v1[:, 0:2, :]
        qkv_in = [y2[:, 0:3, :].rearrange("p t d -> p (t d)"), y3[:, 0:3, :].rearrange("p t d -> p (t d)")]
        wp_in = y1[:, 0:2, :]

        p_load = {n: sig("p_" + n) for n in
                  ("w3", "w4", "w5", "u3", "u5", "wq", "wk", "wv", "qkv", "wp", "W", "a", "adj2",
                   "adjbd", "bias", "rows", "beta")}
        p_ident0, p_ident = sig("p_ident0"), sig("p_ident")
        p_adj0 = sig("p_adj0")
        p_vbd0 = sig("p_vbd0")
        p_fold = sig("p_fold")
        p_turned = sig("p_turned")
        p_hi = sig("p_hi")
        p_lo = sig("p_lo")
        p_wa = sig("p_wa")
        p_wa_sb = sig("p_wa_sb")
        p_small = sig("p_small")
        p_done_act, p_done_dve, p_done_pool = sig("p_done_act"), sig("p_done_dve"), sig("p_done_pool")

        passed_dve, passed_pool = sig("passed_dve"), sig("passed_pool")

        x_loaded = sig("x_loaded", 16)
        x_copied = sig("x_copied", 1)
        xT_ready = sig("xT_ready", H)
        h0_ready = sig("h0_ready", H)
        hh_ready, hl_ready = sig("hh_ready", STEPS * H), sig("hl_ready", STEPS * H)
        aT_ready = sig("aT_ready", STEPS * H)
        ah_ready, al_ready = sig("ah_ready", STEPS * H), sig("al_ready", STEPS * H)
        r_ready, z_ready, v_ready = (sig(n, STEPS * H) for n in ("r_ready", "z_ready", "v_ready"))
        tr_ready, tz_ready, th_ready = (sig(n, STEPS * H) for n in ("tr_ready", "tz_ready", "th_ready"))
        rh_ready = sig("rh_ready", STEPS * H)
        d_ready, zd_ready, hn_ready = (sig(n, STEPS * H) for n in ("d_ready", "zd_ready", "hn_ready"))
        hT_ready = sig("hT_ready", STEPS * 2)
        htok_ready = sig("htok_ready", (STEPS - 1) * 2)
        pre1_ready = sig("pre1_ready", 2)

        ln_stats, ln_aggr = sig("ln_stats", 5 * T), sig("ln_aggr", 5 * T)
        ln_vareps, ln_rstd = sig("ln_vareps", 5), sig("ln_rstd", 5)
        ln_out = sig("ln_out", 5 * T)
        yT_ready, yTh_ready, yTl_ready = (sig(n, 4 * H) for n in ("yT_ready", "yTh_ready", "yTl_ready"))
        tT_ready, tTh_ready, tTl_ready = (sig(n, H) for n in ("tT_ready", "tTh_ready", "tTl_ready"))
        v1_ready, v1_copied = sig("v1_ready", 2), sig("v1_copied", 2)
        rel_ready, relw_ready, relsq_ready = sig("rel_ready", 1), sig("relw_ready", 1), sig("relsq_ready", 1)
        norm2_ready, norm2_copied, rnorm_ready = sig("norm2_ready", 1), sig("norm2_copied", 1), sig("rnorm_ready", 1)
        mix1_ready, pre2_ready = sig("mix1_ready", 2), sig("pre2_ready", T)
        qk_ready, qk_copied = sig("qk_ready", 4), sig("qk_copied", 4)
        v2_ready, v2_copied = sig("v2_ready", 2), sig("v2_copied", 4)
        score_ready, masked_ready, smax_ready = sig("score_ready", 1), sig("masked_ready", R), sig("smax_ready", R)
        shifted_ready, exp_ready = sig("shifted_ready", R), sig("exp_ready", R)
        probT_ready, probT_copied = sig("probT_ready", R), sig("probT_copied", R)
        heads_ready, rsum_ready, o_ready = sig("heads_ready", 1), sig("rsum_ready", 1), sig("o_ready", T)
        proj_ready, o2_ready = sig("proj_ready", 2), sig("o2_ready", 2)
        y2b_ready, res2_ready = sig("y2b_ready", 1), sig("res2_ready", 2)
        gam_ready, pre3_ready = sig("gam_ready", 1), sig("pre3_ready", 1)
        h3_ready, h3_copied = sig("h3_ready", 2), sig("h3_copied", 2)
        s_ready, s_copied, e_sum, e_leaky = sig("s_ready", 2), sig("s_copied", 1), sig("e_sum", 2), sig("e_leaky", 1)
        e_mask, e_max, e_shift, e_exp = sig("e_mask", 1), sig("e_max", 1), sig("e_shift", 1), sig("e_exp", 1)
        e_total, e_inv, e_norm, att_ready = sig("e_total", 1), sig("e_inv", 1), sig("e_norm", 1), sig("att_ready", 2)
        attT_ready, attT_copied = sig("attT_ready", 1), sig("attT_copied", 1)
        mix3_ready, elu_exp, elu_neg, elu_ready = sig("mix3_ready", 2), sig("elu_exp", 2), sig("elu_neg", 2), sig("elu_ready", 2)
        pre4_ready = sig("pre4_ready", 2)
        stored = sig("stored", 16)

        def pairA(use):
            return psA[:, 2 * (use % 2):2 * (use % 2) + 2, :]

        def tok(pair):
            return pair.rearrange("p k (u d) -> p (k u) d", u=2)

        pair0, pair1 = psB[:, 0:2, :], psB[:, 2:4, :]

        def run(eng_chunks, gA, gB):
            for stream, name, step in ORDER:
                if stream == "A" and gA is not None and name in eng_chunks:
                    eng_chunks[name](gA, step)
                if stream == "B" and gB is not None and name in eng_chunks:
                    eng_chunks[name](gB)

        def whole_program(eng, chunks):
            run(chunks, 0, None)
            run(chunks, 1, 0)
            with eng.Fori(1, GROUPS - 1) as g:
                run(chunks, g + 1, g)
            run(chunks, None, GROUPS - 1)

        def first(g):
            return isinstance(g, int) and g == 0

        block = ctx.enter_context(nc.Block())

        @block.sync
        def _(sp):
            sp.dma_start(adj2[0:N, :], adj).then_inc(p_load["adj2"].s, 16)
            sp.dma_start(adj2[N:P, :], adj).then_inc(p_load["adj2"].s, 16)
            for dst, src, n in ((u3_in, u3, "u3"), (w4_in, w4, "w4"), (w3_in, w3, "w3"), (w5_in, w5, "w5"),
                                (u5_in, u5, "u5"), (Wv_in, Wv, "wv"), (Wq_in, Wq, "wq"), (Wk_in, Wk, "wk"),
                                (W_in, W, "W"), (wp_in, w_proj, "wp")):
                sp.dma_start(dst, src.rearrange("(c p) i -> p c i", p=P)).then_inc(p_load[n].s, 16)
            for c in range(H):
                sp.dma_start(qkv_in[c], w_qkv[c * P:(c + 1) * P, :]).then_inc(p_load["qkv"].s, 16)
            sp.wait_ge(p_adj0.s, 1)
            for b in range(2):
                sp.dma_start(adj_bd[b * N:(b + 1) * N, b * N:(b + 1) * N], adj).then_inc(p_load["adjbd"].s, 16)

            def turn_x(g, step):
                if not first(g):
                    sp.wait_ge(x_copied.s, x_copied.at(g - 1, 1))
                    sp.wait_ge(aT_ready.s, aT_ready.at(g - 1, H))
                sp.dma_start(x_in[:, :, :], x_g[bass.ds(g, 1)].rearrange("a p t d -> (a p) t d")
                             ).then_inc(x_loaded.s, 16)

            def attend3(g):
                sp.wait_ge(ln_out.s, ln_out.at(g, 5 * T))
                sp.dma_start(out_g[bass.ds(g, 1)].rearrange("a p t d -> (a p) t d"), y4[:, :, :]
                             ).then_inc(stored.s, 16)

            def run_ahead(gA, gB):
                if gA is not None:
                    turn_x(gA, 0)
                if gB is not None:
                    attend3(gB)

            run_ahead(0, None)
            run_ahead(1, None)
            with sp.Fori(0, GROUPS - 2) as g:
                run_ahead(g + 2, g)
            run_ahead(None, GROUPS - 2)
            run_ahead(None, GROUPS - 1)
            sp.wait_ge(stored.s, stored.at(GROUPS - 1, 16))

        @block.gpsimd
        def _(pool):
            nc.gpsimd.memset(ident[:, :], 0.0).then_inc(p_ident0.s, 1)
            nc.gpsimd.memset(adj_bd[:, :], 0.0).then_inc(p_adj0.s, 1)
            pool.wait_ge(p_ident0.s, 1)
            nc.gpsimd.affine_select(out=ident[:, :], in_=ident[:, :], compare_op=ALU.not_equal, fill=1.0,
                                    base=0, pattern=[[-1, P]], channel_multiplier=1).then_inc(p_ident.s, 1)
            for t, src in enumerate((w3_b, w4_b, w5_b, u3_b, u5_b)):
                for c in range(H):
                    pool.dma_start(biases[:, t, c:c + 1], src[c * P:(c + 1) * P].unsqueeze(1)
                                   ).then_inc(p_load["bias"].s, 16)
            for k in range(2 * H):
                pool.dma_start(a_sb[:, k // H, k % H:k % H + 1], a[k * P:(k + 1) * P, :]).then_inc(p_load["a"].s, 16)
            for dst, src in ((bproj_bc, b_proj), (gamma_bc, ln_gamma), (beta_bc, ln_beta)):
                pool.dma_start(dst[:, :], src.rearrange("(a d) -> a d", a=1).to_broadcast([P, D])
                               ).then_inc(p_load["rows"].s, 16)
            pool.dma_start(beta_col[:, :], beta.rearrange("(a d) -> a d", a=1).to_broadcast([P, 1])
                           ).then_inc(p_load["beta"].s, 16)
            nc.gpsimd.memset(att_bd[:, :, :], 0.0)
            nc.gpsimd.memset(minus_half[:, :], -0.5)
            nc.gpsimd.memset(ones_col[:, :], 1.0)
            nc.gpsimd.memset(vbd[:, :, :, :, :, :], 0.0).then_inc(p_vbd0.s, 1)
            pool.wait_ge(p_vbd0.s, 1)
            for f in range(H):
                last = nc.gpsimd.memset(
                    vbd[f * N:(f + 1) * N, :, :, :, f, HD:HD + 1].rearrange("p t b r o -> p (t b) r o"), 1.0)
            last.then_inc(p_done_pool.s, 1)
            pool.wait_ge(p_done_pool.s, 1)
            pool.wait_ge(p_load["rows"].s, 48)

            def turn_x(g, step):
                if not first(g):
                    pool.wait_ge(pre1_ready.s, pre1_ready.at(g - 1, 2))
                pool.wait_ge(x_loaded.s, x_loaded.at(g, 16))
                pool.sem_inc(passed_pool.s, 1)
                nc.gpsimd.tensor_copy(x_res[:, :, :], x_in[:, :, :]).then_inc(x_copied.s, 1)

            def rstd(g, n):
                pool.wait_ge(ln_vareps.s, ln_vareps.at(g, n + 1))
                nc.gpsimd.tensor_tensor(ln_rs[:, :], ln_ve[:, :], minus_half[:, :], ALU.pow).then_inc(ln_rstd.s, 1)

            def norm1(g):
                rstd(g, 0)

            def relate(g):
                pool.wait_ge(norm2_copied.s, norm2_copied.at(g, 1))
                nc.gpsimd.tensor_tensor(rnorm[:, :], norm2[:, :], minus_half[:, :], ALU.pow).then_inc(rnorm_ready.s, 1)

            def mix1(g):
                rstd(g, 1)

            def qkv(g):
                pool.wait_ge(ln_out.s, ln_out.at(g, 2 * T))
                nc.gpsimd.tensor_tensor(y1[:, :, :], y2[:, :, :], beta_bc[:, :].unsqueeze(1).to_broadcast([P, T, D]),
                                        ALU.add).then_inc(y2b_ready.s, 1)

            def project(g):
                rows = [slice(0, 2), slice(2, 4)]
                for k in range(2):
                    pool.wait_ge(o2_ready.s, o2_ready.at(g, k + 1))
                    if k == 0:
                        pool.wait_ge(y2b_ready.s, y2b_ready.at(g, 1))
                    nc.gpsimd.tensor_tensor(y1[:, rows[k], :], y1[:, rows[k], :], pre[:, rows[k], :],
                                            ALU.add).then_inc(res2_ready.s, 1)
                rstd(g, 2)
                rstd(g, 3)

            def attend3(g):
                for k in range(2):
                    pool.wait_ge(elu_ready.s, elu_ready.at(g, k + 1))
                    nc.gpsimd.tensor_tensor(pre[:, 2 * k:2 * k + 2, :], pre[:, 2 * k:2 * k + 2, :],
                                            y3[:, 2 * k:2 * k + 2, :], ALU.add).then_inc(pre4_ready.s, 1)
                rstd(g, 4)

            whole_program(pool, dict(turn_x=turn_x, norm1=norm1, relate=relate, mix1=mix1, qkv=qkv,
                                     project=project, attend3=attend3))

        @block.tensor
        def _(pe):
            def turn_weight(bank, src):
                for i in range(H):
                    for o in range(H):
                        last = nc.tensor.transpose(bank[:, i * D + o * P:i * D + (o + 1) * P],
                                                   src[:, o, i * P:(i + 1) * P], ident[:, :])
                last.then_inc(p_turned.s, 1)

            pe.wait_ge(p_ident.s, 1)
            pe.wait_ge(p_load["adjbd"].s, 32)
            nc.tensor.transpose(psA[:, 0, 0:P], adj_bd[:, :], ident[:, :]).then_inc(p_turned.s, 1)
            pe.wait_ge(p_load["u3"].s, 16)
            turn_weight(psA[:, 1, :], u3_in)
            for k, (bank, src) in enumerate(((psA[:, 2, :], w4_in), (psA[:, 3, :], w3_in), (psB[:, 0, :], w5_in))):
                pe.wait_ge(p_fold.s, k + 1)
                turn_weight(bank, src)
            pe.wait_ge(p_load["u5"].s, 16)
            turn_weight(psB[:, 1, :], u5_in)
            pe.wait_ge(p_load["wv"].s, 16)
            turn_weight(psB[:, 2, :], Wv_in)
            pe.wait_ge(p_load["wq"].s, 16)
            pe.wait_ge(p_load["wk"].s, 16)
            for i in range(H):
                for c in range(H):
                    last = nc.tensor.matmul(psB[:, 3, i * D:(i + 1) * D], Wq_in[:, c, i * P:(i + 1) * P],
                                            Wk_in[:, c, :], start=(c == 0), stop=(c == H - 1))
            last.then_inc(p_turned.s, 1)
            pe.wait_ge(p_load["W"].s, 16)
            pe.wait_ge(p_hi.s, 1)
            turn_weight(psA[:, 0, :], W_in)
            pe.wait_ge(p_hi.s, 9)
            pe.wait_ge(p_load["a"].s, 32 * H)
            pe.wait_ge(p_lo.s, 1)
            for i in range(H):
                for c in range(H):
                    last = nc.tensor.matmul(psA[:, 1, 2 * i:2 * i + 2], WT[:, c, i * P:(i + 1) * P],
                                            a_sb[:, :, c], start=(c == 0), stop=(c == H - 1))
            last.then_inc(p_wa.s, 1)
            pe.wait_ge(p_done_act.s, 1)
            pe.wait_ge(p_done_dve.s, 1)
            pe.wait_ge(p_done_pool.s, 1)

            def parts3(out, wh, wl, xh, xl, cols, start, stop):
                n = 0
                for c in range(H):
                    for w_, x_ in ((wh, xh), (wh, xl), (wl, xh)):
                        last = nc.tensor.matmul(out, w_[:, c, cols], x_[:, c, :], start=start and n == 0,
                                                stop=stop and n == 3 * H - 1)
                        n += 1
                return last

            def token3(out, t, wh, wl, cols):
                rows = slice(t * P, (t + 1) * P)
                n = 0
                for c in range(H):
                    for x_, w_ in ((yTh, wh), (yTh, wl), (yTl, wh)):
                        last = nc.tensor.matmul(out, x_[:, c, rows], w_[:, c, cols], start=n == 0,
                                                stop=n == 3 * H - 1)
                        n += 1
                return last

            def turn_x(g, step):
                pe.wait_ge(x_loaded.s, x_loaded.at(g, 16))
                for f in range(H):
                    for t in range(T):
                        last = nc.tensor.transpose(pairA(0)[:, f, t * P:(t + 1) * P],
                                                   x_in[:, t, f * P:(f + 1) * P], ident[:, :])
                    last.then_inc(xT_ready.s, 1)

            def neighbours(g, step):
                src = x_in if step == 0 else h_tok
                if step == 0 and not first(g):
                    pe.wait_ge(pre1_ready.s, pre1_ready.at(g - 1, 2))
                if step > 0:
                    pe.wait_ge(htok_ready.s, htok_ready.at(g, 2 * step))
                for f in range(H):
                    for t in range(T):
                        last = nc.tensor.matmul(pairA(1 + 5 * step)[:, f, t * P:(t + 1) * P],
                                                src[:, t, f * P:(f + 1) * P], adjT_bd[:, :],
                                                start=True, stop=True)
                    last.then_inc(aT_ready.s, 1)

            def gates(g, step):
                k = H * step
                pe.wait_ge(hh_ready.s, hh_ready.at(g, k + H))
                pe.wait_ge(hl_ready.s, hl_ready.at(g, k + H))
                for use, wh, wl, ready in ((2, w4h, w4l, r_ready), (3, w3h, w3l, z_ready)):
                    for f in range(H):
                        cols = slice(f * P, (f + 1) * P)
                        if use == 3 and f == 0:
                            pe.wait_ge(al_ready.s, al_ready.at(g, k + H))
                        dst = pairA(use + 5 * step)[:, f, :]
                        parts3(dst, u3h, u3l, hh, hl, cols, True, False)
                        if use == 2:
                            pe.wait_ge(al_ready.s, al_ready.at(g, k + H))
                        parts3(dst, wh, wl, ah, al, cols, False, True).then_inc(ready.s, 1)
                for f in range(H):
                    cols = slice(f * P, (f + 1) * P)
                    dst = pairA(4 + 5 * step)[:, f, :]
                    pe.wait_ge(tr_ready.s, tr_ready.at(g, k + f + 1))
                    parts3(dst, w5h, w5l, ah, al, cols, True, False)
                    for c in range(H):
                        if f == 0:
                            pe.wait_ge(rh_ready.s, rh_ready.at(g, k + c + 1))
                        last = nc.tensor.matmul(dst, u5t[:, c, cols], rh[:, c, :], start=False, stop=(c == H - 1))
                    last.then_inc(v_ready.s, 1)

            def turn_h(g, step):
                dst = tok(pairA(5 + 5 * step))
                for f in range(H):
                    pe.wait_ge(hn_ready.s, hn_ready.at(g, H * step + f + 1))
                    for t in range(T):
                        last = nc.tensor.transpose(dst[:, t, f * P:(f + 1) * P], h[:, f, t * P:(t + 1) * P],
                                                   ident[:, :])
                        if f == H - 1 and t % 2 == 1:
                            last.then_inc(hT_ready.s, 1)

            def turn_y(g, n, src, pair, ready=None, base=0):
                for f in range(H):
                    for t in range(T):
                        if f == 0:
                            pe.wait_ge(ready.s, ready.at(g, base + t + 1))
                        last = nc.tensor.transpose(pair[:, f, t * P:(t + 1) * P],
                                                   src[:, t, f * P:(f + 1) * P], ident[:, :])
                    last.then_inc(yT_ready.s, 1)

            def split_done(g, n):
                pe.wait_ge(yTh_ready.s, yTh_ready.at(g, (n + 1) * H))
                pe.wait_ge(yTl_ready.s, yTl_ready.at(g, (n + 1) * H))

            def norm1(g):
                if not first(g):
                    pe.wait_ge(attT_copied.s, attT_copied.at(g - 1, 1))
                turn_y(g, 0, y1, pair0, ln_out, 0)

            def products1(g):
                split_done(g, 0)
                if not first(g):
                    pe.wait_ge(elu_ready.s, elu_ready.at(g - 1, 2))
                for f in range(H):
                    parts3(pair1[:, f, :], mh, ml, yTh, yTl, slice(f * P, (f + 1) * P), True, True
                           ).then_inc(tT_ready.s, 1)
                for t in range(T):
                    last = token3(tok(pair0)[:, t, :], t, wvh, wvl, slice(0, D))
                    if t % 2 == 1:
                        last.then_inc(v1_ready.s, 1)

            def relate(g):
                pe.wait_ge(tTh_ready.s, tTh_ready.at(g, H))
                pe.wait_ge(tTl_ready.s, tTl_ready.at(g, H))
                for t in range(T):
                    cols = slice(t * P, (t + 1) * P)
                    n = 0
                    for c in range(H):
                        for y_, t_ in ((yTh, tTh), (yTh, tTl), (yTl, tTh)):
                            last = nc.tensor.matmul(pair1[:, 0, cols], y_[:, c, cols], t_[:, c, cols],
                                                    start=n == 0, stop=n == 3 * H - 1)
                            n += 1
                last.then_inc(rel_ready.s, 1)
                pe.wait_ge(relsq_ready.s, relsq_ready.at(g, 1))
                for t in range(T):
                    last = nc.tensor.matmul(pair1[:, 1, t:t + 1], relsq[:, t, :], ones_col[:, :],
                                            start=True, stop=True)
                last.then_inc(norm2_ready.s, 1)

            def mix1(g):
                pe.wait_ge(v1_copied.s, v1_copied.at(g, 2))
                for t in range(T):
                    last = nc.tensor.matmul(tok(pair0)[:, t, :], relw[:, t, :], v1[:, t, :], start=True, stop=True)
                    if t % 2 == 1:
                        last.then_inc(mix1_ready.s, 1)

            def turn2(g):
                pe.wait_ge(norm2_copied.s, norm2_copied.at(g, 1))
                turn_y(g, 1, y2, pair1, ln_out, T)

            def qkv(g):
                split_done(g, 1)
                for i, pair in enumerate((pair0, pair1)):
                    for f in range(H):
                        parts3(pair[:, f, :], qkvh, qkvl, yTh, yTl, slice(i * D + f * P, i * D + (f + 1) * P),
                               True, True).then_inc(qk_ready.s, 1)
                pe.wait_ge(qk_copied.s, qk_copied.at(g, 2))
                for t in range(T):
                    last = token3(tok(pair0)[:, t, :], t, qkvh, qkvl, slice(2 * D, 3 * D))
                    if t % 2 == 1:
                        last.then_inc(v2_ready.s, 1)

            def scores(g):
                pe.wait_ge(qk_copied.s, qk_copied.at(g, 4))
                pe.wait_ge(v2_copied.s, v2_copied.at(g, 4))
                for t in range(T):
                    for f in range(H):
                        for b in range(2):
                            cols = slice(t * P + b * N, t * P + (b + 1) * N)
                            for r in range(R):
                                rows = slice(r * HD, (r + 1) * HD)
                                last = nc.tensor.matmul(
                                    psB[b * N:(b + 1) * N, r, (t * H + f) * N:(t * H + f + 1) * N],
                                    qk[rows, 0, f, cols], qk[rows, 1, f, cols], start=True, stop=True)
                last.then_inc(score_ready.s, 1)

            def turn_probs(g):
                for r in range(R):
                    pe.wait_ge(exp_ready.s, exp_ready.at(g, r + 1))
                    for t in range(T):
                        last = nc.tensor.transpose(
                            psB[:, r, t * P:(t + 1) * P],
                            probs[:, r, t * H:(t + 1) * H, :].rearrange("p f n -> p (f n)"), ident[:, :])
                    last.then_inc(probT_ready.s, 1)

            def attend(g):
                pe.wait_ge(probT_copied.s, probT_copied.at(g, R))
                for t in range(T):
                    for b in range(2):
                        for r in range(R):
                            last = nc.tensor.matmul(
                                psB[b * N:(b + 1) * N, t, r * H * (HD + 1):(r + 1) * H * (HD + 1)],
                                probsT[:, r, t * P + b * N:t * P + (b + 1) * N],
                                vbd[:, t, b, r, :, :].rearrange("p f d -> p (f d)"), start=True, stop=True)
                last.then_inc(heads_ready.s, 1)

            def project(g):
                pe.wait_ge(o_ready.s, o_ready.at(g, T))
                turn_y(g, 2, o_tok, pair0, o_ready, 0)
                split_done(g, 2)
                for t in range(T):
                    last = token3(tok(pair1)[:, t, :], t, wph, wpl, slice(0, D))
                    if t % 2 == 1:
                        last.then_inc(proj_ready.s, 1)

            def turn3(g):
                turn_y(g, 3, y3, pair0, ln_out, 3 * T)

            def products3(g):
                split_done(g, 3)
                for t in range(T):
                    last = token3(pair0[:, 0, 2 * t:2 * t + 2], t, wah, wal, slice(0, 2))
                last.then_inc(s_ready.s, 1)
                parts3(pair0[:, 1, :], wa2h, wa2l, yTh, yTl, slice(0, P), True, True).then_inc(s_ready.s, 1)
                for t in range(T):
                    last = token3(tok(pair1)[:, t, :], t, w3gh, w3gl, slice(0, D))
                    if t % 2 == 1:
                        last.then_inc(h3_ready.s, 1)

            def attend3(g):
                pe.wait_ge(att_ready.s, att_ready.at(g, 2))
                for t in range(T):
                    last = nc.tensor.transpose(pair0[:, 0, t * P:(t + 1) * P], att_bd[:, t, :], ident[:, :])
                last.then_inc(attT_ready.s, 1)
                pe.wait_ge(h3_copied.s, h3_copied.at(g, 2))
                pe.wait_ge(attT_copied.s, attT_copied.at(g, 1))
                for t in range(T):
                    last = nc.tensor.matmul(tok(pair1)[:, t, :], attT[:, t, :], v1[:, t, :], start=True, stop=True)
                    if t % 2 == 1:
                        last.then_inc(mix3_ready.s, 1)

            whole_program(pe, dict(turn_x=turn_x, neighbours=neighbours, gates=gates, turn_h=turn_h,
                                   norm1=norm1, products1=products1, relate=relate, mix1=mix1, turn2=turn2,
                                   qkv=qkv, scores=scores, turn_probs=turn_probs, attend=attend,
                                   project=project, turn3=turn3, products3=products3, attend3=attend3))

        @block.scalar
        def _(act):
            whole = lambda w_: w_[:, :, :].rearrange("p c o -> p (c o)")
            act.wait_ge(p_turned.s, 1)
            nc.scalar.copy(adjT_bd[:, :], psA[:, 0, 0:P]).then_inc(p_hi.s, 1)
            for k, (dst, bank) in enumerate(((u3h, psA[:, 1, :]), (w4h, psA[:, 2, :]), (w3h, psA[:, 3, :]),
                                             (w5h, psB[:, 0, :]))):
                act.wait_ge(p_turned.s, k + 2)
                nc.scalar.copy(whole(dst), bank).then_inc(p_hi.s, 1)
            act.wait_ge(p_turned.s, 6)
            nc.scalar.mul(whole(u5t), psB[:, 1, :], 0.5).then_inc(p_hi.s, 1)
            for k, (dst, bank) in enumerate(((wvh, psB[:, 2, :]), (mh, psB[:, 3, :]))):
                act.wait_ge(p_turned.s, k + 7)
                nc.scalar.copy(whole(dst), bank).then_inc(p_hi.s, 1)
            act.wait_ge(p_turned.s, 9)
            nc.scalar.copy(WT.rearrange("p c o -> p (c o)"), psA[:, 0, :]).then_inc(p_hi.s, 1)
            act.wait_ge(p_load["qkv"].s, 32)
            for c in range(H):
                nc.scalar.copy(qkvh[:, c, :], qkv_in[c]).then_inc(p_hi.s, 1)
            act.wait_ge(p_load["wp"].s, 16)
            nc.scalar.copy(wph[:, :, :], wp_in).then_inc(p_hi.s, 1)
            act.wait_ge(p_load["W"].s, 16)
            nc.scalar.copy(w3gh[:, :, :], W_in).then_inc(p_hi.s, 1)
            act.wait_ge(p_wa.s, 1)
            nc.scalar.copy(wa32[:, :, :].rearrange("p c w -> p (c w)"), psA[:, 1, 0:2 * H]).then_inc(p_wa_sb.s, 1)
            act.wait_ge(p_wa_sb.s, 1)
            nc.scalar.copy(wah[:, :, :], wa32[:, :, :]).then_inc(p_hi.s, 1)
            for c in range(H):
                last = nc.scalar.copy(wa2h[:, c, :], wa32[:, c, 1:2].to_broadcast([P, P]))
                last.then_inc(p_hi.s, 1)
            act.wait_ge(p_hi.s, 16)
            act.wait_ge(p_small.s, 5)
            act.sem_inc(p_done_act.s, 1)

            def turn_x(g, step):
                for f in range(H):
                    act.wait_ge(xT_ready.s, xT_ready.at(g, f + 1))
                    nc.scalar.copy(h[:, f, :], pairA(0)[:, f, :]).then_inc(h0_ready.s, 1)
                split_h(g, 0)

            def split_h(g, step):
                for f in range(H):
                    if step == 0:
                        act.wait_ge(h0_ready.s, h0_ready.at(g, f + 1))
                    else:
                        act.wait_ge(hn_ready.s, hn_ready.at(g, (step - 1) * H + f + 1))
                    nc.scalar.copy(hh[:, f, :], h[:, f, :]).then_inc(hh_ready.s, 1)

            def neighbours(g, step):
                for f in range(H):
                    act.wait_ge(aT_ready.s, aT_ready.at(g, step * H + f + 1))
                    nc.scalar.copy(ah[:, f, :], pairA(1 + 5 * step)[:, f, :]).then_inc(ah_ready.s, 1)

            def gates(g, step):
                for use, dst, bias, scale, ready, done in (
                        (2, tr, bias_r, 0.5, r_ready, tr_ready), (3, tz, bias_z, 0.5, z_ready, tz_ready),
                        (4, th, bias_h, 1.0, v_ready, th_ready)):
                    for f in range(H):
                        act.wait_ge(ready.s, ready.at(g, step * H + f + 1))
                        nc.scalar.activation(dst[:, f, :], pairA(use + 5 * step)[:, f, :], ACT.Tanh,
                                             bias=bias[:, f:f + 1], scale=scale).then_inc(done.s, 1)

            def turn_h(g, step):
                if step == STEPS - 1:
                    return
                dst = tok(pairA(5 + 5 * step))
                for k in range(2):
                    act.wait_ge(hT_ready.s, hT_ready.at(g, 2 * step + k + 1))
                    nc.scalar.copy(h_tok[:, 2 * k:2 * k + 2, :], dst[:, 2 * k:2 * k + 2, :]).then_inc(htok_ready.s, 1)
                split_h(g, step + 1)

            def turned(g, n, pair):
                for f in range(H):
                    act.wait_ge(yT_ready.s, yT_ready.at(g, n * H + f + 1))
                    nc.scalar.copy(yTh[:, f, :], pair[:, f, :]).then_inc(yTh_ready.s, 1)

            def norm1(g):
                turned(g, 0, pair0)

            def products1(g):
                for f in range(H):
                    act.wait_ge(tT_ready.s, tT_ready.at(g, f + 1))
                    nc.scalar.copy(tTh[:, f, :], pair1[:, f, :]).then_inc(tTh_ready.s, 1)
                for k in range(2):
                    act.wait_ge(v1_ready.s, v1_ready.at(g, k + 1))
                    nc.scalar.copy(v1[:, 2 * k:2 * k + 2, :], tok(pair0)[:, 2 * k:2 * k + 2, :]).then_inc(v1_copied.s, 1)

            def relate(g):
                act.wait_ge(relw_ready.s, relw_ready.at(g, 1))
                nc.scalar.activation(relsq[:, :, :], relw[:, :, :], ACT.Square).then_inc(relsq_ready.s, 1)

            def turn2(g):
                turned(g, 1, pair1)

            def qkv(g):
                for i, pair in enumerate((pair0, pair1)):
                    for f in range(H):
                        act.wait_ge(qk_ready.s, qk_ready.at(g, i * H + f + 1))
                        nc.scalar.copy(qk[:, i, f, :], pair[:, f, :]).then_inc(qk_copied.s, 1)

            def scores(g):
                for r in range(R):
                    act.wait_ge(shifted_ready.s, shifted_ready.at(g, r + 1))
                    nc.scalar.activation(probs[:, r, :, :], probs[:, r, :, :], ACT.Exp, scale=SCALE
                                         ).then_inc(exp_ready.s, 1)

            def turn_probs(g):
                for r in range(R):
                    act.wait_ge(probT_ready.s, probT_ready.at(g, r + 1))
                    nc.scalar.copy(probsT[:, r, :], psB[:, r, :]).then_inc(probT_copied.s, 1)

            def project(g):
                turned(g, 2, pair0)

            def turn3(g):
                turned(g, 3, pair0)

            def products3(g):
                for k in range(2):
                    act.wait_ge(h3_ready.s, h3_ready.at(g, k + 1))
                    nc.scalar.copy(v1[:, 2 * k:2 * k + 2, :], tok(pair1)[:, 2 * k:2 * k + 2, :]).then_inc(h3_copied.s, 1)

            def attend3(g):
                act.wait_ge(e_shift.s, e_shift.at(g, 1))
                nc.scalar.activation(e3[:, :, :], e3[:, :, :], ACT.Exp).then_inc(e_exp.s, 1)
                act.wait_ge(attT_ready.s, attT_ready.at(g, 1))
                nc.scalar.copy(attT[:, :, :].rearrange("p t n -> p (t n)"), pair0[:, 0, :]).then_inc(attT_copied.s, 1)
                for k in range(2):
                    act.wait_ge(mix3_ready.s, mix3_ready.at(g, k + 1))
                    nc.scalar.activation(o_tok[:, 2 * k:2 * k + 2, :], tok(pair1)[:, 2 * k:2 * k + 2, :], ACT.Exp
                                         ).then_inc(elu_exp.s, 1)

            whole_program(act, dict(turn_x=turn_x, neighbours=neighbours, gates=gates, turn_h=turn_h,
                                    norm1=norm1, products1=products1, relate=relate, turn2=turn2, qkv=qkv,
                                    scores=scores, turn_probs=turn_probs, project=project, turn3=turn3,
                                    products3=products3, attend3=attend3))

        @block.vector
        def _(dve):
            f32 = lambda ap: ap.bitcast(F32)
            TT = nc.vector.tensor_tensor
            whole = lambda w_: w_[:, :, :].rearrange("p c o -> p (c o)")
            for w_, n in ((w4_in, "w4"), (w3_in, "w3"), (w5_in, "w5")):
                dve.wait_ge(p_load[n].s, 16)
                TT(w_[:, :, 0:D], w_[:, :, 0:D], w_[:, :, D:2 * D], ALU.add).then_inc(p_fold.s, 1)
            for k, (hi, lo, src) in enumerate(((u3h, u3l, psA[:, 1, :]), (w4h, w4l, psA[:, 2, :]),
                                               (w3h, w3l, psA[:, 3, :]), (w5h, w5l, psB[:, 0, :]))):
                dve.wait_ge(p_hi.s, k + 2)
                TT(whole(lo), src, f32(whole(hi)), ALU.subtract).then_inc(p_lo.s, 1)
            for k, (hi, lo, src) in enumerate(((wvh, wvl, psB[:, 2, :]), (mh, ml, psB[:, 3, :]))):
                dve.wait_ge(p_hi.s, k + 7)
                TT(whole(lo), src, f32(whole(hi)), ALU.subtract).then_inc(p_lo.s, 1)
            for c in range(H):
                dve.wait_ge(p_hi.s, 10 + c)
                TT(qkvl[:, c, :], qkv_in[c], f32(qkvh[:, c, :]), ALU.subtract).then_inc(p_lo.s, 1)
            dve.wait_ge(p_hi.s, 12)
            TT(wpl[:, :, :], wp_in, f32(wph[:, :, :]), ALU.subtract).then_inc(p_lo.s, 1)
            dve.wait_ge(p_hi.s, 13)
            TT(w3gl[:, :, :], W_in, f32(w3gh[:, :, :]), ALU.subtract).then_inc(p_lo.s, 1)
            dve.wait_ge(p_load["adj2"].s, 32)
            nc.vector.tensor_scalar(mask_add[:, :], adj2[:, :], 0.0, MASKED, ALU.is_equal, ALU.mult).then_inc(p_small.s, 1)
            dve.wait_ge(p_load["beta"].s, 16)
            dve.wait_ge(p_ident.s, 1)
            for b in range(2):
                rows = slice(b * N, (b + 1) * N)
                nc.vector.tensor_scalar(beta_eye[rows, :], ident[rows, rows], beta_col[rows, 0:1], None, ALU.mult
                                        ).then_inc(p_small.s, 1)
            dve.wait_ge(p_load["bias"].s, 80 * H)
            TT(bias_z[:, :], biases[:, 0, :], biases[:, 3, :], ALU.add).then_inc(p_small.s, 1)
            TT(bias_r[:, :], biases[:, 1, :], biases[:, 3, :], ALU.add).then_inc(p_small.s, 1)
            TT(bias_h[:, :], biases[:, 2, :], biases[:, 4, :], ALU.add).then_inc(p_small.s, 1)
            dve.wait_ge(p_small.s, 6)
            nc.vector.tensor_scalar(bias_z[:, :], bias_z[:, :], 0.5, None, ALU.mult).then_inc(p_small.s, 1)
            nc.vector.tensor_scalar(bias_r[:, :], bias_r[:, :], 0.5, None, ALU.mult).then_inc(p_small.s, 1)
            dve.wait_ge(p_hi.s, 14)
            TT(wal[:, :, :], wa32[:, :, :], f32(wah[:, :, :]), ALU.subtract).then_inc(p_lo.s, 1)
            for c in range(H):
                dve.wait_ge(p_hi.s, 15 + c)
                TT(wa2l[:, c, :], wa32[:, c, 1:2].to_broadcast([P, P]), f32(wa2h[:, c, :]), ALU.subtract
                   ).then_inc(p_lo.s, 1)
            dve.wait_ge(p_load["rows"].s, 48)
            dve.wait_ge(p_lo.s, 13)
            dve.wait_ge(p_small.s, 8)
            dve.sem_inc(p_done_dve.s, 1)

            def split_h(g, step):
                for f in range(H):
                    dve.wait_ge(hh_ready.s, hh_ready.at(g, step * H + f + 1))
                    TT(hl[:, f, :], h[:, f, :], f32(hh[:, f, :]), ALU.subtract).then_inc(hl_ready.s, 1)

            def turn_x(g, step):
                split_h(g, 0)

            def neighbours(g, step):
                for f in range(H):
                    dve.wait_ge(ah_ready.s, ah_ready.at(g, step * H + f + 1))
                    TT(al[:, f, :], pairA(1 + 5 * step)[:, f, :], f32(ah[:, f, :]), ALU.subtract).then_inc(al_ready.s, 1)

            def gates(g, step):
                k = step * H
                for f in range(H):
                    dve.wait_ge(tr_ready.s, tr_ready.at(g, k + f + 1))
                    nc.vector.scalar_tensor_tensor(out=rh[:, f, :], in0=tr[:, f, :], scalar=1.0, in1=h[:, f, :],
                                                   op0=ALU.add, op1=ALU.mult).then_inc(rh_ready.s, 1)
                for f in range(H):
                    dve.wait_ge(th_ready.s, th_ready.at(g, k + f + 1))
                    TT(th[:, f, :], th[:, f, :], h[:, f, :], ALU.subtract).then_inc(d_ready.s, 1)
                for f in range(H):
                    dve.wait_ge(tz_ready.s, tz_ready.at(g, k + f + 1))
                    dve.wait_ge(d_ready.s, d_ready.at(g, k + f + 1))
                    nc.vector.scalar_tensor_tensor(out=th[:, f, :], in0=tz[:, f, :], scalar=1.0, in1=th[:, f, :],
                                                   op0=ALU.add, op1=ALU.mult).then_inc(zd_ready.s, 1)
                for f in range(H):
                    dve.wait_ge(zd_ready.s, zd_ready.at(g, k + f + 1))
                    nc.vector.scalar_tensor_tensor(out=h[:, f, :], in0=th[:, f, :], scalar=0.5, in1=h[:, f, :],
                                                   op0=ALU.mult, op1=ALU.add).then_inc(hn_ready.s, 1)

            def turn_h(g, step):
                if step < STEPS - 1:
                    split_h(g, step + 1)
                    return
                src = tok(pairA(5 + 5 * step))
                dve.wait_ge(x_copied.s, x_copied.at(g, 1))
                for k in range(2):
                    dve.wait_ge(hT_ready.s, hT_ready.at(g, 2 * step + k + 1))
                    TT(pre1[:, 2 * k:2 * k + 2, :], src[:, 2 * k:2 * k + 2, :], x_res[:, 2 * k:2 * k + 2, :], ALU.add
                       ).then_inc(pre1_ready.s, 1)

            def layer_norm(g, n, src, dst, ready):
                for t in range(T):
                    ready(t)
                    nc.vector.bn_stats(ln_st[:, t, :], src[:, t, :]).then_inc(ln_stats.s, 1)
                dve.wait_ge(ln_stats.s, ln_stats.at(g, (n + 1) * T))
                dve.sem_inc(passed_dve.s, 1)
                for t in range(T):
                    nc.vector.bn_aggr(ln_mv[:, t, :], ln_st[:, t, :]).then_inc(ln_aggr.s, 1)
                dve.wait_ge(ln_aggr.s, ln_aggr.at(g, (n + 1) * T))
                nc.vector.tensor_scalar(ln_ve[:, :], ln_mv[:, :, 1], LN_EPS, None, ALU.add).then_inc(ln_vareps.s, 1)
                dve.wait_ge(ln_rstd.s, ln_rstd.at(g, n + 1))
                for t in range(T):
                    nc.vector.tensor_scalar(dst[:, t, :], src[:, t, :], ln_mv[:, t, 0:1], ln_rs[:, t:t + 1],
                                            ALU.subtract, ALU.mult).then_inc(ln_out.s, 1)

            def turned(g, n, pair):
                for f in range(H):
                    dve.wait_ge(yTh_ready.s, yTh_ready.at(g, n * H + f + 1))
                    TT(yTl[:, f, :], pair[:, f, :], f32(yTh[:, f, :]), ALU.subtract).then_inc(yTl_ready.s, 1)

            def norm1(g):
                layer_norm(g, 0, pre1, y1,
                           lambda t: dve.wait_ge(pre1_ready.s, pre1_ready.at(g, t // 2 + 1)))
                turned(g, 0, pair0)

            def products1(g):
                for f in range(H):
                    dve.wait_ge(tTh_ready.s, tTh_ready.at(g, f + 1))
                    TT(tTl[:, f, :], pair1[:, f, :], f32(tTh[:, f, :]), ALU.subtract).then_inc(tTl_ready.s, 1)

            def relate(g):
                dve.wait_ge(rel_ready.s, rel_ready.at(g, 1))
                TT(relw[:, :, :], pair1[:, 0, :].rearrange("p (t n) -> p t n", t=T),
                   adj_bd[:, :].unsqueeze(1).to_broadcast([P, T, P]), ALU.mult).then_inc(relw_ready.s, 1)
                dve.wait_ge(norm2_ready.s, norm2_ready.at(g, 1))
                nc.vector.tensor_copy(norm2[:, :], pair1[:, 1, 0:T]).then_inc(norm2_copied.s, 1)

            def mix1(g):
                dve.wait_ge(rnorm_ready.s, rnorm_ready.at(g, 1))
                for t in range(T):
                    dve.wait_ge(mix1_ready.s, mix1_ready.at(g, t // 2 + 1))
                    nc.vector.scalar_tensor_tensor(out=pre[:, t, :], in0=tok(pair0)[:, t, :], scalar=rnorm[:, t:t + 1],
                                                   in1=y1[:, t, :], op0=ALU.mult, op1=ALU.add).then_inc(pre2_ready.s, 1)
                layer_norm(g, 1, pre, y2, lambda t: dve.wait_ge(pre2_ready.s, pre2_ready.at(g, t + 1)))

            def turn2(g):
                turned(g, 1, pair1)

            def qkv(g):
                for b in range(2):
                    for f in range(H):
                        dve.wait_ge(v2_ready.s, v2_ready.at(g, 2))
                        src = tok(pair0)[b * N:(b + 1) * N, :, f * P:(f + 1) * P].rearrange(
                            "p t (r d) -> p t r d", r=R)
                        nc.vector.tensor_copy(vbd[f * N:(f + 1) * N, :, b, :, f, 0:HD], src).then_inc(v2_copied.s, 1)

            def scores(g):
                dve.wait_ge(score_ready.s, score_ready.at(g, 1))
                for r in range(R):
                    TT(probs[:, r, :, :], psB[:, r, :].rearrange("p (a n) -> p a n", n=N),
                       mask_add[:, :].unsqueeze(1).to_broadcast([P, T * H, N]), ALU.add).then_inc(masked_ready.s, 1)
                for r in range(R):
                    dve.wait_ge(masked_ready.s, masked_ready.at(g, r + 1))
                    nc.vector.tensor_reduce(smax[:, r * T * H:(r + 1) * T * H], probs[:, r, :, :], AX.X, ALU.max
                                            ).then_inc(smax_ready.s, 1)
                for r in range(R):
                    dve.wait_ge(smax_ready.s, smax_ready.at(g, r + 1))
                    TT(probs[:, r, :, :], probs[:, r, :, :],
                       smax[:, r * T * H:(r + 1) * T * H].unsqueeze(2).to_broadcast([P, T * H, N]), ALU.subtract
                       ).then_inc(shifted_ready.s, 1)

            def attend(g):
                dve.wait_ge(heads_ready.s, heads_ready.at(g, 1))
                heads = psB[:, :, 0:R * H * (HD + 1)].rearrange("p t (r f c) -> p t r f c", r=R, f=H)
                nc.vector.reciprocal(rsum[:, :, :, :], heads[:, :, :, :, HD]).then_inc(rsum_ready.s, 1)
                dve.wait_ge(rsum_ready.s, rsum_ready.at(g, 1))
                for t in range(T):
                    TT(o_tok[:, t, :].rearrange("p (f r d) -> p r f d", f=H, r=R), heads[:, t, :, :, 0:HD],
                       rsum[:, t, :, :].unsqueeze(3).to_broadcast([P, R, H, HD]), ALU.mult).then_inc(o_ready.s, 1)

            def project(g):
                turned(g, 2, pair0)
                for k in range(2):
                    dve.wait_ge(proj_ready.s, proj_ready.at(g, k + 1))
                    TT(pre[:, 2 * k:2 * k + 2, :], tok(pair1)[:, 2 * k:2 * k + 2, :],
                       bproj_bc[:, :].unsqueeze(1).to_broadcast([P, 2, D]), ALU.add).then_inc(o2_ready.s, 1)
                layer_norm(g, 2, pre, o_tok, lambda t: dve.wait_ge(o2_ready.s, o2_ready.at(g, t // 2 + 1)))
                dve.wait_ge(ln_out.s, ln_out.at(g, 3 * T))
                TT(o_tok[:, :, :], o_tok[:, :, :], gamma_bc[:, :].unsqueeze(1).to_broadcast([P, T, D]), ALU.mult
                   ).then_inc(gam_ready.s, 1)
                dve.wait_ge(gam_ready.s, gam_ready.at(g, 1))
                dve.wait_ge(res2_ready.s, res2_ready.at(g, 2))
                TT(pre[:, :, :], o_tok[:, :, :], y1[:, :, :], ALU.add).then_inc(pre3_ready.s, 1)
                layer_norm(g, 3, pre, y3, lambda t: dve.wait_ge(pre3_ready.s, pre3_ready.at(g, 1)))

            def turn3(g):
                turned(g, 3, pair0)

            def products3(g):
                dve.wait_ge(s_ready.s, s_ready.at(g, 1))
                nc.vector.tensor_copy(s_tok[:, :, :].rearrange("p t w -> p (t w)"), pair0[:, 0, 0:2 * T]).then_inc(s_copied.s, 1)
                dve.wait_ge(s_copied.s, s_copied.at(g, 1))
                dve.wait_ge(s_ready.s, s_ready.at(g, 2))
                for b in range(2):
                    rows = slice(b * N, (b + 1) * N)
                    TT(e3[rows, :, :], pair0[rows, 1, :].rearrange("p (t b j) -> p t b j", t=T, b=2)[:, :, b, :],
                       s_tok[rows, :, 0:1].to_broadcast([N, T, N]), ALU.add).then_inc(e_sum.s, 1)
                dve.wait_ge(e_sum.s, e_sum.at(g, 2))
                nc.vector.scalar_tensor_tensor(out=e3[:, :, :], in0=e3[:, :, :], scalar=LEAKY_SLOPE, in1=e3[:, :, :],
                                               op0=ALU.mult, op1=ALU.max).then_inc(e_leaky.s, 1)
                dve.wait_ge(e_leaky.s, e_leaky.at(g, 1))
                TT(e3[:, :, :], e3[:, :, :], adj2[:, :].unsqueeze(1).to_broadcast([P, T, N]), ALU.mult).then_inc(e_mask.s, 1)
                dve.wait_ge(e_mask.s, e_mask.at(g, 1))
                nc.vector.tensor_reduce(e3max[:, :], e3[:, :, :], AX.X, ALU.max).then_inc(e_max.s, 1)
                dve.wait_ge(e_max.s, e_max.at(g, 1))
                TT(e3[:, :, :], e3[:, :, :], e3max[:, :].unsqueeze(2).to_broadcast([P, T, N]), ALU.subtract).then_inc(e_shift.s, 1)

            def attend3(g):
                dve.wait_ge(e_exp.s, e_exp.at(g, 1))
                nc.vector.tensor_reduce(e3sum[:, :], e3[:, :, :], AX.X, ALU.add).then_inc(e_total.s, 1)
                dve.wait_ge(e_total.s, e_total.at(g, 1))
                nc.vector.reciprocal(e3inv[:, :], e3sum[:, :]).then_inc(e_inv.s, 1)
                dve.wait_ge(e_inv.s, e_inv.at(g, 1))
                TT(e3[:, :, :], e3[:, :, :], e3inv[:, :].unsqueeze(2).to_broadcast([P, T, N]), ALU.mult).then_inc(e_norm.s, 1)
                dve.wait_ge(e_norm.s, e_norm.at(g, 1))
                for b in range(2):
                    rows = slice(b * N, (b + 1) * N)
                    TT(att_bd[rows, :, rows], e3[rows, :, :], beta_eye[rows, :].unsqueeze(1).to_broadcast([N, T, N]),
                       ALU.add).then_inc(att_ready.s, 1)
                for k in range(2):
                    rows = slice(2 * k, 2 * k + 2)
                    dve.wait_ge(elu_exp.s, elu_exp.at(g, k + 1))
                    nc.vector.tensor_scalar(o_tok[:, rows, :], o_tok[:, rows, :], 1.0, -1.0, ALU.min, ALU.add).then_inc(elu_neg.s, 1)
                for k in range(2):
                    rows = slice(2 * k, 2 * k + 2)
                    dve.wait_ge(elu_neg.s, elu_neg.at(g, k + 1))
                    TT(pre[:, rows, :], tok(pair1)[:, rows, :], o_tok[:, rows, :], ALU.max).then_inc(elu_ready.s, 1)
                if not first(g):
                    dve.wait_ge(stored.s, stored.at(g - 1, 16))
                layer_norm(g, 4, pre, y4, lambda t: dve.wait_ge(pre4_ready.s, pre4_ready.at(g, t // 2 + 1)))

            whole_program(dve, dict(turn_x=turn_x, neighbours=neighbours, gates=gates, turn_h=turn_h,
                                    norm1=norm1, products1=products1, relate=relate, mix1=mix1, turn2=turn2,
                                    qkv=qkv, scores=scores, attend=attend, project=project, turn3=turn3,
                                    products3=products3, attend3=attend3))


_INS = ['x', 'adj', 'L0_gnn_w3_w', 'L0_gnn_w3_b', 'L0_gnn_u3_w', 'L0_gnn_u3_b', 'L0_gnn_w4_w', 'L0_gnn_w4_b',
        'L0_gnn_w5_w', 'L0_gnn_w5_b', 'L0_gnn_u5_w', 'L0_gnn_u5_b', 'L1_gnn_Wq', 'L1_gnn_Wk', 'L1_gnn_Wv',
        'L2_gnn_w_qkv', 'L2_gnn_w_proj', 'L2_gnn_b_proj', 'L2_gnn_ln_gamma', 'L2_gnn_ln_beta', 'L3_gnn_W',
        'L3_gnn_a', 'L3_gnn_beta']
_OUTS = [((128, 64, 256), 'float32')]


def kernel(**inputs):
    import numpy as _np
    import concourse.bacc as _bacc
    from concourse import mybir as _mybir
    from concourse.bass_utils import run_bass_kernel_spmd as _run

    nc = _bacc.Bacc("TRN2", target_bir_lowering=False, num_devices=1)
    arrays, args = {}, []
    for name in _INS:
        arr = _np.ascontiguousarray(inputs[name])
        arrays[f"in_{name}_dram"] = arr
        args.append(nc.dram_tensor(f"in_{name}_dram", arr.shape, _mybir.dt.from_np(arr.dtype), kind="ExternalInput").ap())
    for i, (shape, dtype) in enumerate(_OUTS):
        dt = _mybir.dt.from_np(_np.dtype(dtype))
        args.append(nc.dram_tensor(f"out_{i}_dram", shape, dt, kind="ExternalOutput").ap())
    gnn_kernel(nc, *args)
    r = _run(nc, [arrays], core_ids=[0])
    got = tuple(r.results[0][f"out_{i}_dram"] for i in range(len(_OUTS)))
    return got[0]
```

```python
from contextlib import ExitStack

import concourse.bass as bass
from concourse import mybir

F32 = mybir.dt.float32
F32R = mybir.dt.float32r
ALU = mybir.AluOpType
ACT = mybir.ActivationFunctionType
AX = mybir.AxisListType

P = 128
STEPS = 3
HEADS = 8
LN_EPS = 1e-5
MASKED = -3.0e38
LEAKY_SLOPE = 0.2

ORDER = [
    ("B", "stats", 0), ("B", "normalise", 0), ("A", "turn_x", 0), ("B", "turn_y", 0), ("A", "neighbours", 0),
    ("A", "gate_r", 0), ("B", "products_t", 0), ("B", "products_v", 0), ("B", "relate", 0), ("A", "gate_z", 0),
    ("B", "mix1", 0), ("B", "residual1", 0), ("A", "gate_v", 0), ("B", "stats", 1), ("B", "normalise", 1),
    ("A", "update", 0), ("B", "turn_y", 1), ("A", "turn_h", 0), ("B", "product_q", 0), ("B", "product_k", 0),
    ("B", "product_v", 0), ("A", "neighbours", 1), ("A", "gate_r", 1), ("B", "scores", 0), ("B", "softmax", 0),
    ("A", "gate_z", 1), ("A", "gate_v", 1), ("B", "turn_probs", 0), ("A", "update", 1), ("B", "attend", 0),
    ("B", "divide", 0), ("B", "turn_y", 2), ("A", "turn_h", 1), ("B", "project", 0), ("B", "stats", 2),
    ("A", "neighbours", 2), ("B", "residual2", 0), ("A", "gate_r", 2), ("B", "stats", 3), ("A", "gate_z", 2),
    ("B", "normalise", 3), ("A", "gate_v", 2), ("B", "turn_y", 3), ("B", "products_s", 0),
    ("B", "products_h", 0), ("A", "update", 2), ("B", "logits3", 0), ("B", "softmax3", 0), ("A", "turn_h", 2),
    ("B", "turn_att", 0), ("B", "mix3", 0), ("B", "elu", 0), ("B", "stats", 4), ("B", "normalise", 4),
]


class Signal:

    def __init__(self, sem, per):
        self.s, self.per = sem, per

    def at(self, g, k):
        return g * self.per + k


def gnn_kernel(nc, x, adj, w3, w3_b, u3, u3_b, w4, w4_b, w5, w5_b, u5, u5_b, Wq, Wk, Wv,
               w_qkv, w_proj, b_proj, ln_gamma, ln_beta, W, a, beta, out):
    BATCH, N, D = x.shape
    T = 4
    GT = T * P
    GROUPS = BATCH * N // GT
    H = D // P
    HD = D // HEADS
    R = P // HD
    SCALE = float(HD) ** -0.5
    assert P == 2 * N and H == 2 and R == 4

    x_g = x.rearrange("(g t b) n d -> g (b n) t d", t=T, b=2)
    out_g = out.rearrange("(g t b) n d -> g (b n) t d", t=T, b=2)

    with ExitStack() as ctx:
        def sb(name, shape, dt=F32):
            return ctx.enter_context(nc.sbuf_tensor(name, shape, dt))

        def sig(name, per=0):
            return Signal(ctx.enter_context(nc.semaphore(name)), per)

        psA = ctx.enter_context(nc.psum_tensor("psA", [P, 4, GT], F32))
        psB = ctx.enter_context(nc.psum_tensor("psB", [P, 4, GT], F32))

        w3h, w3l, w4h, w4l, w5h, w5l, u3h, u3l, wvh, wvl, mh, ml, wph, wpl, w3gh, w3gl = (
            sb(n, [P, H, D], F32R) for n in
            ("w3h", "w3l", "w4h", "w4l", "w5h", "w5l", "u3h", "u3l", "wvh", "wvl", "mh", "ml",
             "wph", "wpl", "w3gh", "w3gl"))
        u5t = sb("u5t", [P, H, D])
        qkvh, qkvl = sb("qkvh", [P, H, 3 * D], F32R), sb("qkvl", [P, H, 3 * D], F32R)
        wah, wal = sb("wah", [P, H, 2], F32R), sb("wal", [P, H, 2], F32R)
        wa2h, wa2l = sb("wa2h", [P, H, P], F32R), sb("wa2l", [P, H, P], F32R)
        wa32 = sb("wa32", [P, H, 2])
        a_sb = sb("a_sb", [P, 2, H])
        biases = sb("biases", [P, 5, H])
        bias_z, bias_r, bias_h = (sb(n, [P, H]) for n in ("bias_z", "bias_r", "bias_h"))
        bproj_bc, gamma_bc, beta_bc = (sb(n, [P, D]) for n in ("bproj_bc", "gamma_bc", "beta_bc"))
        ident = sb("ident", [P, P])
        adj2 = sb("adj2", [P, N])
        adj_bd = sb("adj_bd", [P, P])
        adjT_bd = sb("adjT_bd", [P, P])
        mask_add = sb("mask_add", [P, N])
        beta_col = sb("beta_col", [P, 1])
        beta_eye = sb("beta_eye", [P, N])
        minus_half = sb("minus_half", [P, T])
        ones_col = sb("ones_col", [P, 1])

        x_in = sb("x_in", [P, T, D])
        x_res = sb("x_res", [P, T, D])
        h_tok = sb("h_tok", [P, T, D])
        h = sb("h", [P, H, GT])
        hh, hl = sb("hh", [P, H, GT], F32R), sb("hl", [P, H, GT], F32R)
        ah, al = sb("ah", [P, H, GT], F32R), sb("al", [P, H, GT], F32R)
        tr, rh, tz, th = (sb(n, [P, H, GT]) for n in ("tr", "rh", "tz", "th"))
        pre1 = sb("pre1", [P, T, D])

        y1, y2, y3, y4, pre = (sb(n, [P, T, D]) for n in ("y1", "y2", "y3", "y4", "pre"))
        yTh, yTl = sb("yTh", [P, H, GT], F32R), sb("yTl", [P, H, GT], F32R)
        tTh, tTl = sb("tTh", [P, H, GT], F32R), sb("tTl", [P, H, GT], F32R)
        v1 = sb("v1", [P, T, D])
        relw, relsq = sb("relw", [P, T, P]), sb("relsq", [P, T, P])
        norm2, rnorm = sb("norm2", [P, T]), sb("rnorm", [P, T])
        qk = sb("qk", [P, 2, H, GT])
        vbd = sb("vbd", [P, T, 2, R, H, HD + 1])
        probs = sb("probs", [P, R, T * H, N])
        probsT = sb("probsT", [P, R, GT])
        smax = sb("smax", [P, R * T * H])
        rsum = sb("rsum", [P, T, R, H])
        o_tok = sb("o_tok", [P, T, D])
        s_tok = sb("s_tok", [P, T, 2])
        e3 = sb("e3", [P, T, N])
        e3max, e3sum, e3inv = sb("e3max", [P, T]), sb("e3sum", [P, T]), sb("e3inv", [P, T])
        att_bd, attT = sb("att_bd", [P, T, P]), sb("attT", [P, T, P])
        ln_st, ln_mv = sb("ln_st", [P, T, 6]), sb("ln_mv", [P, T, 2])
        ln_ve, ln_rs = sb("ln_ve", [P, T]), sb("ln_rs", [P, T])
        ln_nm, ln_nb = sb("ln_nm", [P, T]), sb("ln_nb", [P, T])
        u3h_sb = sb("u3h_sb", [P, H, GT])

        w3_in = probs[:, :, :, :].rearrange("p r a n -> p (r a n)")[:, 0:4 * D].rearrange(
            "p (c i) -> p c i", c=H)
        w4_in = probs[:, :, :, :].rearrange("p r a n -> p (r a n)")[:, 4 * D:8 * D].rearrange(
            "p (c i) -> p c i", c=H)
        pT_flat = probsT[:, :, :].rearrange("p r n -> p (r n)")
        w5_in = pT_flat[:, 0:4 * D].rearrange("p (c i) -> p c i", c=H)
        u3_in = pT_flat[:, 4 * D:6 * D].rearrange("p (c i) -> p c i", c=H)
        u5_in = pT_flat[:, 6 * D:8 * D].rearrange("p (c i) -> p c i", c=H)
        qk_flat = qk[:, :, :, :].rearrange("p a h n -> p (a h n)")
        Wq_in = qk_flat[:, 0:2 * D].rearrange("p (c i) -> p c i", c=H)
        Wk_in = qk_flat[:, 2 * D:4 * D].rearrange("p (c i) -> p c i", c=H)
        Wv_in = qk_flat[:, 4 * D:6 * D].rearrange("p (c i) -> p c i", c=H)
        W_in = qk_flat[:, 6 * D:8 * D].rearrange("p (c i) -> p c i", c=H)
        WT = v1[:, 0:2, :]
        qkv_in = [y2[:, 0:3, :].rearrange("p t d -> p (t d)"), y3[:, 0:3, :].rearrange("p t d -> p (t d)")]
        wp_in = y1[:, 0:2, :]

        p_load = {n: sig("p_" + n) for n in
                  ("w3", "w4", "w5", "u3", "u5", "wq", "wk", "wv", "qkv", "wp", "W", "a", "adj2",
                   "adjbd", "bias", "rows", "beta")}
        p_ident0, p_ident = sig("p_ident0"), sig("p_ident")
        p_adj0 = sig("p_adj0")
        p_vbd0 = sig("p_vbd0")
        p_fold = sig("p_fold")
        p_turned = sig("p_turned")
        p_hi = sig("p_hi")
        p_lo = sig("p_lo")
        p_wa = sig("p_wa")
        p_wa_sb = sig("p_wa_sb")
        p_small = sig("p_small")
        p_done_act, p_done_dve, p_done_pool = sig("p_done_act"), sig("p_done_dve"), sig("p_done_pool")

        passed_dve, passed_pool = sig("passed_dve"), sig("passed_pool")

        x_loaded = sig("x_loaded", 16)
        x_copied = sig("x_copied", 1)
        xT_ready = sig("xT_ready", H)
        h0_ready = sig("h0_ready", H)
        u_ready, u_copied, zsum_ready = (sig(n, STEPS * H) for n in ("u_ready", "u_copied", "zsum_ready"))
        hh_ready, hl_ready = sig("hh_ready", STEPS * H), sig("hl_ready", STEPS * H)
        aT_ready = sig("aT_ready", STEPS * H)
        ah_ready, al_ready = sig("ah_ready", STEPS * H), sig("al_ready", STEPS * H)
        r_ready, z_ready, v_ready = (sig(n, STEPS * H) for n in ("r_ready", "z_ready", "v_ready"))
        tr_ready, tz_ready, th_ready = (sig(n, STEPS * H) for n in ("tr_ready", "tz_ready", "th_ready"))
        rh_ready = sig("rh_ready", STEPS * H)
        d_ready, zd_ready, hn_ready = (sig(n, STEPS * H) for n in ("d_ready", "zd_ready", "hn_ready"))
        hT_ready = sig("hT_ready", STEPS * 2)
        htok_ready = sig("htok_ready", (STEPS - 1) * 2)
        pre1_ready = sig("pre1_ready", 2)

        ln_stats, ln_aggr = sig("ln_stats", 5 * T), sig("ln_aggr", 5 * T)
        ln_vareps, ln_rstd, ln_shift = sig("ln_vareps", 5 * 2), sig("ln_rstd", 5), sig("ln_shift", 4)
        ln_out = sig("ln_out", 4 * T)
        yT_ready, yTh_ready, yTl_ready = (sig(n, 4 * H) for n in ("yT_ready", "yTh_ready", "yTl_ready"))
        tT_ready, tTh_ready, tTl_ready = (sig(n, H) for n in ("tT_ready", "tTh_ready", "tTl_ready"))
        v1_ready, v1_copied = sig("v1_ready", 2), sig("v1_copied", 2)
        rel_ready, relw_ready, relsq_ready = sig("rel_ready", 1), sig("relw_ready", 1), sig("relsq_ready", 1)
        norm2_ready, norm2_copied, rnorm_ready = sig("norm2_ready", 1), sig("norm2_copied", 1), sig("rnorm_ready", 1)
        mix1_ready, pre2_ready = sig("mix1_ready", 2), sig("pre2_ready", T)
        qk_ready, qk_copied = sig("qk_ready", 4), sig("qk_copied", 4)
        v2_ready, v2_copied = sig("v2_ready", 2), sig("v2_copied", 4)
        score_ready, masked_ready, smax_ready = sig("score_ready", 1), sig("masked_ready", R), sig("smax_ready", R)
        shifted_ready, exp_ready = sig("shifted_ready", R), sig("exp_ready", R)
        probT_ready, probT_copied = sig("probT_ready", R), sig("probT_copied", R)
        heads_ready, rsum_ready, o_ready = sig("heads_ready", 1), sig("rsum_ready", 1), sig("o_ready", T)
        proj_ready, o2_ready = sig("proj_ready", 2), sig("o2_ready", 2)
        y2b_ready, res2_ready = sig("y2b_ready", 1), sig("res2_ready", 2)
        gam_ready, pre3_ready = sig("gam_ready", T), sig("pre3_ready", T)
        h3_ready, h3_copied = sig("h3_ready", 2), sig("h3_copied", 2)
        s_ready, s_copied, e_sum, e_leaky = sig("s_ready", 2), sig("s_copied", 1), sig("e_sum", 2), sig("e_leaky", 1)
        e_mask, e_max, e_shift, e_exp = sig("e_mask", 1), sig("e_max", 1), sig("e_shift", 1), sig("e_exp", 1)
        e_total, e_inv, e_norm, att_ready = sig("e_total", 1), sig("e_inv", 1), sig("e_norm", 1), sig("att_ready", 2)
        attT_ready, attT_copied = sig("attT_ready", 1), sig("attT_copied", 1)
        mix3_ready, elu_exp, elu_neg, elu_ready = sig("mix3_ready", 2), sig("elu_exp", 2), sig("elu_neg", 2), sig("elu_ready", 2)
        pre4_ready = sig("pre4_ready", 2)
        stored = sig("stored", 16)

        def pairA(use):
            return psA[:, 2 * (use % 2):2 * (use % 2) + 2, :]

        def tok(pair):
            return pair.rearrange("p k (u d) -> p (k u) d", u=2)

        pair0, pair1 = psB[:, 0:2, :], psB[:, 2:4, :]
        turn_pair = (pair0, pair1, pair0, pair0)

        def run(eng_chunks, gA, gB):
            for stream, name, step in ORDER:
                if stream == "A" and gA is not None and name in eng_chunks:
                    eng_chunks[name](gA, step)
                if stream == "B" and gB is not None and name in eng_chunks:
                    eng_chunks[name](gB, step)

        def whole_program(eng, chunks):
            run(chunks, 0, None)
            run(chunks, 1, 0)
            with eng.Fori(1, GROUPS - 1) as g:
                run(chunks, g + 1, g)
            run(chunks, None, GROUPS - 1)

        def first(g):
            return isinstance(g, int) and g == 0

        block = ctx.enter_context(nc.Block())

        @block.sync
        def _(sp):
            sp.dma_start(adj2[0:N, :], adj).then_inc(p_load["adj2"].s, 16)
            sp.dma_start(adj2[N:P, :], adj).then_inc(p_load["adj2"].s, 16)
            for dst, src, n in ((u3_in, u3, "u3"), (w4_in, w4, "w4"), (w3_in, w3, "w3"), (w5_in, w5, "w5"),
                                (u5_in, u5, "u5"), (Wv_in, Wv, "wv"), (Wq_in, Wq, "wq"), (Wk_in, Wk, "wk"),
                                (W_in, W, "W"), (wp_in, w_proj, "wp")):
                sp.dma_start(dst, src.rearrange("(c p) i -> p c i", p=P)).then_inc(p_load[n].s, 16)
            for c in range(H):
                sp.dma_start(qkv_in[c], w_qkv[c * P:(c + 1) * P, :]).then_inc(p_load["qkv"].s, 16)
            sp.wait_ge(p_adj0.s, 1)
            for b in range(2):
                sp.dma_start(adj_bd[b * N:(b + 1) * N, b * N:(b + 1) * N], adj).then_inc(p_load["adjbd"].s, 16)

            def turn_x(g, step):
                if not first(g):
                    sp.wait_ge(x_copied.s, x_copied.at(g - 1, 1))
                    sp.wait_ge(aT_ready.s, aT_ready.at(g - 1, H))
                sp.dma_start(x_in[:, :, :], x_g[bass.ds(g, 1)].rearrange("a p t d -> (a p) t d")
                             ).then_inc(x_loaded.s, 16)

            def store(g):
                sp.wait_ge(ln_out.s, ln_out.at(g, 4 * T))
                sp.dma_start(out_g[bass.ds(g, 1)].rearrange("a p t d -> (a p) t d"), y4[:, :, :]
                             ).then_inc(stored.s, 16)

            def run_ahead(gA, gB):
                if gA is not None:
                    turn_x(gA, 0)
                if gB is not None:
                    store(gB)

            run_ahead(0, None)
            run_ahead(1, None)
            with sp.Fori(0, GROUPS - 2) as g:
                run_ahead(g + 2, g)
            run_ahead(None, GROUPS - 2)
            run_ahead(None, GROUPS - 1)
            sp.wait_ge(stored.s, stored.at(GROUPS - 1, 16))

        @block.gpsimd
        def _(pool):
            nc.gpsimd.memset(ident[:, :], 0.0).then_inc(p_ident0.s, 1)
            nc.gpsimd.memset(adj_bd[:, :], 0.0).then_inc(p_adj0.s, 1)
            pool.wait_ge(p_ident0.s, 1)
            nc.gpsimd.affine_select(out=ident[:, :], in_=ident[:, :], compare_op=ALU.not_equal, fill=1.0,
                                    base=0, pattern=[[-1, P]], channel_multiplier=1).then_inc(p_ident.s, 1)
            for t, src in enumerate((w3_b, w4_b, w5_b, u3_b, u5_b)):
                for c in range(H):
                    pool.dma_start(biases[:, t, c:c + 1], src[c * P:(c + 1) * P].unsqueeze(1)
                                   ).then_inc(p_load["bias"].s, 16)
            for k in range(2 * H):
                pool.dma_start(a_sb[:, k // H, k % H:k % H + 1], a[k * P:(k + 1) * P, :]).then_inc(p_load["a"].s, 16)
            for dst, src in ((bproj_bc, b_proj), (gamma_bc, ln_gamma), (beta_bc, ln_beta)):
                pool.dma_start(dst[:, :], src.rearrange("(a d) -> a d", a=1).to_broadcast([P, D])
                               ).then_inc(p_load["rows"].s, 16)
            pool.dma_start(beta_col[:, :], beta.rearrange("(a d) -> a d", a=1).to_broadcast([P, 1])
                           ).then_inc(p_load["beta"].s, 16)
            nc.gpsimd.memset(att_bd[:, :, :], 0.0)
            nc.gpsimd.memset(minus_half[:, :], -0.5)
            nc.gpsimd.memset(ones_col[:, :], 1.0)
            nc.gpsimd.memset(vbd[:, :, :, :, :, :], 0.0).then_inc(p_vbd0.s, 1)
            pool.wait_ge(p_vbd0.s, 1)
            for f in range(H):
                last = nc.gpsimd.memset(
                    vbd[f * N:(f + 1) * N, :, :, :, f, HD:HD + 1].rearrange("p t b r o -> p (t b) r o"), 1.0)
            last.then_inc(p_done_pool.s, 1)
            pool.wait_ge(p_done_pool.s, 1)
            pool.wait_ge(p_load["rows"].s, 48)

            def turn_x(g, step):
                if not first(g):
                    pool.wait_ge(pre1_ready.s, pre1_ready.at(g - 1, 2))
                pool.wait_ge(x_loaded.s, x_loaded.at(g, 16))
                pool.sem_inc(passed_pool.s, 1)
                nc.gpsimd.tensor_copy(x_res[:, :, :], x_in[:, :, :]).then_inc(x_copied.s, 1)

            def stats(g, n):
                pool.wait_ge(ln_vareps.s, ln_vareps.at(g, 2 * n + 2))
                if n > 0 or not first(g):
                    pool.wait_ge(ln_out.s, ln_out.at(g, (n - (n > 2)) * T))
                nc.gpsimd.tensor_tensor(ln_rs[:, :], ln_ve[:, :], minus_half[:, :], ALU.pow).then_inc(ln_rstd.s, 1)
                if n != 2:
                    pool.wait_ge(ln_rstd.s, ln_rstd.at(g, n + 1))
                    nc.gpsimd.tensor_tensor(ln_nb[:, :], ln_nm[:, :], ln_rs[:, :], ALU.mult).then_inc(ln_shift.s, 1)

            def mix1(g, n):
                pool.wait_ge(norm2_copied.s, norm2_copied.at(g, 1))
                nc.gpsimd.tensor_tensor(rnorm[:, :], norm2[:, :], minus_half[:, :], ALU.pow).then_inc(rnorm_ready.s, 1)

            def product_q(g, n):
                pool.wait_ge(ln_out.s, ln_out.at(g, 2 * T))
                nc.gpsimd.tensor_tensor(y1[:, :, :], y2[:, :, :], beta_bc[:, :].unsqueeze(1).to_broadcast([P, T, D]),
                                        ALU.add).then_inc(y2b_ready.s, 1)

            def project(g, n):
                for k in range(2):
                    rows = slice(2 * k, 2 * k + 2)
                    pool.wait_ge(o2_ready.s, o2_ready.at(g, k + 1))
                    if k == 0:
                        pool.wait_ge(y2b_ready.s, y2b_ready.at(g, 1))
                    nc.gpsimd.tensor_tensor(y1[:, rows, :], y1[:, rows, :], pre[:, rows, :],
                                            ALU.add).then_inc(res2_ready.s, 1)

            def elu(g, n):
                for k in range(2):
                    pool.wait_ge(elu_ready.s, elu_ready.at(g, k + 1))
                    nc.gpsimd.tensor_tensor(pre[:, 2 * k:2 * k + 2, :], pre[:, 2 * k:2 * k + 2, :],
                                            y3[:, 2 * k:2 * k + 2, :], ALU.add).then_inc(pre4_ready.s, 1)

            whole_program(pool, dict(turn_x=turn_x, stats=stats, mix1=mix1, product_q=product_q,
                                     project=project, elu=elu))

        @block.tensor
        def _(pe):
            def turn_weight(bank, src):
                for i in range(H):
                    for o in range(H):
                        last = nc.tensor.transpose(bank[:, i * D + o * P:i * D + (o + 1) * P],
                                                   src[:, o, i * P:(i + 1) * P], ident[:, :])
                last.then_inc(p_turned.s, 1)

            pe.wait_ge(p_ident.s, 1)
            pe.wait_ge(p_load["adjbd"].s, 32)
            nc.tensor.transpose(psA[:, 0, 0:P], adj_bd[:, :], ident[:, :]).then_inc(p_turned.s, 1)
            pe.wait_ge(p_load["u3"].s, 16)
            turn_weight(psA[:, 1, :], u3_in)
            for k, (bank, src) in enumerate(((psA[:, 2, :], w4_in), (psA[:, 3, :], w3_in), (psB[:, 0, :], w5_in))):
                pe.wait_ge(p_fold.s, k + 1)
                turn_weight(bank, src)
            pe.wait_ge(p_load["u5"].s, 16)
            turn_weight(psB[:, 1, :], u5_in)
            pe.wait_ge(p_load["wv"].s, 16)
            turn_weight(psB[:, 2, :], Wv_in)
            pe.wait_ge(p_load["wq"].s, 16)
            pe.wait_ge(p_load["wk"].s, 16)
            for i in range(H):
                for c in range(H):
                    last = nc.tensor.matmul(psB[:, 3, i * D:(i + 1) * D], Wq_in[:, c, i * P:(i + 1) * P],
                                            Wk_in[:, c, :], start=(c == 0), stop=(c == H - 1))
            last.then_inc(p_turned.s, 1)
            pe.wait_ge(p_load["W"].s, 16)
            pe.wait_ge(p_hi.s, 1)
            turn_weight(psA[:, 0, :], W_in)
            pe.wait_ge(p_hi.s, 9)
            pe.wait_ge(p_load["a"].s, 32 * H)
            pe.wait_ge(p_lo.s, 1)
            for i in range(H):
                for c in range(H):
                    last = nc.tensor.matmul(psA[:, 1, 2 * i:2 * i + 2], WT[:, c, i * P:(i + 1) * P],
                                            a_sb[:, :, c], start=(c == 0), stop=(c == H - 1))
            last.then_inc(p_wa.s, 1)
            pe.wait_ge(p_done_act.s, 1)
            pe.wait_ge(p_done_dve.s, 1)
            pe.wait_ge(p_done_pool.s, 1)

            def parts3(out, wh, wl, xh, xl, cols, start, stop, reopened=False):
                n = 0
                for c in range(H):
                    for w_, x_ in ((wh, xh), (wh, xl), (wl, xh)):
                        last = nc.tensor.matmul(out, w_[:, c, cols], x_[:, c, :], start=start and n == 0,
                                                stop=stop and n == 3 * H - 1, skip_group_check=reopened)
                        n += 1
                return last

            def token3(out, t, wh, wl, cols):
                rows = slice(t * P, (t + 1) * P)
                n = 0
                for c in range(H):
                    for x_, w_ in ((yTh, wh), (yTh, wl), (yTl, wh)):
                        last = nc.tensor.matmul(out, x_[:, c, rows], w_[:, c, cols], start=n == 0,
                                                stop=n == 3 * H - 1)
                        n += 1
                return last

            def turn_x(g, step):
                pe.wait_ge(x_loaded.s, x_loaded.at(g, 16))
                for f in range(H):
                    for t in range(T):
                        last = nc.tensor.transpose(pairA(0)[:, f, t * P:(t + 1) * P],
                                                   x_in[:, t, f * P:(f + 1) * P], ident[:, :])
                    last.then_inc(xT_ready.s, 1)

            def neighbours(g, step):
                src = x_in if step == 0 else h_tok
                if step == 0 and not first(g):
                    pe.wait_ge(pre1_ready.s, pre1_ready.at(g - 1, 2))
                if step > 0:
                    pe.wait_ge(htok_ready.s, htok_ready.at(g, 2 * step))
                for f in range(H):
                    for t in range(T):
                        last = nc.tensor.matmul(pairA(1 + 5 * step)[:, f, t * P:(t + 1) * P],
                                                src[:, t, f * P:(f + 1) * P], adjT_bd[:, :],
                                                start=True, stop=True)
                    last.then_inc(aT_ready.s, 1)

            def gate_r(g, step):
                k = H * step
                pe.wait_ge(hh_ready.s, hh_ready.at(g, k + H))
                pe.wait_ge(hl_ready.s, hl_ready.at(g, k + H))
                for f in range(H):
                    parts3(pairA(2 + 5 * step)[:, f, :], u3h, u3l, hh, hl, slice(f * P, (f + 1) * P), True, True
                           ).then_inc(u_ready.s, 1)
                pe.wait_ge(al_ready.s, al_ready.at(g, k + H))
                for f in range(H):
                    pe.wait_ge(u_copied.s, u_copied.at(g, k + f + 1))
                    parts3(pairA(2 + 5 * step)[:, f, :], w4h, w4l, ah, al, slice(f * P, (f + 1) * P), False, True,
                           reopened=True).then_inc(r_ready.s, 1)

            def gate_z(g, step):
                for f in range(H):
                    parts3(pairA(3 + 5 * step)[:, f, :], w3h, w3l, ah, al, slice(f * P, (f + 1) * P), True, True
                           ).then_inc(z_ready.s, 1)

            def gate_v(g, step):
                k = H * step
                for f in range(H):
                    cols = slice(f * P, (f + 1) * P)
                    dst = pairA(4 + 5 * step)[:, f, :]
                    pe.wait_ge(tr_ready.s, tr_ready.at(g, k + f + 1))
                    parts3(dst, w5h, w5l, ah, al, cols, True, False)
                for f in range(H):
                    cols = slice(f * P, (f + 1) * P)
                    dst = pairA(4 + 5 * step)[:, f, :]
                    for c in range(H):
                        if f == 0:
                            pe.wait_ge(rh_ready.s, rh_ready.at(g, k + c + 1))
                        last = nc.tensor.matmul(dst, u5t[:, c, cols], rh[:, c, :], start=False, stop=(c == H - 1))
                    last.then_inc(v_ready.s, 1)

            def turn_h(g, step):
                dst = tok(pairA(5 + 5 * step))
                for f in range(H):
                    pe.wait_ge(hn_ready.s, hn_ready.at(g, H * step + f + 1))
                    for t in range(T):
                        last = nc.tensor.transpose(dst[:, t, f * P:(f + 1) * P], h[:, f, t * P:(t + 1) * P],
                                                   ident[:, :])
                        if f == H - 1 and t % 2 == 1:
                            last.then_inc(hT_ready.s, 1)

            def turn_y(g, n):
                src, ready, base = ((y1, ln_out, 0), (y2, ln_out, T), (o_tok, o_ready, 0), (y3, ln_out, 2 * T))[n]
                if n == 0 and not first(g):
                    pe.wait_ge(attT_copied.s, attT_copied.at(g - 1, 1))
                if n == 1:
                    pe.wait_ge(norm2_copied.s, norm2_copied.at(g, 1))
                for f in range(H):
                    for t in range(T):
                        if f == 0:
                            pe.wait_ge(ready.s, ready.at(g, base + t + 1))
                        last = nc.tensor.transpose(turn_pair[n][:, f, t * P:(t + 1) * P],
                                                   src[:, t, f * P:(f + 1) * P], ident[:, :])
                    last.then_inc(yT_ready.s, 1)

            def split_done(g, n):
                pe.wait_ge(yTh_ready.s, yTh_ready.at(g, (n + 1) * H))
                pe.wait_ge(yTl_ready.s, yTl_ready.at(g, (n + 1) * H))

            def products_t(g, n):
                split_done(g, 0)
                if not first(g):
                    pe.wait_ge(elu_ready.s, elu_ready.at(g - 1, 2))
                for f in range(H):
                    parts3(pair1[:, f, :], mh, ml, yTh, yTl, slice(f * P, (f + 1) * P), True, True
                           ).then_inc(tT_ready.s, 1)

            def products_v(g, n):
                for t in range(T):
                    last = token3(tok(pair0)[:, t, :], t, wvh, wvl, slice(0, D))
                    if t % 2 == 1:
                        last.then_inc(v1_ready.s, 1)

            def relate(g, n):
                pe.wait_ge(tTh_ready.s, tTh_ready.at(g, H))
                pe.wait_ge(tTl_ready.s, tTl_ready.at(g, H))
                for t in range(T):
                    cols = slice(t * P, (t + 1) * P)
                    n = 0
                    for c in range(H):
                        for y_, t_ in ((yTh, tTh), (yTh, tTl), (yTl, tTh)):
                            last = nc.tensor.matmul(pair1[:, 0, cols], y_[:, c, cols], t_[:, c, cols],
                                                    start=n == 0, stop=n == 3 * H - 1)
                            n += 1
                last.then_inc(rel_ready.s, 1)

            def mix1(g, n):
                pe.wait_ge(v1_copied.s, v1_copied.at(g, 2))
                pe.wait_ge(relw_ready.s, relw_ready.at(g, 1))
                for t in range(T):
                    last = nc.tensor.matmul(tok(pair0)[:, t, :], relw[:, t, :], v1[:, t, :], start=True, stop=True)
                    if t == 0:
                        pe.wait_ge(relsq_ready.s, relsq_ready.at(g, 1))
                        for q in range(T):
                            sums = nc.tensor.matmul(pair1[:, 1, q:q + 1], relsq[:, q, :], ones_col[:, :],
                                                    start=True, stop=True)
                        sums.then_inc(norm2_ready.s, 1)
                    if t % 2 == 1:
                        last.then_inc(mix1_ready.s, 1)

            def product_q(g, n):
                split_done(g, 1)
                for f in range(H):
                    parts3(pair0[:, f, :], qkvh, qkvl, yTh, yTl, slice(f * P, (f + 1) * P), True, True
                           ).then_inc(qk_ready.s, 1)

            def product_k(g, n):
                for f in range(H):
                    parts3(pair1[:, f, :], qkvh, qkvl, yTh, yTl, slice(D + f * P, D + (f + 1) * P), True, True
                           ).then_inc(qk_ready.s, 1)

            def product_v(g, n):
                pe.wait_ge(qk_copied.s, qk_copied.at(g, 2))
                for t in range(T):
                    last = token3(tok(pair0)[:, t, :], t, qkvh, qkvl, slice(2 * D, 3 * D))
                    if t % 2 == 1:
                        last.then_inc(v2_ready.s, 1)

            def scores(g, n):
                pe.wait_ge(qk_copied.s, qk_copied.at(g, 4))
                pe.wait_ge(v2_copied.s, v2_copied.at(g, 4))
                for t in range(T):
                    for f in range(H):
                        for b in range(2):
                            cols = slice(t * P + b * N, t * P + (b + 1) * N)
                            for r in range(R):
                                rows = slice(r * HD, (r + 1) * HD)
                                last = nc.tensor.matmul(
                                    psB[b * N:(b + 1) * N, r, (t * H + f) * N:(t * H + f + 1) * N],
                                    qk[rows, 0, f, cols], qk[rows, 1, f, cols], start=True, stop=True)
                last.then_inc(score_ready.s, 1)

            def turn_probs(g, n):
                for r in range(R):
                    pe.wait_ge(exp_ready.s, exp_ready.at(g, r + 1))
                    for t in range(T):
                        last = nc.tensor.transpose(
                            psB[:, r, t * P:(t + 1) * P],
                            probs[:, r, t * H:(t + 1) * H, :].rearrange("p f n -> p (f n)"), ident[:, :])
                    last.then_inc(probT_ready.s, 1)

            def attend(g, n):
                pe.wait_ge(probT_copied.s, probT_copied.at(g, R))
                for t in range(T):
                    for b in range(2):
                        for r in range(R):
                            last = nc.tensor.matmul(
                                psB[b * N:(b + 1) * N, t, r * H * (HD + 1):(r + 1) * H * (HD + 1)],
                                probsT[:, r, t * P + b * N:t * P + (b + 1) * N],
                                vbd[:, t, b, r, :, :].rearrange("p f d -> p (f d)"), start=True, stop=True)
                last.then_inc(heads_ready.s, 1)

            def project(g, n):
                split_done(g, 2)
                for t in range(T):
                    last = token3(tok(pair1)[:, t, :], t, wph, wpl, slice(0, D))
                    if t % 2 == 1:
                        last.then_inc(proj_ready.s, 1)

            def products_s(g, n):
                split_done(g, 3)
                for t in range(T):
                    last = token3(pair0[:, 0, 2 * t:2 * t + 2], t, wah, wal, slice(0, 2))
                last.then_inc(s_ready.s, 1)
                parts3(pair0[:, 1, :], wa2h, wa2l, yTh, yTl, slice(0, P), True, True).then_inc(s_ready.s, 1)

            def products_h(g, n):
                for t in range(T):
                    last = token3(tok(pair1)[:, t, :], t, w3gh, w3gl, slice(0, D))
                    if t % 2 == 1:
                        last.then_inc(h3_ready.s, 1)

            def turn_att(g, n):
                pe.wait_ge(att_ready.s, att_ready.at(g, 2))
                for t in range(T):
                    last = nc.tensor.transpose(pair0[:, 0, t * P:(t + 1) * P], att_bd[:, t, :], ident[:, :])
                last.then_inc(attT_ready.s, 1)

            def mix3(g, n):
                pe.wait_ge(h3_copied.s, h3_copied.at(g, 2))
                pe.wait_ge(attT_copied.s, attT_copied.at(g, 1))
                for t in range(T):
                    last = nc.tensor.matmul(tok(pair1)[:, t, :], attT[:, t, :], v1[:, t, :], start=True, stop=True)
                    if t % 2 == 1:
                        last.then_inc(mix3_ready.s, 1)

            whole_program(pe, dict(
                turn_x=turn_x, neighbours=neighbours, gate_r=gate_r, gate_z=gate_z, gate_v=gate_v, turn_h=turn_h,
                turn_y=turn_y, products_t=products_t, products_v=products_v, relate=relate, mix1=mix1,
                product_q=product_q, product_k=product_k, product_v=product_v, scores=scores,
                turn_probs=turn_probs, attend=attend, project=project, products_s=products_s,
                products_h=products_h, turn_att=turn_att, mix3=mix3))

        @block.scalar
        def _(act):
            whole = lambda w_: w_[:, :, :].rearrange("p c o -> p (c o)")
            act.wait_ge(p_turned.s, 1)
            nc.scalar.copy(adjT_bd[:, :], psA[:, 0, 0:P]).then_inc(p_hi.s, 1)
            for k, (dst, bank) in enumerate(((u3h, psA[:, 1, :]), (w4h, psA[:, 2, :]), (w3h, psA[:, 3, :]),
                                             (w5h, psB[:, 0, :]))):
                act.wait_ge(p_turned.s, k + 2)
                nc.scalar.copy(whole(dst), bank).then_inc(p_hi.s, 1)
            act.wait_ge(p_turned.s, 6)
            nc.scalar.mul(whole(u5t), psB[:, 1, :], 0.5).then_inc(p_hi.s, 1)
            for k, (dst, bank) in enumerate(((wvh, psB[:, 2, :]), (mh, psB[:, 3, :]))):
                act.wait_ge(p_turned.s, k + 7)
                nc.scalar.copy(whole(dst), bank).then_inc(p_hi.s, 1)
            act.wait_ge(p_turned.s, 9)
            nc.scalar.copy(WT.rearrange("p c o -> p (c o)"), psA[:, 0, :]).then_inc(p_hi.s, 1)
            act.wait_ge(p_load["qkv"].s, 32)
            for c in range(H):
                nc.scalar.copy(qkvh[:, c, :], qkv_in[c]).then_inc(p_hi.s, 1)
            act.wait_ge(p_load["wp"].s, 16)
            nc.scalar.copy(wph[:, :, :], wp_in).then_inc(p_hi.s, 1)
            act.wait_ge(p_load["W"].s, 16)
            nc.scalar.copy(w3gh[:, :, :], W_in).then_inc(p_hi.s, 1)
            act.wait_ge(p_wa.s, 1)
            nc.scalar.copy(wa32[:, :, :].rearrange("p c w -> p (c w)"), psA[:, 1, 0:2 * H]).then_inc(p_wa_sb.s, 1)
            act.wait_ge(p_wa_sb.s, 1)
            nc.scalar.copy(wah[:, :, :], wa32[:, :, :]).then_inc(p_hi.s, 1)
            for c in range(H):
                last = nc.scalar.copy(wa2h[:, c, :], wa32[:, c, 1:2].to_broadcast([P, P]))
                last.then_inc(p_hi.s, 1)
            act.wait_ge(p_hi.s, 16)
            act.wait_ge(p_small.s, 5)
            act.sem_inc(p_done_act.s, 1)

            def turn_x(g, step):
                for f in range(H):
                    act.wait_ge(xT_ready.s, xT_ready.at(g, f + 1))
                    nc.scalar.copy(h[:, f, :], pairA(0)[:, f, :]).then_inc(h0_ready.s, 1)
                split_h(g, 0)

            def split_h(g, step):
                for f in range(H):
                    if step == 0:
                        act.wait_ge(h0_ready.s, h0_ready.at(g, f + 1))
                    else:
                        act.wait_ge(hn_ready.s, hn_ready.at(g, (step - 1) * H + f + 1))
                    nc.scalar.copy(hh[:, f, :], h[:, f, :]).then_inc(hh_ready.s, 1)

            def neighbours(g, step):
                for f in range(H):
                    act.wait_ge(aT_ready.s, aT_ready.at(g, step * H + f + 1))
                    nc.scalar.copy(ah[:, f, :], pairA(1 + 5 * step)[:, f, :]).then_inc(ah_ready.s, 1)

            def gate_r(g, step):
                for f in range(H):
                    act.wait_ge(u_ready.s, u_ready.at(g, step * H + f + 1))
                    nc.scalar.copy(u3h_sb[:, f, :], pairA(2 + 5 * step)[:, f, :]).then_inc(u_copied.s, 1)
                for f in range(H):
                    act.wait_ge(r_ready.s, r_ready.at(g, step * H + f + 1))
                    nc.scalar.activation(tr[:, f, :], pairA(2 + 5 * step)[:, f, :], ACT.Tanh,
                                         bias=bias_r[:, f:f + 1], scale=0.5).then_inc(tr_ready.s, 1)

            def gate_z(g, step):
                for f in range(H):
                    act.wait_ge(zsum_ready.s, zsum_ready.at(g, step * H + f + 1))
                    nc.scalar.activation(tz[:, f, :], tz[:, f, :], ACT.Tanh, bias=bias_z[:, f:f + 1], scale=0.5
                                         ).then_inc(tz_ready.s, 1)

            def gate_v(g, step):
                for f in range(H):
                    act.wait_ge(v_ready.s, v_ready.at(g, step * H + f + 1))
                    nc.scalar.activation(th[:, f, :], pairA(4 + 5 * step)[:, f, :], ACT.Tanh,
                                         bias=bias_h[:, f:f + 1]).then_inc(th_ready.s, 1)

            def update(g, step):
                if step < STEPS - 1:
                    split_h(g, step + 1)

            def turn_h(g, step):
                if step == STEPS - 1:
                    return
                dst = tok(pairA(5 + 5 * step))
                for k in range(2):
                    act.wait_ge(hT_ready.s, hT_ready.at(g, 2 * step + k + 1))
                    nc.scalar.copy(h_tok[:, 2 * k:2 * k + 2, :], dst[:, 2 * k:2 * k + 2, :]).then_inc(htok_ready.s, 1)

            def normalise(g, n):
                src, dst = {0: (pre1, y1), 1: (pre, y2), 3: (pre, y3), 4: (pre, y4)}[n]
                if n == 4 and not first(g):
                    act.wait_ge(stored.s, stored.at(g - 1, 16))
                act.wait_ge(ln_shift.s, ln_shift.at(g, n + 1 - (n > 2)))
                for t in range(T):
                    nc.scalar.activation(dst[:, t, :], src[:, t, :], ACT.Identity, bias=ln_nb[:, t:t + 1],
                                         scale=ln_rs[:, t:t + 1]).then_inc(ln_out.s, 1)

            def turn_y(g, n):
                for f in range(H):
                    act.wait_ge(yT_ready.s, yT_ready.at(g, n * H + f + 1))
                    nc.scalar.copy(yTh[:, f, :], turn_pair[n][:, f, :]).then_inc(yTh_ready.s, 1)

            def products_t(g, n):
                for f in range(H):
                    act.wait_ge(tT_ready.s, tT_ready.at(g, f + 1))
                    nc.scalar.copy(tTh[:, f, :], pair1[:, f, :]).then_inc(tTh_ready.s, 1)

            def products_v(g, n):
                for k in range(2):
                    act.wait_ge(v1_ready.s, v1_ready.at(g, k + 1))
                    nc.scalar.copy(v1[:, 2 * k:2 * k + 2, :], tok(pair0)[:, 2 * k:2 * k + 2, :]).then_inc(v1_copied.s, 1)

            def relate(g, n):
                act.wait_ge(relw_ready.s, relw_ready.at(g, 1))
                nc.scalar.activation(relsq[:, :, :], relw[:, :, :], ACT.Square).then_inc(relsq_ready.s, 1)

            def product_q(g, n, i=0, pair=pair0):
                for f in range(H):
                    act.wait_ge(qk_ready.s, qk_ready.at(g, i * H + f + 1))
                    nc.scalar.copy(qk[:, i, f, :], pair[:, f, :]).then_inc(qk_copied.s, 1)

            def product_k(g, n):
                product_q(g, n, 1, pair1)

            def product_v(g, n):
                for b in range(2):
                    for f in range(H):
                        act.wait_ge(v2_ready.s, v2_ready.at(g, 2))
                        src = tok(pair0)[b * N:(b + 1) * N, :, f * P:(f + 1) * P].rearrange(
                            "p t (r d) -> p t r d", r=R)
                        nc.scalar.copy(vbd[f * N:(f + 1) * N, :, b, :, f, 0:HD], src).then_inc(v2_copied.s, 1)

            def softmax(g, n):
                for r in range(R):
                    act.wait_ge(shifted_ready.s, shifted_ready.at(g, r + 1))
                    nc.scalar.activation(probs[:, r, :, :], probs[:, r, :, :], ACT.Exp, scale=SCALE
                                         ).then_inc(exp_ready.s, 1)

            def turn_probs(g, n):
                for r in range(R):
                    act.wait_ge(probT_ready.s, probT_ready.at(g, r + 1))
                    nc.scalar.copy(probsT[:, r, :], psB[:, r, :]).then_inc(probT_copied.s, 1)

            def products_h(g, n):
                for k in range(2):
                    act.wait_ge(h3_ready.s, h3_ready.at(g, k + 1))
                    nc.scalar.copy(v1[:, 2 * k:2 * k + 2, :], tok(pair1)[:, 2 * k:2 * k + 2, :]).then_inc(h3_copied.s, 1)

            def softmax3(g, n):
                act.wait_ge(e_shift.s, e_shift.at(g, 1))
                nc.scalar.activation(e3[:, :, :], e3[:, :, :], ACT.Exp).then_inc(e_exp.s, 1)

            def turn_att(g, n):
                act.wait_ge(attT_ready.s, attT_ready.at(g, 1))
                nc.scalar.copy(attT[:, :, :].rearrange("p t n -> p (t n)"), pair0[:, 0, :]).then_inc(attT_copied.s, 1)

            def elu(g, n):
                for k in range(2):
                    act.wait_ge(mix3_ready.s, mix3_ready.at(g, k + 1))
                    nc.scalar.activation(o_tok[:, 2 * k:2 * k + 2, :], tok(pair1)[:, 2 * k:2 * k + 2, :], ACT.Exp
                                         ).then_inc(elu_exp.s, 1)

            whole_program(act, dict(
                turn_x=turn_x, neighbours=neighbours, gate_r=gate_r, gate_z=gate_z, gate_v=gate_v, update=update,
                turn_h=turn_h, normalise=normalise, turn_y=turn_y, products_t=products_t, products_v=products_v,
                relate=relate, product_q=product_q, product_k=product_k, product_v=product_v, softmax=softmax,
                turn_probs=turn_probs, products_h=products_h, softmax3=softmax3, turn_att=turn_att, elu=elu))

        @block.vector
        def _(dve):
            f32 = lambda ap: ap.bitcast(F32)
            TT = nc.vector.tensor_tensor
            whole = lambda w_: w_[:, :, :].rearrange("p c o -> p (c o)")
            for w_, n in ((w4_in, "w4"), (w3_in, "w3"), (w5_in, "w5")):
                dve.wait_ge(p_load[n].s, 16)
                TT(w_[:, :, 0:D], w_[:, :, 0:D], w_[:, :, D:2 * D], ALU.add).then_inc(p_fold.s, 1)
            for k, (hi, lo, src) in enumerate(((u3h, u3l, psA[:, 1, :]), (w4h, w4l, psA[:, 2, :]),
                                               (w3h, w3l, psA[:, 3, :]), (w5h, w5l, psB[:, 0, :]))):
                dve.wait_ge(p_hi.s, k + 2)
                TT(whole(lo), src, f32(whole(hi)), ALU.subtract).then_inc(p_lo.s, 1)
            for k, (hi, lo, src) in enumerate(((wvh, wvl, psB[:, 2, :]), (mh, ml, psB[:, 3, :]))):
                dve.wait_ge(p_hi.s, k + 7)
                TT(whole(lo), src, f32(whole(hi)), ALU.subtract).then_inc(p_lo.s, 1)
            for c in range(H):
                dve.wait_ge(p_hi.s, 10 + c)
                TT(qkvl[:, c, :], qkv_in[c], f32(qkvh[:, c, :]), ALU.subtract).then_inc(p_lo.s, 1)
            dve.wait_ge(p_hi.s, 12)
            TT(wpl[:, :, :], wp_in, f32(wph[:, :, :]), ALU.subtract).then_inc(p_lo.s, 1)
            dve.wait_ge(p_hi.s, 13)
            TT(w3gl[:, :, :], W_in, f32(w3gh[:, :, :]), ALU.subtract).then_inc(p_lo.s, 1)
            dve.wait_ge(p_load["adj2"].s, 32)
            nc.vector.tensor_scalar(mask_add[:, :], adj2[:, :], 0.0, MASKED, ALU.is_equal, ALU.mult).then_inc(p_small.s, 1)
            dve.wait_ge(p_load["beta"].s, 16)
            dve.wait_ge(p_ident.s, 1)
            for b in range(2):
                rows = slice(b * N, (b + 1) * N)
                nc.vector.tensor_scalar(beta_eye[rows, :], ident[rows, rows], beta_col[rows, 0:1], None, ALU.mult
                                        ).then_inc(p_small.s, 1)
            dve.wait_ge(p_load["bias"].s, 80 * H)
            TT(bias_z[:, :], biases[:, 0, :], biases[:, 3, :], ALU.add).then_inc(p_small.s, 1)
            TT(bias_r[:, :], biases[:, 1, :], biases[:, 3, :], ALU.add).then_inc(p_small.s, 1)
            TT(bias_h[:, :], biases[:, 2, :], biases[:, 4, :], ALU.add).then_inc(p_small.s, 1)
            dve.wait_ge(p_small.s, 6)
            nc.vector.tensor_scalar(bias_z[:, :], bias_z[:, :], 0.5, None, ALU.mult).then_inc(p_small.s, 1)
            nc.vector.tensor_scalar(bias_r[:, :], bias_r[:, :], 0.5, None, ALU.mult).then_inc(p_small.s, 1)
            dve.wait_ge(p_hi.s, 14)
            TT(wal[:, :, :], wa32[:, :, :], f32(wah[:, :, :]), ALU.subtract).then_inc(p_lo.s, 1)
            for c in range(H):
                dve.wait_ge(p_hi.s, 15 + c)
                TT(wa2l[:, c, :], wa32[:, c, 1:2].to_broadcast([P, P]), f32(wa2h[:, c, :]), ALU.subtract
                   ).then_inc(p_lo.s, 1)
            dve.wait_ge(p_load["rows"].s, 48)
            dve.wait_ge(p_lo.s, 13)
            dve.wait_ge(p_small.s, 8)
            dve.sem_inc(p_done_dve.s, 1)

            def split_h(g, step):
                for f in range(H):
                    dve.wait_ge(hh_ready.s, hh_ready.at(g, step * H + f + 1))
                    TT(hl[:, f, :], h[:, f, :], f32(hh[:, f, :]), ALU.subtract).then_inc(hl_ready.s, 1)

            def turn_x(g, step):
                split_h(g, 0)

            def neighbours(g, step):
                for f in range(H):
                    dve.wait_ge(ah_ready.s, ah_ready.at(g, step * H + f + 1))
                    TT(al[:, f, :], pairA(1 + 5 * step)[:, f, :], f32(ah[:, f, :]), ALU.subtract).then_inc(al_ready.s, 1)

            def gate_r(g, step):
                for f in range(H):
                    dve.wait_ge(tr_ready.s, tr_ready.at(g, step * H + f + 1))
                    nc.vector.scalar_tensor_tensor(out=rh[:, f, :], in0=tr[:, f, :], scalar=1.0, in1=h[:, f, :],
                                                   op0=ALU.add, op1=ALU.mult).then_inc(rh_ready.s, 1)

            def gate_z(g, step):
                for f in range(H):
                    dve.wait_ge(z_ready.s, z_ready.at(g, step * H + f + 1))
                    TT(tz[:, f, :], pairA(3 + 5 * step)[:, f, :], u3h_sb[:, f, :], ALU.add).then_inc(zsum_ready.s, 1)

            def update(g, step):
                k = step * H
                for f in range(H):
                    dve.wait_ge(th_ready.s, th_ready.at(g, k + f + 1))
                    TT(th[:, f, :], th[:, f, :], h[:, f, :], ALU.subtract).then_inc(d_ready.s, 1)
                    dve.wait_ge(tz_ready.s, tz_ready.at(g, k + f + 1))
                    dve.wait_ge(d_ready.s, d_ready.at(g, k + f + 1))
                    nc.vector.scalar_tensor_tensor(out=th[:, f, :], in0=tz[:, f, :], scalar=1.0, in1=th[:, f, :],
                                                   op0=ALU.add, op1=ALU.mult).then_inc(zd_ready.s, 1)
                    dve.wait_ge(zd_ready.s, zd_ready.at(g, k + f + 1))
                    nc.vector.scalar_tensor_tensor(out=h[:, f, :], in0=th[:, f, :], scalar=0.5, in1=h[:, f, :],
                                                   op0=ALU.mult, op1=ALU.add).then_inc(hn_ready.s, 1)
                if step < STEPS - 1:
                    split_h(g, step + 1)

            def turn_h(g, step):
                if step < STEPS - 1:
                    return
                src = tok(pairA(5 + 5 * step))
                dve.wait_ge(x_copied.s, x_copied.at(g, 1))
                for k in range(2):
                    dve.wait_ge(hT_ready.s, hT_ready.at(g, 2 * step + k + 1))
                    TT(pre1[:, 2 * k:2 * k + 2, :], src[:, 2 * k:2 * k + 2, :], x_res[:, 2 * k:2 * k + 2, :], ALU.add
                       ).then_inc(pre1_ready.s, 1)

            def stats(g, n):
                src, ready, base, per = ((pre1, pre1_ready, 0, 2), (pre, pre2_ready, 0, 1), (pre, o2_ready, 0, 2),
                                         (pre, pre3_ready, 0, 1), (pre, pre4_ready, 0, 2))[n]
                for t in range(T):
                    dve.wait_ge(ready.s, ready.at(g, t // per + 1))
                    nc.vector.bn_stats(ln_st[:, t, :], src[:, t, :]).then_inc(ln_stats.s, 1)
                dve.wait_ge(ln_stats.s, ln_stats.at(g, (n + 1) * T))
                dve.sem_inc(passed_dve.s, 1)
                for t in range(T):
                    nc.vector.bn_aggr(ln_mv[:, t, :], ln_st[:, t, :]).then_inc(ln_aggr.s, 1)
                dve.wait_ge(ln_aggr.s, ln_aggr.at(g, (n + 1) * T))
                if n > 0 or not first(g):
                    dve.wait_ge(ln_rstd.s, ln_rstd.at(g, n))
                    dve.wait_ge(ln_shift.s, ln_shift.at(g, n - (n > 2)))
                nc.vector.tensor_scalar(ln_ve[:, :], ln_mv[:, :, 1], LN_EPS, None, ALU.add).then_inc(ln_vareps.s, 1)
                nc.vector.tensor_scalar(ln_nm[:, :], ln_mv[:, :, 0], -1.0, None, ALU.mult).then_inc(ln_vareps.s, 1)

            def turn_y(g, n):
                for f in range(H):
                    dve.wait_ge(yTh_ready.s, yTh_ready.at(g, n * H + f + 1))
                    TT(yTl[:, f, :], turn_pair[n][:, f, :], f32(yTh[:, f, :]), ALU.subtract).then_inc(yTl_ready.s, 1)

            def products_t(g, n):
                for f in range(H):
                    dve.wait_ge(tTh_ready.s, tTh_ready.at(g, f + 1))
                    TT(tTl[:, f, :], pair1[:, f, :], f32(tTh[:, f, :]), ALU.subtract).then_inc(tTl_ready.s, 1)

            def relate(g, n):
                dve.wait_ge(rel_ready.s, rel_ready.at(g, 1))
                TT(relw[:, :, :], pair1[:, 0, :].rearrange("p (t n) -> p t n", t=T),
                   adj_bd[:, :].unsqueeze(1).to_broadcast([P, T, P]), ALU.mult).then_inc(relw_ready.s, 1)

            def mix1(g, n):
                dve.wait_ge(norm2_ready.s, norm2_ready.at(g, 1))
                nc.vector.tensor_copy(norm2[:, :], pair1[:, 1, 0:T]).then_inc(norm2_copied.s, 1)

            def residual1(g, n):
                dve.wait_ge(rnorm_ready.s, rnorm_ready.at(g, 1))
                for t in range(T):
                    dve.wait_ge(mix1_ready.s, mix1_ready.at(g, t // 2 + 1))
                    nc.vector.scalar_tensor_tensor(out=pre[:, t, :], in0=tok(pair0)[:, t, :], scalar=rnorm[:, t:t + 1],
                                                   in1=y1[:, t, :], op0=ALU.mult, op1=ALU.add).then_inc(pre2_ready.s, 1)

            def softmax(g, n):
                dve.wait_ge(score_ready.s, score_ready.at(g, 1))
                for k in range(R + 2):
                    if k < R:
                        TT(probs[:, k, :, :], psB[:, k, :].rearrange("p (a n) -> p a n", n=N),
                           mask_add[:, :].unsqueeze(1).to_broadcast([P, T * H, N]), ALU.add).then_inc(masked_ready.s, 1)
                    if 1 <= k <= R:
                        r = k - 1
                        dve.wait_ge(masked_ready.s, masked_ready.at(g, r + 1))
                        nc.vector.tensor_reduce(smax[:, r * T * H:(r + 1) * T * H], probs[:, r, :, :], AX.X, ALU.max
                                                ).then_inc(smax_ready.s, 1)
                    if k >= 2:
                        r = k - 2
                        dve.wait_ge(smax_ready.s, smax_ready.at(g, r + 1))
                        TT(probs[:, r, :, :], probs[:, r, :, :],
                           smax[:, r * T * H:(r + 1) * T * H].unsqueeze(2).to_broadcast([P, T * H, N]), ALU.subtract
                           ).then_inc(shifted_ready.s, 1)

            def divide(g, n):
                dve.wait_ge(heads_ready.s, heads_ready.at(g, 1))
                heads = psB[:, :, 0:R * H * (HD + 1)].rearrange("p t (r f c) -> p t r f c", r=R, f=H)
                nc.vector.reciprocal(rsum[:, :, :, :], heads[:, :, :, :, HD]).then_inc(rsum_ready.s, 1)
                dve.wait_ge(rsum_ready.s, rsum_ready.at(g, 1))
                for t in range(T):
                    TT(o_tok[:, t, :].rearrange("p (f r d) -> p r f d", f=H, r=R), heads[:, t, :, :, 0:HD],
                       rsum[:, t, :, :].unsqueeze(3).to_broadcast([P, R, H, HD]), ALU.mult).then_inc(o_ready.s, 1)

            def project(g, n):
                for k in range(2):
                    dve.wait_ge(proj_ready.s, proj_ready.at(g, k + 1))
                    TT(pre[:, 2 * k:2 * k + 2, :], tok(pair1)[:, 2 * k:2 * k + 2, :],
                       bproj_bc[:, :].unsqueeze(1).to_broadcast([P, 2, D]), ALU.add).then_inc(o2_ready.s, 1)

            def residual2(g, n):
                for t in range(T):
                    nc.vector.scalar_tensor_tensor(out=o_tok[:, t, :], in0=pre[:, t, :], scalar=ln_mv[:, t, 0:1],
                                                   in1=gamma_bc[:, :], op0=ALU.subtract, op1=ALU.mult
                                                   ).then_inc(gam_ready.s, 1)
                dve.wait_ge(ln_rstd.s, ln_rstd.at(g, 3))
                dve.wait_ge(res2_ready.s, res2_ready.at(g, 2))
                for t in range(T):
                    dve.wait_ge(gam_ready.s, gam_ready.at(g, t + 1))
                    nc.vector.scalar_tensor_tensor(out=pre[:, t, :], in0=o_tok[:, t, :], scalar=ln_rs[:, t:t + 1],
                                                   in1=y1[:, t, :], op0=ALU.mult, op1=ALU.add).then_inc(pre3_ready.s, 1)

            def logits3(g, n):
                dve.wait_ge(s_ready.s, s_ready.at(g, 1))
                nc.vector.tensor_copy(s_tok[:, :, :].rearrange("p t w -> p (t w)"), pair0[:, 0, 0:2 * T]).then_inc(s_copied.s, 1)
                dve.wait_ge(s_copied.s, s_copied.at(g, 1))
                dve.wait_ge(s_ready.s, s_ready.at(g, 2))
                for b in range(2):
                    rows = slice(b * N, (b + 1) * N)
                    TT(e3[rows, :, :], pair0[rows, 1, :].rearrange("p (t b j) -> p t b j", t=T, b=2)[:, :, b, :],
                       s_tok[rows, :, 0:1].to_broadcast([N, T, N]), ALU.add).then_inc(e_sum.s, 1)
                dve.wait_ge(e_sum.s, e_sum.at(g, 2))
                nc.vector.scalar_tensor_tensor(out=e3[:, :, :], in0=e3[:, :, :], scalar=LEAKY_SLOPE, in1=e3[:, :, :],
                                               op0=ALU.mult, op1=ALU.max).then_inc(e_leaky.s, 1)
                dve.wait_ge(e_leaky.s, e_leaky.at(g, 1))
                TT(e3[:, :, :], e3[:, :, :], adj2[:, :].unsqueeze(1).to_broadcast([P, T, N]), ALU.mult).then_inc(e_mask.s, 1)
                dve.wait_ge(e_mask.s, e_mask.at(g, 1))
                nc.vector.tensor_reduce(e3max[:, :], e3[:, :, :], AX.X, ALU.max).then_inc(e_max.s, 1)
                dve.wait_ge(e_max.s, e_max.at(g, 1))
                TT(e3[:, :, :], e3[:, :, :], e3max[:, :].unsqueeze(2).to_broadcast([P, T, N]), ALU.subtract).then_inc(e_shift.s, 1)

            def softmax3(g, n):
                dve.wait_ge(e_exp.s, e_exp.at(g, 1))
                nc.vector.tensor_reduce(e3sum[:, :], e3[:, :, :], AX.X, ALU.add).then_inc(e_total.s, 1)
                dve.wait_ge(e_total.s, e_total.at(g, 1))
                nc.vector.reciprocal(e3inv[:, :], e3sum[:, :]).then_inc(e_inv.s, 1)
                dve.wait_ge(e_inv.s, e_inv.at(g, 1))
                TT(e3[:, :, :], e3[:, :, :], e3inv[:, :].unsqueeze(2).to_broadcast([P, T, N]), ALU.mult).then_inc(e_norm.s, 1)
                dve.wait_ge(e_norm.s, e_norm.at(g, 1))
                for b in range(2):
                    rows = slice(b * N, (b + 1) * N)
                    TT(att_bd[rows, :, rows], e3[rows, :, :], beta_eye[rows, :].unsqueeze(1).to_broadcast([N, T, N]),
                       ALU.add).then_inc(att_ready.s, 1)

            def elu(g, n):
                for k in range(2):
                    rows = slice(2 * k, 2 * k + 2)
                    dve.wait_ge(elu_exp.s, elu_exp.at(g, k + 1))
                    nc.vector.tensor_scalar(o_tok[:, rows, :], o_tok[:, rows, :], 1.0, -1.0, ALU.min, ALU.add).then_inc(elu_neg.s, 1)
                    dve.wait_ge(elu_neg.s, elu_neg.at(g, k + 1))
                    TT(pre[:, rows, :], tok(pair1)[:, rows, :], o_tok[:, rows, :], ALU.max).then_inc(elu_ready.s, 1)

            whole_program(dve, dict(
                turn_x=turn_x, neighbours=neighbours, gate_r=gate_r, gate_z=gate_z, update=update, turn_h=turn_h,
                stats=stats, turn_y=turn_y, products_t=products_t, relate=relate, mix1=mix1, residual1=residual1,
                softmax=softmax, divide=divide, project=project, residual2=residual2, logits3=logits3,
                softmax3=softmax3, elu=elu))


_INS = ['x', 'adj', 'L0_gnn_w3_w', 'L0_gnn_w3_b', 'L0_gnn_u3_w', 'L0_gnn_u3_b', 'L0_gnn_w4_w', 'L0_gnn_w4_b',
        'L0_gnn_w5_w', 'L0_gnn_w5_b', 'L0_gnn_u5_w', 'L0_gnn_u5_b', 'L1_gnn_Wq', 'L1_gnn_Wk', 'L1_gnn_Wv',
        'L2_gnn_w_qkv', 'L2_gnn_w_proj', 'L2_gnn_b_proj', 'L2_gnn_ln_gamma', 'L2_gnn_ln_beta', 'L3_gnn_W',
        'L3_gnn_a', 'L3_gnn_beta']
_OUTS = [((128, 64, 256), 'float32')]


def kernel(**inputs):
    import numpy as _np
    import concourse.bacc as _bacc
    from concourse import mybir as _mybir
    from concourse.bass_utils import run_bass_kernel_spmd as _run

    nc = _bacc.Bacc("TRN2", target_bir_lowering=False, num_devices=1)
    arrays, args = {}, []
    for name in _INS:
        arr = _np.ascontiguousarray(inputs[name])
        arrays[f"in_{name}_dram"] = arr
        args.append(nc.dram_tensor(f"in_{name}_dram", arr.shape, _mybir.dt.from_np(arr.dtype), kind="ExternalInput").ap())
    for i, (shape, dtype) in enumerate(_OUTS):
        dt = _mybir.dt.from_np(_np.dtype(dtype))
        args.append(nc.dram_tensor(f"out_{i}_dram", shape, dt, kind="ExternalOutput").ap())
    gnn_kernel(nc, *args)
    r = _run(nc, [arrays], core_ids=[0])
    got = tuple(r.results[0][f"out_{i}_dram"] for i in range(len(_OUTS)))
    return got[0]
```

```python
from contextlib import ExitStack

import concourse.bass as bass
from concourse import mybir

F32 = mybir.dt.float32
F32R = mybir.dt.float32r
ALU = mybir.AluOpType
ACT = mybir.ActivationFunctionType
AX = mybir.AxisListType

P = 128
STEPS = 3
HEADS = 8
LN_EPS = 1e-5
MASKED = -3.0e38
LEAKY_SLOPE = 0.2

ORDER = [
    ("B", "scores", 2, 1), ("A", "neighbours", 2, 1), ("B", "scores", 3, 1), ("A", "gate_u", 2, 1),
    ("B", "softmax", 0, 1), ("A", "gate_r", 2, 1), ("A", "gate_z", 2, 1), ("C", "turn_att", 0, 1),
    ("A", "gate_w", 2, 1), ("A", "gate_v", 2, 1), ("B", "softmax", 1, 1), ("C", "mix3", 0, 1),
    ("B", "turn_probs", 0, 1), ("A", "update", 2, 1), ("A", "turn_h", 2, 1), ("C", "elu", 0, 1),
    ("B", "attend", 0, 1), ("B", "divide", 0, 1), ("A", "turn_x", 0, 0), ("A", "neighbours", 0, 0),
    ("A", "stats_x", 0, 1), ("C", "stats", 2, 1), ("C", "turn_c", 0, 0), ("A", "gate_u", 0, 0),
    ("A", "gate_r", 0, 0), ("A", "normalise_x", 0, 1), ("A", "gate_z", 0, 0), ("B", "turn_y", 0, 0),
    ("C", "normalise", 2, 1), ("C", "project", 0, 0), ("C", "stats", 0, 0), ("A", "gate_w", 0, 0),
    ("A", "gate_v", 0, 0), ("A", "update", 0, 0), ("B", "products_t", 0, 0), ("C", "residual2", 0, 0),
    ("A", "turn_h", 0, 0), ("B", "products_v", 0, 0), ("B", "relate", 0, 0), ("C", "stats", 1, 0),
    ("A", "neighbours", 1, 0), ("B", "mix1", 0, 0), ("C", "normalise", 1, 0), ("B", "residual1", 0, 0),
    ("A", "gate_u", 1, 0), ("B", "stats_y", 0, 0), ("A", "gate_r", 1, 0), ("C", "turn_c", 1, 0),
    ("B", "normalise_y", 0, 0), ("A", "gate_z", 1, 0), ("C", "products_s", 0, 0), ("B", "turn_y", 1, 0),
    ("A", "gate_w", 1, 0), ("C", "products_s2", 0, 0), ("B", "product_q", 0, 0), ("B", "product_k", 0, 0),
    ("B", "product_v", 0, 0), ("A", "gate_v", 1, 0), ("C", "logits3", 0, 0), ("B", "scores", 0, 0),
    ("A", "update", 1, 0), ("C", "products_h", 0, 0), ("B", "scores", 1, 0), ("C", "softmax3", 0, 0),
    ("A", "turn_h", 1, 0),
]


class Signal:

    def __init__(self, sem, per):
        self.s, self.per = sem, per

    def at(self, g, k):
        return g * self.per + k


def gnn_kernel(nc, x, adj, w3, w3_b, u3, u3_b, w4, w4_b, w5, w5_b, u5, u5_b, Wq, Wk, Wv,
               w_qkv, w_proj, b_proj, ln_gamma, ln_beta, W, a, beta, out):
    BATCH, N, D = x.shape
    T = 4
    GT = T * P
    GROUPS = BATCH * N // GT
    H = D // P
    HD = D // HEADS
    R = P // HD
    SCALE = float(HD) ** -0.5
    assert P == 2 * N and H == 2 and R == 4

    x_g = x.rearrange("(g t b) n d -> g (b n) t d", t=T, b=2)
    out_g = out.rearrange("(g t b) n d -> g (b n) t d", t=T, b=2)

    with ExitStack() as ctx:
        def sb(name, shape, dt=F32):
            return ctx.enter_context(nc.sbuf_tensor(name, shape, dt))

        def sig(name, per=0):
            return Signal(ctx.enter_context(nc.semaphore(name)), per)

        psA = ctx.enter_context(nc.psum_tensor("psA", [P, 2, GT], F32))
        psB = ctx.enter_context(nc.psum_tensor("psB", [P, 4, GT], F32))
        psC = ctx.enter_context(nc.psum_tensor("psC", [P, 2, GT], F32))

        w3h, w3l, w4h, w4l, w5h, w5l, u3h, u3l, wvh, wvl, mh, ml, wph, wpl, w3gh, w3gl = (
            sb(n, [P, H, D], F32R) for n in
            ("w3h", "w3l", "w4h", "w4l", "w5h", "w5l", "u3h", "u3l", "wvh", "wvl", "mh", "ml",
             "wph", "wpl", "w3gh", "w3gl"))
        u5t = sb("u5t", [P, H, D])
        qkvh, qkvl = sb("qkvh", [P, H, 3 * D], F32R), sb("qkvl", [P, H, 3 * D], F32R)
        wah, wal = sb("wah", [P, H, 2], F32R), sb("wal", [P, H, 2], F32R)
        wa2h, wa2l = sb("wa2h", [P, H, P], F32R), sb("wa2l", [P, H, P], F32R)
        wa32 = sb("wa32", [P, H, 2])
        a_sb = sb("a_sb", [P, 2, H])
        biases = sb("biases", [P, 5, H])
        bias_z, bias_r, bias_h = (sb(n, [P, H]) for n in ("bias_z", "bias_r", "bias_h"))
        bproj_bc, gamma_bc, beta_bc = (sb(n, [P, D]) for n in ("bproj_bc", "gamma_bc", "beta_bc"))
        ident = sb("ident", [P, P])
        adj2 = sb("adj2", [P, N])
        adj_bd = sb("adj_bd", [P, P])
        adjT_bd = sb("adjT_bd", [P, P])
        mask_add = sb("mask_add", [P, N])
        beta_col = sb("beta_col", [P, 1])
        beta_eye = sb("beta_eye", [P, N])
        minus_half = sb("minus_half", [P, T])
        ones_col = sb("ones_col", [P, 1])

        x_in = sb("x_in", [P, T, D])
        x_res = sb("x_res", [P, T, D])
        h_tok = sb("h_tok", [P, T, D])
        h = sb("h", [P, H, GT])
        hh, hl = sb("hh", [P, H, GT], F32R), sb("hl", [P, H, GT], F32R)
        ah, al = sb("ah", [P, H, GT], F32R), sb("al", [P, H, GT], F32R)
        tr, tz, th = (sb(n, [P, H, GT]) for n in ("tr", "tz", "th"))
        rh = tr
        pre1 = h_tok

        y1, y2, pre2 = (sb(n, [P, T, D]) for n in ("y1", "y2", "pre2"))
        yTh, yTl = sb("yTh", [P, H, GT], F32R), sb("yTl", [P, H, GT], F32R)
        tTh, tTl = sb("tTh", [P, H, GT], F32R), sb("tTl", [P, H, GT], F32R)
        v1 = sb("v1", [P, T, D])
        rel = sb("rel", [P, 2, T, P])
        relw, relsq = rel[:, 0, :, :], rel[:, 1, :, :]
        qk = [b.rearrange("p h n -> p (h n)").rearrange("p (h n) -> p h n", h=H)
              for b in (v1[:, :, :], rel[:, :, :, :].rearrange("p s t n -> p (s t) n"))]
        norm2, rnorm = sb("norm2", [P, T]), sb("rnorm", [P, T])
        vbd = sb("vbd", [P, T, 2, R, H, HD + 1])
        probs = sb("probs", [P, R, T * H, N])
        probsT = sb("probsT", [P, R, GT])
        smax = sb("smax", [P, R * T * H])
        rsum = sb("rsum", [P, T, R, H])
        o_tok = sb("o_tok", [P, T, D])

        y3, y4, pre = (sb(n, [P, T, D]) for n in ("y3", "y4", "pre"))
        cTh, cTl = sb("cTh", [P, H, GT], F32R), sb("cTl", [P, H, GT], F32R)
        h3 = sb("h3", [P, T, D])
        s_tok = sb("s_tok", [P, T, 2])
        e3 = sb("e3", [P, T, N])
        e3max, e3sum, e3inv = sb("e3max", [P, T]), sb("e3sum", [P, T]), sb("e3inv", [P, T])
        att_bd, attT = sb("att_bd", [P, T, P]), sb("attT", [P, T, P])

        ln_st, ln_mv = ([sb(n + s, [P, T, w]) for s in "ABC"] for n, w in (("ln_st", 6), ("ln_mv", 2)))
        ln_ve, ln_rs, ln_nm, ln_nb = ([sb(n + s, [P, T]) for s in "ABC"] for n in ("ln_ve", "ln_rs", "ln_nm", "ln_nb"))

        w3_in = probs[:, :, :, :].rearrange("p r a n -> p (r a n)")[:, 0:4 * D].rearrange(
            "p (c i) -> p c i", c=H)
        w4_in = probs[:, :, :, :].rearrange("p r a n -> p (r a n)")[:, 4 * D:8 * D].rearrange(
            "p (c i) -> p c i", c=H)
        pT_flat = probsT[:, :, :].rearrange("p r n -> p (r n)")
        w5_in = pT_flat[:, 0:4 * D].rearrange("p (c i) -> p c i", c=H)
        u3_in = pT_flat[:, 4 * D:6 * D].rearrange("p (c i) -> p c i", c=H)
        u5_in = pT_flat[:, 6 * D:8 * D].rearrange("p (c i) -> p c i", c=H)
        Wq_in, Wk_in, Wv_in, W_in = (
            b[:, k, :].rearrange("p (c i) -> p c i", c=H) for b in (tr, tz) for k in range(2))
        WT = v1[:, 0:2, :]
        qkv_in = [y2[:, 0:3, :].rearrange("p t d -> p (t d)"), y3[:, 0:3, :].rearrange("p t d -> p (t d)")]
        wp_in = y1[:, 0:2, :]

        p_load = {n: sig("p_" + n) for n in
                  ("w3", "w4", "w5", "u3", "u5", "wq", "wk", "wv", "qkv", "wp", "W", "a", "adj2",
                   "adjbd", "bias", "rows", "beta")}
        p_ident0, p_ident = sig("p_ident0"), sig("p_ident")
        p_adj0 = sig("p_adj0")
        p_vbd0 = sig("p_vbd0")
        p_fold = sig("p_fold")
        p_turned = sig("p_turned")
        p_hi = sig("p_hi")
        p_lo = sig("p_lo")
        p_wa = sig("p_wa")
        p_wa_sb = sig("p_wa_sb")
        p_small = sig("p_small")
        p_done_act, p_done_dve, p_done_pool = sig("p_done_act"), sig("p_done_dve"), sig("p_done_pool")

        passed_dve, passed_pool = sig("passed_dve"), sig("passed_pool")

        x_loaded = sig("x_loaded", 16)
        x_copied = sig("x_copied", 1)
        xT_ready = sig("xT_ready", H)
        h0_ready = sig("h0_ready", H)
        u_ready, u_copied, zsum_ready = (sig(n, STEPS * H) for n in ("u_ready", "u_copied", "zsum_ready"))
        hh_ready, hl_ready = sig("hh_ready", STEPS * H), sig("hl_ready", STEPS * H)
        aT_ready = sig("aT_ready", STEPS * H)
        ah_ready, al_ready = sig("ah_ready", STEPS * H), sig("al_ready", STEPS * H)
        r_ready, z_ready, v_ready = (sig(n, STEPS * H) for n in ("r_ready", "z_ready", "v_ready"))
        tr_ready, tz_ready, th_ready = (sig(n, STEPS * H) for n in ("tr_ready", "tz_ready", "th_ready"))
        rh_ready = sig("rh_ready", STEPS * H)
        d_ready, zd_ready, hn_ready = (sig(n, STEPS * H) for n in ("d_ready", "zd_ready", "hn_ready"))
        hT_ready = sig("hT_ready", STEPS * 2)
        htok_ready = sig("htok_ready", (STEPS - 1) * 2)
        pre1_ready = sig("pre1_ready", 2)

        ln_stats, ln_aggr = ([sig(n + s, k * T) for s, k in (("A", 1), ("B", 1), ("C", 3))]
                             for n in ("ln_stats", "ln_aggr"))
        ln_vareps, ln_rstd = ([sig(n + s, m * k) for s, k in (("A", 1), ("B", 1), ("C", 3))]
                              for n, m in (("ln_vareps", 2), ("ln_rstd", 1)))
        ln_shift = [sig("ln_shiftA", 1), sig("ln_shiftB", 1), sig("ln_shiftC", 2)]
        ln_out = [sig("y1_ready", T), sig("y2_ready", T), sig("y34_ready", 2 * T)]

        yT_ready, yTh_ready, yTl_ready = (sig(n, 2 * H) for n in ("yT_ready", "yTh_ready", "yTl_ready"))
        cT_ready, cTh_ready, cTl_ready = (sig(n, 2 * H) for n in ("cT_ready", "cTh_ready", "cTl_ready"))
        tT_ready, tTh_ready, tTl_ready = (sig(n, H) for n in ("tT_ready", "tTh_ready", "tTl_ready"))
        v1_ready, v1_copied = sig("v1_ready", 2), sig("v1_copied", 2)
        rel_ready, relw_ready, relsq_ready = sig("rel_ready", 2), sig("relw_ready", 2), sig("relsq_ready", 2)
        norm2_ready, norm2_copied, rnorm_ready = sig("norm2_ready", 1), sig("norm2_copied", 1), sig("rnorm_ready", 1)
        mix1_ready, pre2_ready = sig("mix1_ready", 2), sig("pre2_ready", T)
        qk_ready, qk_copied = sig("qk_ready", 4), sig("qk_copied", 4)
        v2_ready, v2_copied = sig("v2_ready", 2), sig("v2_copied", 4)
        score_ready, masked_ready, smax_ready = sig("score_ready", 1), sig("masked_ready", R), sig("smax_ready", R)
        shifted_ready, exp_ready = sig("shifted_ready", R), sig("exp_ready", R)
        probT_ready, probT_copied = sig("probT_ready", R), sig("probT_copied", R)
        heads_ready, rsum_ready, o_ready = sig("heads_ready", 1), sig("rsum_ready", 1), sig("o_ready", T)
        proj_ready, o2_ready = sig("proj_ready", 2), sig("o2_ready", 2)
        y2b_ready, res2_ready = sig("y2b_ready", 1), sig("res2_ready", 2)
        gam_ready, pre3_ready = sig("gam_ready", T), sig("pre3_ready", T)
        h3_ready, h3_copied = sig("h3_ready", 2), sig("h3_copied", 2)
        s_ready, s_copied, e_sum, e_leaky = sig("s_ready", 2), sig("s_copied", 1), sig("e_sum", 2), sig("e_leaky", 1)
        e_mask, e_max, e_shift, e_exp = sig("e_mask", 1), sig("e_max", 1), sig("e_shift", 1), sig("e_exp", 1)
        e_total, e_inv, e_norm, att_ready = sig("e_total", 1), sig("e_inv", 1), sig("e_norm", 1), sig("att_ready", 2)
        attT_ready, attT_copied = sig("attT_ready", 1), sig("attT_copied", 1)
        mix3_ready, elu_exp, elu_neg, elu_ready = sig("mix3_ready", 2), sig("elu_exp", 2), sig("elu_neg", 2), sig("elu_ready", 2)
        pre4_ready = sig("pre4_ready", 2)
        stored = sig("stored", 16)

        def tok(pair):
            return pair.rearrange("p k (u d) -> p (k u) d", u=2)

        pair0, pair1 = psB[:, 0:2, :], psB[:, 2:4, :]

        def run(chunks, i):
            for stream, name, n, late in ORDER:
                g = i + {"A": 3, "B": 2, "C": 1}[stream] - late
                if name in chunks and not (isinstance(g, int) and not 0 <= g < GROUPS):
                    chunks[name](g, n)

        def whole_program(eng, chunks):
            for i in range(-3, 1):
                run(chunks, i)
            with eng.Fori(1, GROUPS - 3) as g:
                run(chunks, g)
            for i in range(GROUPS - 3, GROUPS):
                run(chunks, i)

        def first(g):
            return isinstance(g, int) and g == 0

        block = ctx.enter_context(nc.Block())

        @block.sync
        def _(sp):
            sp.dma_start(adj2[0:N, :], adj).then_inc(p_load["adj2"].s, 16)
            sp.dma_start(adj2[N:P, :], adj).then_inc(p_load["adj2"].s, 16)
            for dst, src, n in ((u3_in, u3, "u3"), (w4_in, w4, "w4"), (w3_in, w3, "w3"), (w5_in, w5, "w5"),
                                (u5_in, u5, "u5"), (Wv_in, Wv, "wv"), (Wq_in, Wq, "wq"), (Wk_in, Wk, "wk"),
                                (W_in, W, "W"), (wp_in, w_proj, "wp")):
                sp.dma_start(dst, src.rearrange("(c p) i -> p c i", p=P)).then_inc(p_load[n].s, 16)
            for c in range(H):
                sp.dma_start(qkv_in[c], w_qkv[c * P:(c + 1) * P, :]).then_inc(p_load["qkv"].s, 16)
            sp.wait_ge(p_adj0.s, 1)
            for b in range(2):
                sp.dma_start(adj_bd[b * N:(b + 1) * N, b * N:(b + 1) * N], adj).then_inc(p_load["adjbd"].s, 16)

            def turn_x(g, step):
                if not first(g):
                    sp.wait_ge(x_copied.s, x_copied.at(g - 1, 1))
                    sp.wait_ge(aT_ready.s, aT_ready.at(g - 1, H))
                sp.dma_start(x_in[:, :, :], x_g[bass.ds(g, 1)].rearrange("a p t d -> (a p) t d")
                             ).then_inc(x_loaded.s, 16)

            def store(g):
                sp.wait_ge(ln_out[2].s, ln_out[2].at(g, 2 * T))
                sp.dma_start(out_g[bass.ds(g, 1)].rearrange("a p t d -> (a p) t d"), y4[:, :, :]
                             ).then_inc(stored.s, 16)

            def run_ahead(gA, gB):
                if gA is not None:
                    turn_x(gA, 0)
                if gB is not None:
                    store(gB)

            for g in range(3):
                run_ahead(g, None)
            with sp.Fori(0, GROUPS - 3) as g:
                run_ahead(g + 3, g)
            for g in range(GROUPS - 3, GROUPS):
                run_ahead(None, g)
            sp.wait_ge(stored.s, stored.at(GROUPS - 1, 16))

        @block.gpsimd
        def _(pool):
            nc.gpsimd.memset(ident[:, :], 0.0).then_inc(p_ident0.s, 1)
            nc.gpsimd.memset(adj_bd[:, :], 0.0).then_inc(p_adj0.s, 1)
            pool.wait_ge(p_ident0.s, 1)
            nc.gpsimd.affine_select(out=ident[:, :], in_=ident[:, :], compare_op=ALU.not_equal, fill=1.0,
                                    base=0, pattern=[[-1, P]], channel_multiplier=1).then_inc(p_ident.s, 1)
            for t, src in enumerate((w3_b, w4_b, w5_b, u3_b, u5_b)):
                for c in range(H):
                    pool.dma_start(biases[:, t, c:c + 1], src[c * P:(c + 1) * P].unsqueeze(1)
                                   ).then_inc(p_load["bias"].s, 16)
            for k in range(2 * H):
                pool.dma_start(a_sb[:, k // H, k % H:k % H + 1], a[k * P:(k + 1) * P, :]).then_inc(p_load["a"].s, 16)
            for dst, src in ((bproj_bc, b_proj), (gamma_bc, ln_gamma), (beta_bc, ln_beta)):
                pool.dma_start(dst[:, :], src.rearrange("(a d) -> a d", a=1).to_broadcast([P, D])
                               ).then_inc(p_load["rows"].s, 16)
            pool.dma_start(beta_col[:, :], beta.rearrange("(a d) -> a d", a=1).to_broadcast([P, 1])
                           ).then_inc(p_load["beta"].s, 16)
            nc.gpsimd.memset(att_bd[:, :, :], 0.0)
            nc.gpsimd.memset(minus_half[:, :], -0.5)
            nc.gpsimd.memset(ones_col[:, :], 1.0)
            nc.gpsimd.memset(vbd[:, :, :, :, :, :], 0.0).then_inc(p_vbd0.s, 1)
            pool.wait_ge(p_vbd0.s, 1)
            for f in range(H):
                last = nc.gpsimd.memset(
                    vbd[f * N:(f + 1) * N, :, :, :, f, HD:HD + 1].rearrange("p t b r o -> p (t b) r o"), 1.0)
            last.then_inc(p_done_pool.s, 1)
            pool.wait_ge(p_done_pool.s, 1)
            pool.wait_ge(p_load["rows"].s, 48)

            def turn_x(g, step):
                if not first(g):
                    pool.wait_ge(pre1_ready.s, pre1_ready.at(g - 1, 2))
                pool.wait_ge(x_loaded.s, x_loaded.at(g, 16))
                pool.sem_inc(passed_pool.s, 1)
                nc.gpsimd.tensor_copy(x_res[:, :, :], x_in[:, :, :]).then_inc(x_copied.s, 1)

            def norm(g, n, s):
                pool.wait_ge(ln_vareps[s].s, ln_vareps[s].at(g, 2 * n + 2))
                if n == 2 or (n == 0 and not first(g)):
                    pool.wait_ge(ln_out[s].s, ln_out[s].at(g, max(n - 1, 0) * T))
                nc.gpsimd.tensor_tensor(ln_rs[s][:, :], ln_ve[s][:, :], minus_half[:, :], ALU.pow
                                        ).then_inc(ln_rstd[s].s, 1)
                if (s, n) != (2, 0):
                    pool.wait_ge(ln_rstd[s].s, ln_rstd[s].at(g, n + 1))
                    nc.gpsimd.tensor_tensor(ln_nb[s][:, :], ln_nm[s][:, :], ln_rs[s][:, :], ALU.mult
                                            ).then_inc(ln_shift[s].s, 1)

            def stats_x(g, n):
                norm(g, 0, 0)

            def stats_y(g, n):
                norm(g, 0, 1)

            def stats(g, n):
                norm(g, n, 2)

            def mix1(g, n):
                pool.wait_ge(norm2_copied.s, norm2_copied.at(g, 1))
                nc.gpsimd.tensor_tensor(rnorm[:, :], norm2[:, :], minus_half[:, :], ALU.pow).then_inc(rnorm_ready.s, 1)

            def product_q(g, n):
                pool.wait_ge(yT_ready.s, yT_ready.at(g, 2 * H))
                nc.gpsimd.tensor_tensor(y2[:, :, :], y2[:, :, :], beta_bc[:, :].unsqueeze(1).to_broadcast([P, T, D]),
                                        ALU.add).then_inc(y2b_ready.s, 1)

            def project(g, n):
                for k in range(2):
                    rows = slice(2 * k, 2 * k + 2)
                    pool.wait_ge(o2_ready.s, o2_ready.at(g, k + 1))
                    if k == 0:
                        pool.wait_ge(y2b_ready.s, y2b_ready.at(g, 1))
                    nc.gpsimd.tensor_tensor(y2[:, rows, :], y2[:, rows, :], y3[:, rows, :],
                                            ALU.add).then_inc(res2_ready.s, 1)

            def elu(g, n):
                for k in range(2):
                    pool.wait_ge(elu_ready.s, elu_ready.at(g, k + 1))
                    nc.gpsimd.tensor_tensor(pre[:, 2 * k:2 * k + 2, :], pre[:, 2 * k:2 * k + 2, :],
                                            y3[:, 2 * k:2 * k + 2, :], ALU.add).then_inc(pre4_ready.s, 1)

            whole_program(pool, dict(turn_x=turn_x, stats_x=stats_x, stats_y=stats_y, stats=stats, mix1=mix1, product_q=product_q,
                                     project=project, elu=elu))

        @block.tensor
        def _(pe):
            def turn_weight(bank, src):
                for i in range(H):
                    for o in range(H):
                        last = nc.tensor.transpose(bank[:, i * D + o * P:i * D + (o + 1) * P],
                                                   src[:, o, i * P:(i + 1) * P], ident[:, :])
                last.then_inc(p_turned.s, 1)

            pe.wait_ge(p_ident.s, 1)
            pe.wait_ge(p_load["adjbd"].s, 32)
            nc.tensor.transpose(psA[:, 0, 0:P], adj_bd[:, :], ident[:, :]).then_inc(p_turned.s, 1)
            pe.wait_ge(p_load["u3"].s, 16)
            turn_weight(psA[:, 1, :], u3_in)
            for k, (bank, src) in enumerate(((psC[:, 0, :], w4_in), (psC[:, 1, :], w3_in), (psB[:, 0, :], w5_in))):
                pe.wait_ge(p_fold.s, k + 1)
                turn_weight(bank, src)
            pe.wait_ge(p_load["u5"].s, 16)
            turn_weight(psB[:, 1, :], u5_in)
            pe.wait_ge(p_load["wv"].s, 16)
            turn_weight(psB[:, 2, :], Wv_in)
            pe.wait_ge(p_load["wq"].s, 16)
            pe.wait_ge(p_load["wk"].s, 16)
            for i in range(H):
                for c in range(H):
                    last = nc.tensor.matmul(psB[:, 3, i * D:(i + 1) * D], Wq_in[:, c, i * P:(i + 1) * P],
                                            Wk_in[:, c, :], start=(c == 0), stop=(c == H - 1))
            last.then_inc(p_turned.s, 1)
            pe.wait_ge(p_load["W"].s, 16)
            pe.wait_ge(p_hi.s, 1)
            turn_weight(psA[:, 0, :], W_in)
            pe.wait_ge(p_hi.s, 9)
            pe.wait_ge(p_load["a"].s, 32 * H)
            pe.wait_ge(p_lo.s, 1)
            for i in range(H):
                for c in range(H):
                    last = nc.tensor.matmul(psA[:, 1, 2 * i:2 * i + 2], WT[:, c, i * P:(i + 1) * P],
                                            a_sb[:, :, c], start=(c == 0), stop=(c == H - 1))
            last.then_inc(p_wa.s, 1)
            pe.wait_ge(p_done_act.s, 1)
            pe.wait_ge(p_done_dve.s, 1)
            pe.wait_ge(p_done_pool.s, 1)

            def parts3(out, wh, wl, xh, xl, cols, start, stop, reopened=False, arrival=None):
                n = 0
                for c in range(H):
                    for w_, x_ in ((wh, xh), (wl, xh), (wh, xl)):
                        if arrival and (w_, x_) == (wh, xh):
                            pe.wait_ge(arrival[0].s, arrival[0].at(arrival[2], arrival[3] + c + 1))
                        if arrival and x_ is xl:
                            pe.wait_ge(arrival[1].s, arrival[1].at(arrival[2], arrival[3] + c + 1))
                        last = nc.tensor.matmul(out, w_[:, c, cols], x_[:, c, :], start=start and n == 0,
                                                stop=stop and n == 3 * H - 1, skip_group_check=reopened)
                        n += 1
                return last

            def token3(out, t, xh, xl, wh, wl, cols, arrival=None):
                rows = slice(t * P, (t + 1) * P)
                n = 0
                for c in range(H):
                    if arrival and t == 0:
                        pe.wait_ge(arrival[0].s, arrival[0].at(arrival[2], arrival[3] + c + 1))
                        pe.wait_ge(arrival[1].s, arrival[1].at(arrival[2], arrival[3] + c + 1))
                    for x_, w_ in ((xh, wh), (xh, wl), (xl, wh)):
                        last = nc.tensor.matmul(out, x_[:, c, rows], w_[:, c, cols], start=n == 0,
                                                stop=n == 3 * H - 1)
                        n += 1
                return last

            def turn_x(g, step):
                pe.wait_ge(x_loaded.s, x_loaded.at(g, 16))
                if not first(g):
                    pe.wait_ge(pre1_ready.s, pre1_ready.at(g - 1, 2))
                for f in range(H):
                    for t in range(T):
                        last = nc.tensor.transpose(psA[:, f, t * P:(t + 1) * P],
                                                   x_in[:, t, f * P:(f + 1) * P], ident[:, :])
                    last.then_inc(xT_ready.s, 1)

            def neighbours(g, step):
                src = x_in if step == 0 else h_tok
                if step > 0:
                    pe.wait_ge(htok_ready.s, htok_ready.at(g, 2 * step))
                for f in range(H):
                    if step == 0:
                        pe.wait_ge(h0_ready.s, h0_ready.at(g, f + 1))
                    for t in range(T):
                        last = nc.tensor.matmul(psA[:, f, t * P:(t + 1) * P],
                                                src[:, t, f * P:(f + 1) * P], adjT_bd[:, :],
                                                start=True, stop=True)
                    last.then_inc(aT_ready.s, 1)

            def gate_u(g, step):
                k = H * step
                for f in range(H):
                    pe.wait_ge(al_ready.s, al_ready.at(g, k + f + 1))
                    parts3(psA[:, f, :], u3h, u3l, hh, hl, slice(f * P, (f + 1) * P), True, True,
                           arrival=(hh_ready, hl_ready, g, k) if f == 0 else None).then_inc(u_ready.s, 1)

            def gate_r(g, step):
                k = H * step
                for f in range(H):
                    pe.wait_ge(u_copied.s, u_copied.at(g, k + f + 1))
                    parts3(psA[:, f, :], w4h, w4l, ah, al, slice(f * P, (f + 1) * P), False, True,
                           reopened=True).then_inc(r_ready.s, 1)

            def gate_z(g, step):
                for f in range(H):
                    pe.wait_ge(tr_ready.s, tr_ready.at(g, H * step + f + 1))
                    parts3(psA[:, f, :], w3h, w3l, ah, al, slice(f * P, (f + 1) * P), True, True
                           ).then_inc(z_ready.s, 1)

            def gate_w(g, step):
                k = H * step
                for f in range(H):
                    cols = slice(f * P, (f + 1) * P)
                    dst = psA[:, f, :]
                    pe.wait_ge(zsum_ready.s, zsum_ready.at(g, k + f + 1))
                    parts3(dst, w5h, w5l, ah, al, cols, True, False)

            def gate_v(g, step):
                k = H * step
                for f in range(H):
                    cols = slice(f * P, (f + 1) * P)
                    dst = psA[:, f, :]
                    for c in range(H):
                        if f == 0:
                            pe.wait_ge(rh_ready.s, rh_ready.at(g, k + c + 1))
                        last = nc.tensor.matmul(dst, u5t[:, c, cols], rh[:, c, :], start=False, stop=(c == H - 1))
                    last.then_inc(v_ready.s, 1)

            def turn_h(g, step):
                dst = tok(psA)
                pe.wait_ge(th_ready.s, th_ready.at(g, H * step + H))
                for f in range(H):
                    pe.wait_ge(hn_ready.s, hn_ready.at(g, H * step + f + 1))
                    for t in range(T):
                        last = nc.tensor.transpose(dst[:, t, f * P:(f + 1) * P], h[:, f, t * P:(t + 1) * P],
                                                   ident[:, :])
                        if f == H - 1 and t % 2 == 1:
                            last.then_inc(hT_ready.s, 1)

            def turn(g, n, src, ready, base, pair, done):
                for f in range(H):
                    for t in range(T):
                        if f == 0:
                            pe.wait_ge(ready.s, ready.at(g, base + t + 1))
                        last = nc.tensor.transpose(pair[:, f, t * P:(t + 1) * P],
                                                   src[:, t, f * P:(f + 1) * P], ident[:, :])
                    last.then_inc(done.s, 1)

            def turn_y(g, n):
                if n == 0 and not first(g):
                    pe.wait_ge(o_ready.s, o_ready.at(g - 1, T))
                if n == 1:
                    pe.wait_ge(norm2_copied.s, norm2_copied.at(g, 1))
                turn(g, n, (y1, y2)[n], ln_out[n], 0, (pair0, pair1)[n], yT_ready)

            def turn_c(g, n):
                if n == 0 and not first(g):
                    pe.wait_ge(elu_ready.s, elu_ready.at(g - 1, 2))
                turn(g, n, (o_tok, y3)[n], (o_ready, ln_out[2])[n], 0, psC, cT_ready)

            def splitC(g, n):
                return cTh_ready, cTl_ready, g, n * H

            def split(g, n):
                return yTh_ready, yTl_ready, g, n * H

            def products_t(g, n):
                for f in range(H):
                    parts3(pair1[:, f, :], mh, ml, yTh, yTl, slice(f * P, (f + 1) * P), True, True,
                           arrival=split(g, 0) if f == 0 else None).then_inc(tT_ready.s, 1)

            def products_v(g, n):
                for t in range(T):
                    last = token3(tok(pair0)[:, t, :], t, yTh, yTl, wvh, wvl, slice(0, D))
                    if t % 2 == 1:
                        last.then_inc(v1_ready.s, 1)

            def relate(g, n):
                pe.wait_ge(tTh_ready.s, tTh_ready.at(g, H))
                pe.wait_ge(tTl_ready.s, tTl_ready.at(g, H))
                for t in range(T):
                    cols = slice(t * P, (t + 1) * P)
                    n = 0
                    for c in range(H):
                        for y_, t_ in ((yTh, tTh), (yTh, tTl), (yTl, tTh)):
                            last = nc.tensor.matmul(tok(pair1)[:, t, 0:P], y_[:, c, cols], t_[:, c, cols],
                                                    start=n == 0, stop=n == 3 * H - 1)
                            n += 1
                    if t % 2 == 1:
                        last.then_inc(rel_ready.s, 1)

            def mix1(g, n):
                for k in range(2):
                    pe.wait_ge(v1_copied.s, v1_copied.at(g, 2))
                    pe.wait_ge(relw_ready.s, relw_ready.at(g, k + 1))
                    for t in (2 * k, 2 * k + 1):
                        last = nc.tensor.matmul(tok(pair0)[:, t, :], relw[:, t, :], v1[:, t, :], start=True, stop=True)
                    last.then_inc(mix1_ready.s, 1)
                for t in range(T):
                    pe.wait_ge(relsq_ready.s, relsq_ready.at(g, t // 2 + 1))
                    last = nc.tensor.matmul(pair1[:, 0, t:t + 1], relsq[:, t, :], ones_col[:, :], start=True, stop=True)
                last.then_inc(norm2_ready.s, 1)

            def product_q(g, n):
                for f in range(H):
                    parts3(pair0[:, f, :], qkvh, qkvl, yTh, yTl, slice(f * P, (f + 1) * P), True, True,
                           arrival=split(g, 1) if f == 0 else None).then_inc(qk_ready.s, 1)

            def product_k(g, n):
                for f in range(H):
                    parts3(pair1[:, f, :], qkvh, qkvl, yTh, yTl, slice(D + f * P, D + (f + 1) * P), True, True
                           ).then_inc(qk_ready.s, 1)

            def product_v(g, n):
                pe.wait_ge(qk_copied.s, qk_copied.at(g, 2))
                for t in range(T):
                    last = token3(tok(pair0)[:, t, :], t, yTh, yTl, qkvh, qkvl, slice(2 * D, 3 * D))
                    if t % 2 == 1:
                        last.then_inc(v2_ready.s, 1)

            def scores(g, n):
                if n == 0:
                    pe.wait_ge(qk_copied.s, qk_copied.at(g, 4))
                    pe.wait_ge(v2_copied.s, v2_copied.at(g, 4))
                for f in range(H):
                    for b in range(2):
                        cols = slice(n * P + b * N, n * P + (b + 1) * N)
                        for r in range(R):
                            rows = slice(r * HD, (r + 1) * HD)
                            last = nc.tensor.matmul(
                                psB[b * N:(b + 1) * N, r, (n * H + f) * N:(n * H + f + 1) * N],
                                qk[0][rows, f, cols], qk[1][rows, f, cols], start=True, stop=True)
                if n == T - 1:
                    last.then_inc(score_ready.s, 1)

            def turn_probs(g, n):
                for r in range(R):
                    pe.wait_ge(exp_ready.s, exp_ready.at(g, r + 1))
                    for t in range(T):
                        last = nc.tensor.transpose(
                            psB[:, r, t * P:(t + 1) * P],
                            probs[:, r, t * H:(t + 1) * H, :].rearrange("p f n -> p (f n)"), ident[:, :])
                    last.then_inc(probT_ready.s, 1)

            def attend(g, n):
                pe.wait_ge(probT_copied.s, probT_copied.at(g, R))
                for t in range(T):
                    for b in range(2):
                        for r in range(R):
                            last = nc.tensor.matmul(
                                psB[b * N:(b + 1) * N, t, r * H * (HD + 1):(r + 1) * H * (HD + 1)],
                                probsT[:, r, t * P + b * N:t * P + (b + 1) * N],
                                vbd[:, t, b, r, :, :].rearrange("p f d -> p (f d)"), start=True, stop=True)
                last.then_inc(heads_ready.s, 1)

            def project(g, n):
                for t in range(T):
                    last = token3(tok(psC)[:, t, :], t, cTh, cTl, wph, wpl, slice(0, D), splitC(g, 0))
                    if t % 2 == 1:
                        last.then_inc(proj_ready.s, 1)

            def products_s(g, n):
                for t in range(T):
                    last = token3(psC[:, 0, 2 * t:2 * t + 2], t, cTh, cTl, wah, wal, slice(0, 2), splitC(g, 1))
                last.then_inc(s_ready.s, 1)

            def products_s2(g, n):
                parts3(psC[:, 1, :], wa2h, wa2l, cTh, cTl, slice(0, P), True, True).then_inc(s_ready.s, 1)

            def products_h(g, n):
                pe.wait_ge(e_sum.s, e_sum.at(g, 2))
                for t in range(T):
                    last = token3(tok(psC)[:, t, :], t, cTh, cTl, w3gh, w3gl, slice(0, D))
                    if t % 2 == 1:
                        last.then_inc(h3_ready.s, 1)

            def turn_att(g, n):
                pe.wait_ge(att_ready.s, att_ready.at(g, 2))
                pe.wait_ge(h3_copied.s, h3_copied.at(g, 1))
                for t in range(T):
                    last = nc.tensor.transpose(psC[:, 0, t * P:(t + 1) * P], att_bd[:, t, :], ident[:, :])
                last.then_inc(attT_ready.s, 1)

            def mix3(g, n):
                pe.wait_ge(h3_copied.s, h3_copied.at(g, 2))
                pe.wait_ge(attT_copied.s, attT_copied.at(g, 1))
                for t in range(T):
                    last = nc.tensor.matmul(tok(psC)[:, t, :], attT[:, t, :], h3[:, t, :], start=True, stop=True)
                    if t % 2 == 1:
                        last.then_inc(mix3_ready.s, 1)

            whole_program(pe, dict(
                turn_x=turn_x, neighbours=neighbours, gate_u=gate_u, gate_r=gate_r, gate_z=gate_z, gate_w=gate_w, gate_v=gate_v, turn_h=turn_h,
                turn_y=turn_y, turn_c=turn_c, products_t=products_t, products_v=products_v, relate=relate,
                mix1=mix1, product_q=product_q, product_k=product_k, product_v=product_v, scores=scores,
                turn_probs=turn_probs, attend=attend, project=project, products_s=products_s, products_s2=products_s2,
                products_h=products_h, turn_att=turn_att, mix3=mix3))

        @block.scalar
        def _(act):
            whole = lambda w_: w_[:, :, :].rearrange("p c o -> p (c o)")
            act.wait_ge(p_turned.s, 1)
            nc.scalar.copy(adjT_bd[:, :], psA[:, 0, 0:P]).then_inc(p_hi.s, 1)
            for k, (dst, bank) in enumerate(((u3h, psA[:, 1, :]), (w4h, psC[:, 0, :]), (w3h, psC[:, 1, :]),
                                             (w5h, psB[:, 0, :]))):
                act.wait_ge(p_turned.s, k + 2)
                nc.scalar.copy(whole(dst), bank).then_inc(p_hi.s, 1)
            act.wait_ge(p_turned.s, 6)
            nc.scalar.mul(whole(u5t), psB[:, 1, :], 0.5).then_inc(p_hi.s, 1)
            for k, (dst, bank) in enumerate(((wvh, psB[:, 2, :]), (mh, psB[:, 3, :]))):
                act.wait_ge(p_turned.s, k + 7)
                nc.scalar.copy(whole(dst), bank).then_inc(p_hi.s, 1)
            act.wait_ge(p_turned.s, 9)
            nc.scalar.copy(WT.rearrange("p c o -> p (c o)"), psA[:, 0, :]).then_inc(p_hi.s, 1)
            act.wait_ge(p_load["qkv"].s, 32)
            for c in range(H):
                nc.scalar.copy(qkvh[:, c, :], qkv_in[c]).then_inc(p_hi.s, 1)
            act.wait_ge(p_load["wp"].s, 16)
            nc.scalar.copy(wph[:, :, :], wp_in).then_inc(p_hi.s, 1)
            act.wait_ge(p_load["W"].s, 16)
            nc.scalar.copy(w3gh[:, :, :], W_in).then_inc(p_hi.s, 1)
            act.wait_ge(p_wa.s, 1)
            nc.scalar.copy(wa32[:, :, :].rearrange("p c w -> p (c w)"), psA[:, 1, 0:2 * H]).then_inc(p_wa_sb.s, 1)
            act.wait_ge(p_wa_sb.s, 1)
            nc.scalar.copy(wah[:, :, :], wa32[:, :, :]).then_inc(p_hi.s, 1)
            for c in range(H):
                last = nc.scalar.copy(wa2h[:, c, :], wa32[:, c, 1:2].to_broadcast([P, P]))
                last.then_inc(p_hi.s, 1)
            act.wait_ge(p_hi.s, 16)
            act.wait_ge(p_small.s, 5)
            act.sem_inc(p_done_act.s, 1)

            def turn_x(g, step):
                for f in range(H):
                    act.wait_ge(xT_ready.s, xT_ready.at(g, f + 1))
                    nc.scalar.copy(h[:, f, :], psA[:, f, :]).then_inc(h0_ready.s, 1)
                split_h(g, 0)

            def split_h(g, step):
                for f in range(H):
                    if step == 0:
                        act.wait_ge(h0_ready.s, h0_ready.at(g, f + 1))
                    else:
                        act.wait_ge(hn_ready.s, hn_ready.at(g, (step - 1) * H + f + 1))
                    nc.scalar.copy(hh[:, f, :], h[:, f, :]).then_inc(hh_ready.s, 1)

            def neighbours(g, step):
                for f in range(H):
                    act.wait_ge(aT_ready.s, aT_ready.at(g, step * H + f + 1))
                    nc.scalar.copy(ah[:, f, :], psA[:, f, :]).then_inc(ah_ready.s, 1)

            def gate_u(g, step):
                for f in range(H):
                    act.wait_ge(u_ready.s, u_ready.at(g, step * H + f + 1))
                    nc.scalar.copy(tz[:, f, :], psA[:, f, :]).then_inc(u_copied.s, 1)

            def gate_r(g, step):
                for f in range(H):
                    act.wait_ge(r_ready.s, r_ready.at(g, step * H + f + 1))
                    nc.scalar.activation(tr[:, f, :], psA[:, f, :], ACT.Tanh,
                                         bias=bias_r[:, f:f + 1], scale=0.5).then_inc(tr_ready.s, 1)

            def gate_z(g, step):
                for f in range(H):
                    act.wait_ge(zsum_ready.s, zsum_ready.at(g, step * H + f + 1))
                    nc.scalar.activation(tz[:, f, :], tz[:, f, :], ACT.Tanh, bias=bias_z[:, f:f + 1], scale=0.5
                                         ).then_inc(tz_ready.s, 1)

            def gate_v(g, step):
                for f in range(H):
                    act.wait_ge(v_ready.s, v_ready.at(g, step * H + f + 1))
                    nc.scalar.activation(th[:, f, :], psA[:, f, :], ACT.Tanh,
                                         bias=bias_h[:, f:f + 1]).then_inc(th_ready.s, 1)

            def update(g, step):
                if step < STEPS - 1:
                    split_h(g, step + 1)

            def turn_h(g, step):
                if step == STEPS - 1:
                    return
                dst = tok(psA)
                for k in range(2):
                    act.wait_ge(hT_ready.s, hT_ready.at(g, 2 * step + k + 1))
                    nc.scalar.copy(h_tok[:, 2 * k:2 * k + 2, :], dst[:, 2 * k:2 * k + 2, :]).then_inc(htok_ready.s, 1)

            def norm(g, n, s, src, dst):
                act.wait_ge(ln_shift[s].s, ln_shift[s].at(g, max(n, 1)))
                for t in range(T):
                    nc.scalar.activation(dst[:, t, :], src[:, t, :], ACT.Identity, bias=ln_nb[s][:, t:t + 1],
                                         scale=ln_rs[s][:, t:t + 1]).then_inc(ln_out[s].s, 1)

            def normalise_x(g, n):
                if not first(g):
                    act.wait_ge(pre2_ready.s, pre2_ready.at(g - 1, T))
                norm(g, 0, 0, pre1, y1)

            def normalise_y(g, n):
                if not first(g):
                    act.wait_ge(pre3_ready.s, pre3_ready.at(g - 1, T))
                norm(g, 0, 1, pre2, y2)

            def normalise(g, n):
                norm(g, n, 2, pre, (None, y3, y4)[n])

            def turn_y(g, n):
                for f in range(H):
                    act.wait_ge(yT_ready.s, yT_ready.at(g, n * H + f + 1))
                    nc.scalar.copy(yTh[:, f, :], (pair0, pair1)[n][:, f, :]).then_inc(yTh_ready.s, 1)

            def turn_c(g, n):
                for f in range(H):
                    act.wait_ge(cT_ready.s, cT_ready.at(g, n * H + f + 1))
                    nc.scalar.copy(cTh[:, f, :], psC[:, f, :]).then_inc(cTh_ready.s, 1)

            def products_t(g, n):
                for f in range(H):
                    act.wait_ge(tT_ready.s, tT_ready.at(g, f + 1))
                    nc.scalar.copy(tTh[:, f, :], pair1[:, f, :]).then_inc(tTh_ready.s, 1)

            def products_v(g, n):
                for k in range(2):
                    act.wait_ge(v1_ready.s, v1_ready.at(g, k + 1))
                    nc.scalar.copy(v1[:, 2 * k:2 * k + 2, :], tok(pair0)[:, 2 * k:2 * k + 2, :]).then_inc(v1_copied.s, 1)

            def relate(g, n):
                for k in range(2):
                    rows = slice(2 * k, 2 * k + 2)
                    act.wait_ge(relw_ready.s, relw_ready.at(g, k + 1))
                    nc.scalar.activation(relsq[:, rows, :], relw[:, rows, :], ACT.Square).then_inc(relsq_ready.s, 1)

            def product_q(g, n, i=0, pair=pair0):
                for f in range(H):
                    act.wait_ge(qk_ready.s, qk_ready.at(g, i * H + f + 1))
                    nc.scalar.copy(qk[i][:, f, :], pair[:, f, :]).then_inc(qk_copied.s, 1)

            def product_k(g, n):
                product_q(g, n, 1, pair1)

            def product_v(g, n):
                for b in range(2):
                    for f in range(H):
                        act.wait_ge(v2_ready.s, v2_ready.at(g, 2))
                        src = tok(pair0)[b * N:(b + 1) * N, :, f * P:(f + 1) * P].rearrange(
                            "p t (r d) -> p t r d", r=R)
                        nc.scalar.copy(vbd[f * N:(f + 1) * N, :, b, :, f, 0:HD], src).then_inc(v2_copied.s, 1)

            def softmax(g, n):
                for r in range(2 * n, 2 * n + 2):
                    act.wait_ge(shifted_ready.s, shifted_ready.at(g, r + 1))
                    nc.scalar.activation(probs[:, r, :, :], probs[:, r, :, :], ACT.Exp, scale=SCALE
                                         ).then_inc(exp_ready.s, 1)

            def turn_probs(g, n):
                for r in range(R):
                    act.wait_ge(probT_ready.s, probT_ready.at(g, r + 1))
                    nc.scalar.copy(probsT[:, r, :], psB[:, r, :]).then_inc(probT_copied.s, 1)

            def products_h(g, n):
                for k in range(2):
                    act.wait_ge(h3_ready.s, h3_ready.at(g, k + 1))
                    nc.scalar.copy(h3[:, 2 * k:2 * k + 2, :], tok(psC)[:, 2 * k:2 * k + 2, :]).then_inc(h3_copied.s, 1)

            def softmax3(g, n):
                act.wait_ge(e_shift.s, e_shift.at(g, 1))
                nc.scalar.activation(e3[:, :, :], e3[:, :, :], ACT.Exp).then_inc(e_exp.s, 1)

            def turn_att(g, n):
                act.wait_ge(attT_ready.s, attT_ready.at(g, 1))
                nc.scalar.copy(attT[:, :, :].rearrange("p t n -> p (t n)"), psC[:, 0, :]).then_inc(attT_copied.s, 1)

            def elu(g, n):
                for k in range(2):
                    act.wait_ge(mix3_ready.s, mix3_ready.at(g, k + 1))
                    nc.scalar.activation(y4[:, 2 * k:2 * k + 2, :], tok(psC)[:, 2 * k:2 * k + 2, :], ACT.Exp
                                         ).then_inc(elu_exp.s, 1)

            whole_program(act, dict(
                turn_x=turn_x, neighbours=neighbours, gate_u=gate_u, gate_r=gate_r, gate_z=gate_z, gate_v=gate_v, update=update,
                turn_h=turn_h, normalise_x=normalise_x, normalise_y=normalise_y, normalise=normalise,
                turn_y=turn_y, turn_c=turn_c, products_t=products_t, products_v=products_v,
                relate=relate, product_q=product_q, product_k=product_k, product_v=product_v, softmax=softmax,
                turn_probs=turn_probs, products_h=products_h, softmax3=softmax3, turn_att=turn_att, elu=elu))

        @block.vector
        def _(dve):
            f32 = lambda ap: ap.bitcast(F32)
            TT = nc.vector.tensor_tensor
            whole = lambda w_: w_[:, :, :].rearrange("p c o -> p (c o)")
            for w_, n in ((w4_in, "w4"), (w3_in, "w3"), (w5_in, "w5")):
                dve.wait_ge(p_load[n].s, 16)
                TT(w_[:, :, 0:D], w_[:, :, 0:D], w_[:, :, D:2 * D], ALU.add).then_inc(p_fold.s, 1)
            for k, (hi, lo, src) in enumerate(((u3h, u3l, psA[:, 1, :]), (w4h, w4l, psC[:, 0, :]),
                                               (w3h, w3l, psC[:, 1, :]), (w5h, w5l, psB[:, 0, :]))):
                dve.wait_ge(p_hi.s, k + 2)
                TT(whole(lo), src, f32(whole(hi)), ALU.subtract).then_inc(p_lo.s, 1)
            for k, (hi, lo, src) in enumerate(((wvh, wvl, psB[:, 2, :]), (mh, ml, psB[:, 3, :]))):
                dve.wait_ge(p_hi.s, k + 7)
                TT(whole(lo), src, f32(whole(hi)), ALU.subtract).then_inc(p_lo.s, 1)
            for c in range(H):
                dve.wait_ge(p_hi.s, 10 + c)
                TT(qkvl[:, c, :], qkv_in[c], f32(qkvh[:, c, :]), ALU.subtract).then_inc(p_lo.s, 1)
            dve.wait_ge(p_hi.s, 12)
            TT(wpl[:, :, :], wp_in, f32(wph[:, :, :]), ALU.subtract).then_inc(p_lo.s, 1)
            dve.wait_ge(p_hi.s, 13)
            TT(w3gl[:, :, :], W_in, f32(w3gh[:, :, :]), ALU.subtract).then_inc(p_lo.s, 1)
            dve.wait_ge(p_load["adj2"].s, 32)
            nc.vector.tensor_scalar(mask_add[:, :], adj2[:, :], 0.0, MASKED, ALU.is_equal, ALU.mult).then_inc(p_small.s, 1)
            dve.wait_ge(p_load["beta"].s, 16)
            dve.wait_ge(p_ident.s, 1)
            for b in range(2):
                rows = slice(b * N, (b + 1) * N)
                nc.vector.tensor_scalar(beta_eye[rows, :], ident[rows, rows], beta_col[rows, 0:1], None, ALU.mult
                                        ).then_inc(p_small.s, 1)
            dve.wait_ge(p_load["bias"].s, 80 * H)
            TT(bias_z[:, :], biases[:, 0, :], biases[:, 3, :], ALU.add).then_inc(p_small.s, 1)
            TT(bias_r[:, :], biases[:, 1, :], biases[:, 3, :], ALU.add).then_inc(p_small.s, 1)
            TT(bias_h[:, :], biases[:, 2, :], biases[:, 4, :], ALU.add).then_inc(p_small.s, 1)
            dve.wait_ge(p_small.s, 6)
            nc.vector.tensor_scalar(bias_z[:, :], bias_z[:, :], 0.5, None, ALU.mult).then_inc(p_small.s, 1)
            nc.vector.tensor_scalar(bias_r[:, :], bias_r[:, :], 0.5, None, ALU.mult).then_inc(p_small.s, 1)
            dve.wait_ge(p_hi.s, 14)
            TT(wal[:, :, :], wa32[:, :, :], f32(wah[:, :, :]), ALU.subtract).then_inc(p_lo.s, 1)
            for c in range(H):
                dve.wait_ge(p_hi.s, 15 + c)
                TT(wa2l[:, c, :], wa32[:, c, 1:2].to_broadcast([P, P]), f32(wa2h[:, c, :]), ALU.subtract
                   ).then_inc(p_lo.s, 1)
            dve.wait_ge(p_load["rows"].s, 48)
            dve.wait_ge(p_lo.s, 13)
            dve.wait_ge(p_small.s, 8)
            dve.sem_inc(p_done_dve.s, 1)

            def split_h(g, step):
                for f in range(H):
                    dve.wait_ge(hh_ready.s, hh_ready.at(g, step * H + f + 1))
                    TT(hl[:, f, :], h[:, f, :], f32(hh[:, f, :]), ALU.subtract).then_inc(hl_ready.s, 1)

            def turn_x(g, step):
                split_h(g, 0)

            def neighbours(g, step):
                for f in range(H):
                    dve.wait_ge(ah_ready.s, ah_ready.at(g, step * H + f + 1))
                    TT(al[:, f, :], psA[:, f, :], f32(ah[:, f, :]), ALU.subtract).then_inc(al_ready.s, 1)

            def gate_r(g, step):
                for f in range(H):
                    dve.wait_ge(tr_ready.s, tr_ready.at(g, step * H + f + 1))
                    nc.vector.scalar_tensor_tensor(out=rh[:, f, :], in0=tr[:, f, :], scalar=1.0, in1=h[:, f, :],
                                                   op0=ALU.add, op1=ALU.mult).then_inc(rh_ready.s, 1)

            def gate_z(g, step):
                for f in range(H):
                    dve.wait_ge(z_ready.s, z_ready.at(g, step * H + f + 1))
                    TT(tz[:, f, :], psA[:, f, :], tz[:, f, :], ALU.add).then_inc(zsum_ready.s, 1)

            def update(g, step):
                k = step * H
                for f in range(H):
                    dve.wait_ge(th_ready.s, th_ready.at(g, k + f + 1))
                    TT(th[:, f, :], th[:, f, :], h[:, f, :], ALU.subtract).then_inc(d_ready.s, 1)
                    dve.wait_ge(tz_ready.s, tz_ready.at(g, k + f + 1))
                    dve.wait_ge(d_ready.s, d_ready.at(g, k + f + 1))
                    nc.vector.scalar_tensor_tensor(out=th[:, f, :], in0=tz[:, f, :], scalar=1.0, in1=th[:, f, :],
                                                   op0=ALU.add, op1=ALU.mult).then_inc(zd_ready.s, 1)
                    dve.wait_ge(zd_ready.s, zd_ready.at(g, k + f + 1))
                    nc.vector.scalar_tensor_tensor(out=h[:, f, :], in0=th[:, f, :], scalar=0.5, in1=h[:, f, :],
                                                   op0=ALU.mult, op1=ALU.add).then_inc(hn_ready.s, 1)
                if step < STEPS - 1:
                    split_h(g, step + 1)

            def turn_h(g, step):
                if step < STEPS - 1:
                    return
                src = tok(psA)
                dve.wait_ge(x_copied.s, x_copied.at(g, 1))
                for k in range(2):
                    dve.wait_ge(hT_ready.s, hT_ready.at(g, 2 * step + k + 1))
                    TT(pre1[:, 2 * k:2 * k + 2, :], src[:, 2 * k:2 * k + 2, :], x_res[:, 2 * k:2 * k + 2, :], ALU.add
                       ).then_inc(pre1_ready.s, 1)

            def norm(g, n, s, src, ready, per):
                for t in range(T):
                    dve.wait_ge(ready.s, ready.at(g, t // per + 1))
                    nc.vector.bn_stats(ln_st[s][:, t, :], src[:, t, :]).then_inc(ln_stats[s].s, 1)
                dve.wait_ge(ln_stats[s].s, ln_stats[s].at(g, (n + 1) * T))
                dve.sem_inc(passed_dve.s, 1)
                for t in range(T):
                    nc.vector.bn_aggr(ln_mv[s][:, t, :], ln_st[s][:, t, :]).then_inc(ln_aggr[s].s, 1)
                dve.wait_ge(ln_aggr[s].s, ln_aggr[s].at(g, (n + 1) * T))
                if n > 0 or not first(g):
                    dve.wait_ge(ln_rstd[s].s, ln_rstd[s].at(g, n))
                    if n != 1:
                        dve.wait_ge(ln_shift[s].s, ln_shift[s].at(g, max(n - 1, 0)))
                nc.vector.tensor_scalar(ln_ve[s][:, :], ln_mv[s][:, :, 1], LN_EPS, None, ALU.add
                                        ).then_inc(ln_vareps[s].s, 1)
                nc.vector.tensor_scalar(ln_nm[s][:, :], ln_mv[s][:, :, 0], -1.0, None, ALU.mult
                                        ).then_inc(ln_vareps[s].s, 1)

            def stats_x(g, n):
                norm(g, 0, 0, pre1, pre1_ready, 2)

            def stats_y(g, n):
                norm(g, 0, 1, pre2, pre2_ready, 1)

            def stats(g, n):
                norm(g, n, 2, *((y3, o2_ready, 2), (pre, pre3_ready, 1), (pre, pre4_ready, 2))[n])

            def turn_y(g, n):
                for f in range(H):
                    dve.wait_ge(yTh_ready.s, yTh_ready.at(g, n * H + f + 1))
                    TT(yTl[:, f, :], (pair0, pair1)[n][:, f, :], f32(yTh[:, f, :]), ALU.subtract).then_inc(yTl_ready.s, 1)

            def turn_c(g, n):
                for f in range(H):
                    dve.wait_ge(cTh_ready.s, cTh_ready.at(g, n * H + f + 1))
                    TT(cTl[:, f, :], psC[:, f, :], f32(cTh[:, f, :]), ALU.subtract).then_inc(cTl_ready.s, 1)

            def products_t(g, n):
                for f in range(H):
                    dve.wait_ge(tTh_ready.s, tTh_ready.at(g, f + 1))
                    TT(tTl[:, f, :], pair1[:, f, :], f32(tTh[:, f, :]), ALU.subtract).then_inc(tTl_ready.s, 1)

            def relate(g, n):
                for k in range(2):
                    rows = slice(2 * k, 2 * k + 2)
                    dve.wait_ge(rel_ready.s, rel_ready.at(g, k + 1))
                    TT(relw[:, rows, :], tok(pair1)[:, rows, 0:P],
                       adj_bd[:, :].unsqueeze(1).to_broadcast([P, 2, P]), ALU.mult).then_inc(relw_ready.s, 1)

            def mix1(g, n):
                dve.wait_ge(norm2_ready.s, norm2_ready.at(g, 1))
                nc.vector.tensor_copy(norm2[:, :], pair1[:, 0, 0:T]).then_inc(norm2_copied.s, 1)

            def residual1(g, n):
                dve.wait_ge(rnorm_ready.s, rnorm_ready.at(g, 1))
                for t in range(T):
                    dve.wait_ge(mix1_ready.s, mix1_ready.at(g, t // 2 + 1))
                    nc.vector.scalar_tensor_tensor(out=pre2[:, t, :], in0=tok(pair0)[:, t, :], scalar=rnorm[:, t:t + 1],
                                                   in1=y1[:, t, :], op0=ALU.mult, op1=ALU.add).then_inc(pre2_ready.s, 1)

            def softmax(g, n):
                dve.wait_ge(score_ready.s, score_ready.at(g, 1))
                for k in range(2 * n, 2 * n + 4):
                    if k < 2 * n + 2:
                        TT(probs[:, k, :, :], psB[:, k, :].rearrange("p (a n) -> p a n", n=N),
                           mask_add[:, :].unsqueeze(1).to_broadcast([P, T * H, N]), ALU.add).then_inc(masked_ready.s, 1)
                    if 2 * n + 1 <= k <= 2 * n + 2:
                        r = k - 1
                        dve.wait_ge(masked_ready.s, masked_ready.at(g, r + 1))
                        nc.vector.tensor_reduce(smax[:, r * T * H:(r + 1) * T * H], probs[:, r, :, :], AX.X, ALU.max
                                                ).then_inc(smax_ready.s, 1)
                    if k >= 2 * n + 2:
                        r = k - 2
                        dve.wait_ge(smax_ready.s, smax_ready.at(g, r + 1))
                        TT(probs[:, r, :, :], probs[:, r, :, :],
                           smax[:, r * T * H:(r + 1) * T * H].unsqueeze(2).to_broadcast([P, T * H, N]), ALU.subtract
                           ).then_inc(shifted_ready.s, 1)

            def divide(g, n):
                dve.wait_ge(heads_ready.s, heads_ready.at(g, 1))
                heads = psB[:, :, 0:R * H * (HD + 1)].rearrange("p t (r f c) -> p t r f c", r=R, f=H)
                nc.vector.reciprocal(rsum[:, :, :, :], heads[:, :, :, :, HD]).then_inc(rsum_ready.s, 1)
                dve.wait_ge(rsum_ready.s, rsum_ready.at(g, 1))
                if not first(g):
                    dve.wait_ge(cT_ready.s, cT_ready.at(g - 1, H))
                for t in range(T):
                    TT(o_tok[:, t, :].rearrange("p (f r d) -> p r f d", f=H, r=R), heads[:, t, :, :, 0:HD],
                       rsum[:, t, :, :].unsqueeze(3).to_broadcast([P, R, H, HD]), ALU.mult).then_inc(o_ready.s, 1)

            def project(g, n):
                for k in range(2):
                    dve.wait_ge(proj_ready.s, proj_ready.at(g, k + 1))
                    TT(y3[:, 2 * k:2 * k + 2, :], tok(psC)[:, 2 * k:2 * k + 2, :],
                       bproj_bc[:, :].unsqueeze(1).to_broadcast([P, 2, D]), ALU.add).then_inc(o2_ready.s, 1)

            def residual2(g, n):
                if not first(g):
                    dve.wait_ge(stored.s, stored.at(g - 1, 16))
                for t in range(T):
                    nc.vector.scalar_tensor_tensor(out=y4[:, t, :], in0=y3[:, t, :], scalar=ln_mv[2][:, t, 0:1],
                                                   in1=gamma_bc[:, :], op0=ALU.subtract, op1=ALU.mult
                                                   ).then_inc(gam_ready.s, 1)
                dve.wait_ge(ln_rstd[2].s, ln_rstd[2].at(g, 1))
                dve.wait_ge(res2_ready.s, res2_ready.at(g, 2))
                for t in range(T):
                    dve.wait_ge(gam_ready.s, gam_ready.at(g, t + 1))
                    nc.vector.scalar_tensor_tensor(out=pre[:, t, :], in0=y4[:, t, :], scalar=ln_rs[2][:, t:t + 1],
                                                   in1=y2[:, t, :], op0=ALU.mult, op1=ALU.add).then_inc(pre3_ready.s, 1)

            def logits3(g, n):
                dve.wait_ge(s_ready.s, s_ready.at(g, 1))
                nc.vector.tensor_copy(s_tok[:, :, :].rearrange("p t w -> p (t w)"), psC[:, 0, 0:2 * T]).then_inc(s_copied.s, 1)
                dve.wait_ge(s_copied.s, s_copied.at(g, 1))
                dve.wait_ge(s_ready.s, s_ready.at(g, 2))
                for b in range(2):
                    rows = slice(b * N, (b + 1) * N)
                    TT(e3[rows, :, :], psC[rows, 1, :].rearrange("p (t b j) -> p t b j", t=T, b=2)[:, :, b, :],
                       s_tok[rows, :, 0:1].to_broadcast([N, T, N]), ALU.add).then_inc(e_sum.s, 1)
                dve.wait_ge(e_sum.s, e_sum.at(g, 2))
                nc.vector.scalar_tensor_tensor(out=e3[:, :, :], in0=e3[:, :, :], scalar=LEAKY_SLOPE, in1=e3[:, :, :],
                                               op0=ALU.mult, op1=ALU.max).then_inc(e_leaky.s, 1)
                dve.wait_ge(e_leaky.s, e_leaky.at(g, 1))
                TT(e3[:, :, :], e3[:, :, :], adj2[:, :].unsqueeze(1).to_broadcast([P, T, N]), ALU.mult).then_inc(e_mask.s, 1)
                dve.wait_ge(e_mask.s, e_mask.at(g, 1))
                nc.vector.tensor_reduce(e3max[:, :], e3[:, :, :], AX.X, ALU.max).then_inc(e_max.s, 1)
                dve.wait_ge(e_max.s, e_max.at(g, 1))
                TT(e3[:, :, :], e3[:, :, :], e3max[:, :].unsqueeze(2).to_broadcast([P, T, N]), ALU.subtract).then_inc(e_shift.s, 1)

            def softmax3(g, n):
                dve.wait_ge(e_exp.s, e_exp.at(g, 1))
                nc.vector.tensor_reduce(e3sum[:, :], e3[:, :, :], AX.X, ALU.add).then_inc(e_total.s, 1)
                dve.wait_ge(e_total.s, e_total.at(g, 1))
                nc.vector.reciprocal(e3inv[:, :], e3sum[:, :]).then_inc(e_inv.s, 1)
                dve.wait_ge(e_inv.s, e_inv.at(g, 1))
                TT(e3[:, :, :], e3[:, :, :], e3inv[:, :].unsqueeze(2).to_broadcast([P, T, N]), ALU.mult).then_inc(e_norm.s, 1)
                dve.wait_ge(e_norm.s, e_norm.at(g, 1))
                for b in range(2):
                    rows = slice(b * N, (b + 1) * N)
                    TT(att_bd[rows, :, rows], e3[rows, :, :], beta_eye[rows, :].unsqueeze(1).to_broadcast([N, T, N]),
                       ALU.add).then_inc(att_ready.s, 1)

            def elu(g, n):
                for k in range(2):
                    rows = slice(2 * k, 2 * k + 2)
                    dve.wait_ge(elu_exp.s, elu_exp.at(g, k + 1))
                    nc.vector.tensor_scalar(y4[:, rows, :], y4[:, rows, :], 1.0, -1.0, ALU.min, ALU.add).then_inc(elu_neg.s, 1)
                    dve.wait_ge(elu_neg.s, elu_neg.at(g, k + 1))
                    TT(pre[:, rows, :], tok(psC)[:, rows, :], y4[:, rows, :], ALU.max).then_inc(elu_ready.s, 1)

            whole_program(dve, dict(
                turn_x=turn_x, neighbours=neighbours, gate_r=gate_r, gate_z=gate_z, update=update, turn_h=turn_h,
                stats_x=stats_x, stats_y=stats_y, stats=stats, turn_y=turn_y, turn_c=turn_c, products_t=products_t, relate=relate, mix1=mix1, residual1=residual1,
                softmax=softmax, divide=divide, project=project, residual2=residual2, logits3=logits3,
                softmax3=softmax3, elu=elu))


_INS = ['x', 'adj', 'L0_gnn_w3_w', 'L0_gnn_w3_b', 'L0_gnn_u3_w', 'L0_gnn_u3_b', 'L0_gnn_w4_w', 'L0_gnn_w4_b',
        'L0_gnn_w5_w', 'L0_gnn_w5_b', 'L0_gnn_u5_w', 'L0_gnn_u5_b', 'L1_gnn_Wq', 'L1_gnn_Wk', 'L1_gnn_Wv',
        'L2_gnn_w_qkv', 'L2_gnn_w_proj', 'L2_gnn_b_proj', 'L2_gnn_ln_gamma', 'L2_gnn_ln_beta', 'L3_gnn_W',
        'L3_gnn_a', 'L3_gnn_beta']
_OUTS = [((128, 64, 256), 'float32')]


def kernel(**inputs):
    import numpy as _np
    import concourse.bacc as _bacc
    from concourse import mybir as _mybir
    from concourse.bass_utils import run_bass_kernel_spmd as _run

    nc = _bacc.Bacc("TRN2", target_bir_lowering=False, num_devices=1)
    arrays, args = {}, []
    for name in _INS:
        arr = _np.ascontiguousarray(inputs[name])
        arrays[f"in_{name}_dram"] = arr
        args.append(nc.dram_tensor(f"in_{name}_dram", arr.shape, _mybir.dt.from_np(arr.dtype), kind="ExternalInput").ap())
    for i, (shape, dtype) in enumerate(_OUTS):
        dt = _mybir.dt.from_np(_np.dtype(dtype))
        args.append(nc.dram_tensor(f"out_{i}_dram", shape, dt, kind="ExternalOutput").ap())
    gnn_kernel(nc, *args)
    r = _run(nc, [arrays], core_ids=[0])
    got = tuple(r.results[0][f"out_{i}_dram"] for i in range(len(_OUTS)))
    return got[0]
```
